# Optimizing a Trainium2 kernel written in Bass

```python
import numpy as np
import jax
import jax.numpy as jnp

def _softmax(x, axis=-1):
    return jax.nn.softmax(x, axis=axis)

def _gelu(x):
    return jax.nn.gelu(x, approximate=True)

def _silu(x):
    return jax.nn.silu(x)

def _sigmoid(x):
    return jax.nn.sigmoid(x)

def _layernorm(x, axis=-1, eps=1e-05):
    m = jnp.mean(x, axis=axis, keepdims=True)
    v = jnp.var(x, axis=axis, keepdims=True)
    return (x - m) / jnp.sqrt(v + eps)

def _scatter_add(tgt, idx, src, axis=0):
    return tgt.at[idx].add(src)

def _segment_sum(src, seg, n):
    return jax.ops.segment_sum(src, seg, n)
kernel_name = 'mk_cond_seq_d4_seqx_r4_c81b8e'

def setup_inputs(seed: int=0):
    np.random.seed(seed)
    _w = jnp.asarray

    def _rec_inputs():
        import jax
        import jax.numpy as jnp
        _rk = jax.random.key(seed)
        x = 1.648e-05 + 1 * jax.random.normal(jax.random.fold_in(_rk, 1), (4, 512, 288), jnp.float32)
        _lenS = 512 - jax.random.randint(jax.random.fold_in(_rk, 7), (4,), 0, max(1, 512 // 4) + 1, jnp.int32)
        _lenS2 = 512 - jax.random.randint(jax.random.fold_in(_rk, 8), (4,), 0, max(1, 512 // 4) + 1, jnp.int32)
        cond_1152 = 0.00914911 + 1.00357 * jax.random.normal(jax.random.fold_in(_rk, 11), (4, 288), jnp.float32)
        return (x, cond_1152)
    x, cond_1152 = _rec_inputs()

    def _L0_cond_setup():
        import jax, jax.numpy as jnp
        import numpy as np
        NUM_HEADS = 16
        NUM_EXPERTS = 4
        TOP_K = 2
        LN_EPS = 1e-06

        def _ln(h):
            mu = jnp.mean(h, axis=-1, keepdims=True)
            var = jnp.var(h, axis=-1, keepdims=True)
            return (h - mu) * jax.lax.rsqrt(var + LN_EPS)

        def _modulate(h, shift, scale):
            return h * (1.0 + scale[:, None, :]) + shift[:, None, :]
        key = jax.random.key(seed)
        ks = jax.random.split(key, 12)
        B, N, C = (8, 256, 288)
        H = 4 * C
        E = NUM_EXPERTS
        s = 0.02
        return {'x': jax.random.normal(ks[0], (B, N, C), jnp.float32), 'c': jax.random.normal(ks[1], (B, C), jnp.float32), 'w_adaln': jax.random.normal(ks[2], (C, 6 * C), jnp.float32) * s, 'b_adaln': jnp.zeros((6 * C,), jnp.float32), 'w_qkv': jax.random.normal(ks[3], (C, 3 * C), jnp.float32) * s, 'b_qkv': jnp.zeros((3 * C,), jnp.float32), 'w_proj': jax.random.normal(ks[4], (C, C), jnp.float32) * s, 'b_proj': jnp.zeros((C,), jnp.float32), 'w_gate': jax.random.normal(ks[5], (C, E), jnp.float32) * s, 'w1': jax.random.normal(ks[6], (E, C, H), jnp.float32) * s, 'b1': jnp.zeros((E, H), jnp.float32), 'w2': jax.random.normal(ks[7], (E, H, C), jnp.float32) * s, 'b2': jnp.zeros((E, C), jnp.float32)}
    _L0_cond_all = _L0_cond_setup()
    _L0_cond_in = {k: v for k, v in _L0_cond_all.items() if k in ('w_adaln', 'b_adaln', 'w_qkv', 'b_qkv', 'w_proj', 'b_proj', 'w_gate', 'w1', 'b1', 'w2', 'b2')}
    del _L0_cond_all

    def _L1_cond_setup():
        import jax, jax.numpy as jnp
        import numpy as np
        from jax.scipy.linalg import expm
        N, D, COND_DIM = (288, 64, 288)
        B, T = (16, 256)

        def _rotation(cond, W, b):
            v = jax.nn.silu(cond) @ W.T + b
            iu, ju = jnp.triu_indices(D, k=1)
            A = jnp.zeros((cond.shape[0], D, D), dtype=v.dtype)
            A = A.at[:, iu, ju].set(v).at[:, ju, iu].set(-v)
            return expm(A)
        key = jax.random.key(seed)
        k1, k2, k3, k4, k5 = jax.random.split(key, 5)
        x = jax.random.normal(k1, (B, T, N), dtype=jnp.float32)
        cond = jax.random.normal(k2, (B, COND_DIM), dtype=jnp.float32)
        P = jax.random.normal(k3, (N, D), dtype=jnp.float32)
        n_skew = D * (D - 1) // 2
        bound = 1.0 / np.sqrt(COND_DIM)
        W = jax.random.uniform(k4, (n_skew, COND_DIM), minval=-bound, maxval=bound, dtype=jnp.float32)
        b = jax.random.uniform(k5, (n_skew,), minval=-bound, maxval=bound, dtype=jnp.float32)
        return {'x': x, 'cond': cond, 'P': P, 'W': W, 'b': b}
    _L1_cond_all = _L1_cond_setup()
    _L1_cond_in = {k: v for k, v in _L1_cond_all.items() if k in ('P', 'W', 'b')}
    del _L1_cond_all

    def _L2_cond_setup():
        import jax, jax.numpy as jnp
        import numpy as np
        H = 288
        NH = 16
        HD = H // NH
        MLP = int(H * 4.0)
        EPS = 1e-06

        def _ln(z, scale=None):
            m = jnp.mean(z, axis=-1, keepdims=True)
            v = jnp.mean(jnp.square(z - m), axis=-1, keepdims=True)
            y = (z - m) * jax.lax.rsqrt(v + EPS)
            if scale is not None:
                y = y * scale
            return y
        key = jax.random.key(seed)
        ks = jax.random.split(key, 16)
        B, N = (16, 256)
        x = jax.random.normal(ks[0], (B, N, H), dtype=jnp.float32)
        c = jax.random.normal(ks[1], (B, H), dtype=jnp.float32)

        def xav(k, fan_in, fan_out):
            lim = np.sqrt(6.0 / (fan_in + fan_out))
            return jax.random.uniform(k, (fan_in, fan_out), jnp.float32, -lim, lim)
        w_mod = 0.02 * jax.random.normal(ks[2], (H, 6 * H), dtype=jnp.float32)
        b_mod = 0.02 * jax.random.normal(ks[3], (6 * H,), dtype=jnp.float32)
        w_qkv = xav(ks[4], H, 3 * H)
        b_qkv = jnp.zeros((3 * H,), jnp.float32)
        g_q = jnp.ones((HD,), jnp.float32)
        g_k = jnp.ones((HD,), jnp.float32)
        w_proj = xav(ks[5], H, H)
        b_proj = jnp.zeros((H,), jnp.float32)
        w1 = xav(ks[6], H, MLP)
        b1 = jnp.zeros((MLP,), jnp.float32)
        w2 = xav(ks[7], MLP, H)
        b2 = jnp.zeros((H,), jnp.float32)
        return dict(x=x, c=c, w_mod=w_mod, b_mod=b_mod, w_qkv=w_qkv, b_qkv=b_qkv, g_q=g_q, g_k=g_k, w_proj=w_proj, b_proj=b_proj, w1=w1, b1=b1, w2=w2, b2=b2)
    _L2_cond_all = _L2_cond_setup()
    _L2_cond_in = {k: v for k, v in _L2_cond_all.items() if k in ('w_mod', 'b_mod', 'w_qkv', 'b_qkv', 'g_q', 'g_k', 'w_proj', 'b_proj', 'w1', 'b1', 'w2', 'b2')}
    del _L2_cond_all

    def _L3_cond_setup():
        import jax, jax.numpy as jnp
        import numpy as np
        B, L, C = (8, 256, 288)
        H = 16
        D = C // H
        FF = int(C * 4.0)
        EPS = 1e-06

        def _layernorm(x):
            mu = jnp.mean(x, axis=-1, keepdims=True)
            var = jnp.mean(jnp.square(x - mu), axis=-1, keepdims=True)
            return (x - mu) * jax.lax.rsqrt(var + EPS)

        def _modulate(x, shift, scale):
            return x * (1.0 + scale) + shift

        def _attention(h, W_qkv, b_qkv, W_proj, b_proj):
            b, l, c = h.shape
            qkv = h @ W_qkv + b_qkv
            qkv = qkv.reshape(b, l, 3, H, D)
            q, k, v = (qkv[:, :, 0], qkv[:, :, 1], qkv[:, :, 2])
            scale = D ** (-0.5)
            scores = jnp.einsum('blhd,bmhd->bhlm', q * scale, k)
            attn = jax.nn.softmax(scores, axis=-1)
            o = jnp.einsum('bhlm,bmhd->blhd', attn, v).reshape(b, l, c)
            return o @ W_proj + b_proj
        key = jax.random.key(seed)
        ks = jax.random.split(key, 12)
        s = 0.02
        return {'x': jax.random.normal(ks[0], (B, L, C), jnp.float32), 'c': jax.random.normal(ks[1], (B, 1, C), jnp.float32), 'W_qkv': jax.random.normal(ks[2], (C, 3 * C), jnp.float32) * s, 'b_qkv': jnp.zeros((3 * C,), jnp.float32), 'W_proj': jax.random.normal(ks[3], (C, C), jnp.float32) * s, 'b_proj': jnp.zeros((C,), jnp.float32), 'W_fc1': jax.random.normal(ks[4], (C, FF), jnp.float32) * s, 'b_fc1': jnp.zeros((FF,), jnp.float32), 'W_fc2': jax.random.normal(ks[5], (FF, C), jnp.float32) * s, 'b_fc2': jnp.zeros((C,), jnp.float32), 'W_ada': jax.random.normal(ks[6], (C, 6 * C), jnp.float32) * s, 'b_ada': jnp.zeros((6 * C,), jnp.float32)}
    _L3_cond_all = _L3_cond_setup()
    _L3_cond_in = {k: v for k, v in _L3_cond_all.items() if k in ('W_qkv', 'b_qkv', 'W_proj', 'b_proj', 'W_fc1', 'b_fc1', 'W_fc2', 'b_fc2', 'W_ada', 'b_ada')}
    del _L3_cond_all
    return {'x': x, 'cond_1152': cond_1152, 'L0_cond_w_adaln': _L0_cond_in['w_adaln'], 'L0_cond_b_adaln': _L0_cond_in['b_adaln'], 'L0_cond_w_qkv': _L0_cond_in['w_qkv'], 'L0_cond_b_qkv': _L0_cond_in['b_qkv'], 'L0_cond_w_proj': _L0_cond_in['w_proj'], 'L0_cond_b_proj': _L0_cond_in['b_proj'], 'L0_cond_w_gate': _L0_cond_in['w_gate'], 'L0_cond_w1': _L0_cond_in['w1'], 'L0_cond_b1': _L0_cond_in['b1'], 'L0_cond_w2': _L0_cond_in['w2'], 'L0_cond_b2': _L0_cond_in['b2'], 'L1_cond_P': _L1_cond_in['P'], 'L1_cond_W': _L1_cond_in['W'], 'L1_cond_b': _L1_cond_in['b'], 'L2_cond_w_mod': _L2_cond_in['w_mod'], 'L2_cond_b_mod': _L2_cond_in['b_mod'], 'L2_cond_w_qkv': _L2_cond_in['w_qkv'], 'L2_cond_b_qkv': _L2_cond_in['b_qkv'], 'L2_cond_g_q': _L2_cond_in['g_q'], 'L2_cond_g_k': _L2_cond_in['g_k'], 'L2_cond_w_proj': _L2_cond_in['w_proj'], 'L2_cond_b_proj': _L2_cond_in['b_proj'], 'L2_cond_w1': _L2_cond_in['w1'], 'L2_cond_b1': _L2_cond_in['b1'], 'L2_cond_w2': _L2_cond_in['w2'], 'L2_cond_b2': _L2_cond_in['b2'], 'L3_cond_W_qkv': _L3_cond_in['W_qkv'], 'L3_cond_b_qkv': _L3_cond_in['b_qkv'], 'L3_cond_W_proj': _L3_cond_in['W_proj'], 'L3_cond_b_proj': _L3_cond_in['b_proj'], 'L3_cond_W_fc1': _L3_cond_in['W_fc1'], 'L3_cond_b_fc1': _L3_cond_in['b_fc1'], 'L3_cond_W_fc2': _L3_cond_in['W_fc2'], 'L3_cond_b_fc2': _L3_cond_in['b_fc2'], 'L3_cond_W_ada': _L3_cond_in['W_ada'], 'L3_cond_b_ada': _L3_cond_in['b_ada']}

def reference(x, cond_1152, L0_cond_w_adaln, L0_cond_b_adaln, L0_cond_w_qkv, L0_cond_b_qkv, L0_cond_w_proj, L0_cond_b_proj, L0_cond_w_gate, L0_cond_w1, L0_cond_b1, L0_cond_w2, L0_cond_b2, L1_cond_P, L1_cond_W, L1_cond_b, L2_cond_w_mod, L2_cond_b_mod, L2_cond_w_qkv, L2_cond_b_qkv, L2_cond_g_q, L2_cond_g_k, L2_cond_w_proj, L2_cond_b_proj, L2_cond_w1, L2_cond_b1, L2_cond_w2, L2_cond_b2, L3_cond_W_qkv, L3_cond_b_qkv, L3_cond_W_proj, L3_cond_b_proj, L3_cond_W_fc1, L3_cond_b_fc1, L3_cond_W_fc2, L3_cond_b_fc2, L3_cond_W_ada, L3_cond_b_ada):
    import jax
    import jax.numpy as jnp

    def _L0_cond_ref(x, c, w_adaln, b_adaln, w_qkv, b_qkv, w_proj, b_proj, w_gate, w1, b1, w2, b2):
        import jax, jax.numpy as jnp
        import numpy as np
        NUM_HEADS = 16
        NUM_EXPERTS = 4
        TOP_K = 2
        LN_EPS = 1e-06

        def _ln(h):
            mu = jnp.mean(h, axis=-1, keepdims=True)
            var = jnp.var(h, axis=-1, keepdims=True)
            return (h - mu) * jax.lax.rsqrt(var + LN_EPS)

        def _modulate(h, shift, scale):
            return h * (1.0 + scale[:, None, :]) + shift[:, None, :]
        B, N, C = x.shape
        nh = NUM_HEADS
        hd = C // nh
        mod = jax.nn.silu(c) @ w_adaln + b_adaln
        sh_msa, sc_msa, g_msa, sh_mlp, sc_mlp, g_mlp = jnp.split(mod, 6, axis=-1)
        h = _modulate(_ln(x), sh_msa, sc_msa)
        qkv = (h @ w_qkv + b_qkv).reshape(B, N, 3, nh, hd).transpose(2, 0, 3, 1, 4)
        q, k, v = (qkv[0], qkv[1], qkv[2])
        attn = jax.nn.softmax(jnp.einsum('bhqd,bhkd->bhqk', q, k) * hd ** (-0.5), axis=-1)
        o = jnp.einsum('bhqk,bhkd->bhqd', attn, v).transpose(0, 2, 1, 3).reshape(B, N, C)
        o = o @ w_proj + b_proj
        x = x + g_msa[:, None, :] * o
        xn = _modulate(_ln(x), sh_mlp, sc_mlp)
        xf = xn.reshape(-1, C)
        gate_logits = xf @ w_gate
        topk_logits, topk_idx = jax.lax.top_k(gate_logits, TOP_K)
        gates = jax.nn.softmax(topk_logits, axis=-1)
        cw = jnp.sum(jax.nn.one_hot(topk_idx, NUM_EXPERTS, dtype=xf.dtype) * gates[..., None], axis=1)
        hmid = jax.nn.gelu(jnp.einsum('tc,ech->eth', xf, w1) + b1[:, None, :], approximate=True)
        eo = jnp.einsum('eth,ehc->etc', hmid, w2) + b2[:, None, :]
        moe = jnp.einsum('te,etc->tc', cw, eo).reshape(B, N, C)
        return x + g_mlp[:, None, :] * moe

    def _L1_cond_ref(x, cond, P, W, b):
        import jax, jax.numpy as jnp
        import numpy as np
        from jax.scipy.linalg import expm
        N, D, COND_DIM = (288, 64, 288)
        B, T = (16, 256)

        def _rotation(cond, W, b):
            v = jax.nn.silu(cond) @ W.T + b
            iu, ju = jnp.triu_indices(D, k=1)
            A = jnp.zeros((cond.shape[0], D, D), dtype=v.dtype)
            A = A.at[:, iu, ju].set(v).at[:, ju, iu].set(-v)
            return expm(A)
        U, _ = jnp.linalg.qr(P)
        R = _rotation(cond, W, b)
        z = jnp.einsum('btn,nd->btd', x, U)
        z_rot = jnp.einsum('btd,bde->bte', z, R)
        x_rot = x + jnp.einsum('btd,nd->btn', z_rot - z, U)
        return x_rot

    def _L2_cond_ref(x, c, w_mod, b_mod, w_qkv, b_qkv, g_q, g_k, w_proj, b_proj, w1, b1, w2, b2):
        import jax, jax.numpy as jnp
        import numpy as np
        H = 288
        NH = 16
        HD = H // NH
        MLP = int(H * 4.0)
        EPS = 1e-06

        def _ln(z, scale=None):
            m = jnp.mean(z, axis=-1, keepdims=True)
            v = jnp.mean(jnp.square(z - m), axis=-1, keepdims=True)
            y = (z - m) * jax.lax.rsqrt(v + EPS)
            if scale is not None:
                y = y * scale
            return y
        B, N, _ = x.shape
        mod = jax.nn.swish(c) @ w_mod + b_mod
        sh_msa, sc_msa, g_msa, sh_mlp, sc_mlp, g_mlp = jnp.split(mod, 6, axis=1)
        xn = _ln(x) * (1 + sc_msa[:, None, :]) + sh_msa[:, None, :]
        qkv = xn @ w_qkv + b_qkv
        qkv = qkv.reshape(B, N, 3, NH, HD).transpose(2, 0, 3, 1, 4)
        q, k, v = (qkv[0], qkv[1], qkv[2])
        q = _ln(q, g_q)
        k = _ln(k, g_k)
        attn = jax.nn.softmax(jnp.einsum('bhqd,bhkd->bhqk', q, k) * HD ** (-0.5), axis=-1)
        o = jnp.einsum('bhqk,bhkd->bhqd', attn, v)
        o = o.transpose(0, 2, 1, 3).reshape(B, N, H) @ w_proj + b_proj
        x = x + g_msa[:, None, :] * o
        xn2 = _ln(x) * (1 + sc_mlp[:, None, :]) + sh_mlp[:, None, :]
        h = jax.nn.gelu(xn2 @ w1 + b1, approximate=True)
        x = x + g_mlp[:, None, :] * (h @ w2 + b2)
        return x

    def _L3_cond_ref(x, c, W_qkv, b_qkv, W_proj, b_proj, W_fc1, b_fc1, W_fc2, b_fc2, W_ada, b_ada):
        import jax, jax.numpy as jnp
        import numpy as np
        B, L, C = (8, 256, 288)
        H = 16
        D = C // H
        FF = int(C * 4.0)
        EPS = 1e-06

        def _layernorm(x):
            mu = jnp.mean(x, axis=-1, keepdims=True)
            var = jnp.mean(jnp.square(x - mu), axis=-1, keepdims=True)
            return (x - mu) * jax.lax.rsqrt(var + EPS)

        def _modulate(x, shift, scale):
            return x * (1.0 + scale) + shift

        def _attention(h, W_qkv, b_qkv, W_proj, b_proj):
            b, l, c = h.shape
            qkv = h @ W_qkv + b_qkv
            qkv = qkv.reshape(b, l, 3, H, D)
            q, k, v = (qkv[:, :, 0], qkv[:, :, 1], qkv[:, :, 2])
            scale = D ** (-0.5)
            scores = jnp.einsum('blhd,bmhd->bhlm', q * scale, k)
            attn = jax.nn.softmax(scores, axis=-1)
            o = jnp.einsum('bhlm,bmhd->blhd', attn, v).reshape(b, l, c)
            return o @ W_proj + b_proj
        ada = jax.nn.silu(c) @ W_ada + b_ada
        shift_msa, scale_msa, gate_msa, shift_mlp, scale_mlp, gate_mlp = jnp.split(ada, 6, axis=-1)
        h = _modulate(_layernorm(x), shift_msa, scale_msa)
        x = x + gate_msa * _attention(h, W_qkv, b_qkv, W_proj, b_proj)
        h = _modulate(_layernorm(x), shift_mlp, scale_mlp)
        mlp = jax.nn.gelu(h @ W_fc1 + b_fc1, approximate=True) @ W_fc2 + b_fc2
        x = x + gate_mlp * mlp
        return x
    x = _L0_cond_ref(x, cond_1152, L0_cond_w_adaln, L0_cond_b_adaln, L0_cond_w_qkv, L0_cond_b_qkv, L0_cond_w_proj, L0_cond_b_proj, L0_cond_w_gate, L0_cond_w1, L0_cond_b1, L0_cond_w2, L0_cond_b2)
    x = _L1_cond_ref(x, cond_1152, L1_cond_P, L1_cond_W, L1_cond_b)
    x = _L2_cond_ref(x, cond_1152, L2_cond_w_mod, L2_cond_b_mod, L2_cond_w_qkv, L2_cond_b_qkv, L2_cond_g_q, L2_cond_g_k, L2_cond_w_proj, L2_cond_b_proj, L2_cond_w1, L2_cond_b1, L2_cond_w2, L2_cond_b2)
    x = _L3_cond_ref(x, cond_1152[:, None, :], L3_cond_W_qkv, L3_cond_b_qkv, L3_cond_W_proj, L3_cond_b_proj, L3_cond_W_fc1, L3_cond_b_fc1, L3_cond_W_fc2, L3_cond_b_fc2, L3_cond_W_ada, L3_cond_b_ada)
    return x

_drawn_inputs = setup_inputs


def setup_inputs(seed=0):
    import zlib

    import numpy as np

    out = dict(_drawn_inputs(seed))
    spreads = {'L0_cond_b_adaln': (0.0, 0.431),
     'L0_cond_b_qkv': (0.0, 0.8),
     'L0_cond_b_proj': (0.0, 0.35),
     'L0_cond_b1': (0.0, 0.8),
     'L0_cond_b2': (0.0, 0.507),
     'L2_cond_b_qkv': (0.0, 0.393),
     'L2_cond_g_q': (1.0, 0.6),
     'L2_cond_g_k': (1.0, 0.6),
     'L2_cond_b_proj': (0.0, 0.398),
     'L2_cond_b1': (0.0, 0.524),
     'L2_cond_b2': (0.0, 0.411),
     'L3_cond_b_qkv': (0.0, 0.8),
     'L3_cond_b_proj': (0.0, 0.354),
     'L3_cond_b_fc1': (0.0, 0.8),
     'L3_cond_b_fc2': (0.0, 0.349),
     'L3_cond_b_ada': (0.0, 0.377)}
    factors = {'L0_cond_w_qkv': 8.0,
     'L0_cond_w_proj': 5.375,
     'L0_cond_w_gate': 2.868,
     'L0_cond_w1': 2.706,
     'L2_cond_b_mod': 5.103,
     'L3_cond_W_qkv': 8.0,
     'L3_cond_W_proj': 5.232}
    for name, (base, spread) in spreads.items():
        noise = np.random.default_rng([zlib.crc32(name.encode()), seed]).standard_normal(out[name].shape)
        drawn = base * np.exp(spread * noise) if base else spread * noise
        out[name] = jnp.asarray(drawn.astype(out[name].dtype))
    for name, factor in factors.items():
        out[name] = (out[name] * factor).astype(out[name].dtype)
    return out
```

```python
from contextlib import ExitStack

import numpy as np

import concourse.bass as bass
from concourse import mybir

F32 = mybir.dt.float32
BF16 = mybir.dt.bfloat16
ALU = mybir.AluOpType
ACT = mybir.ActivationFunctionType
AX_X = mybir.AxisListType.X

P = 128
B, N, C = 4, 512, 288
TB = N // P
NT = B * TB
CH = 96
NC3 = C // CH
NH, HD = 16, C // 16
G = 4
NG = NH // G
GW = G * HD
HP = 32
HID = 4 * C
MH = HID // P
E = 4
D = 64
LAYERS = ("L0", "L2", "L3")
KM = 6 * HD
KS = KM + 3
SCALE = float(HD) ** -0.5
EPS = 1e-6
TAYLOR = 12
SQUARINGS = 16
CREDIT = 16

A_QKV = 0
A_V = A_QKV + TB * 3 * C * 4
A_KP = A_V + 2 * TB * G * HP * 4
A_QP = A_KP + 2 * TB * G * 112 * 2
A_SPL = A_QP + 2 * TB * G * 112 * 2
A_KT = A_SPL + 2 * (TB * GW * 4 + 2 * TB * GW * 2)
A_QT = A_KT + 2 * G * N * 2
A_PT = A_QT + 2 * G * N * 2
A_OT = A_PT + 2 * G * N * 4
A_RD = A_OT + NG * N * 4
A_END = A_RD + N * 4
M_HID = 0
M_W1 = MH * N * 4
W1_B, W2_B = NC3 * HID * 4, MH * C * 4
W_BYTES = W1_B + W2_B + C * 4 + MH * 4
M_LIN = M_W1 + W_BYTES + 28
M_LIN += -M_LIN % 32
I_WS = M_LIN
I_BS = I_WS + 2 * NC3 * 512 * 4


class Signal:

    def __init__(self, sem, per):
        self.sem, self.per = sem, per

    def at(self, turn, k):
        return turn * self.per + (k + CREDIT)


def host_constants():
    r = np.arange(D)
    eye = np.eye(P, dtype=np.float32)
    sel = np.zeros((P, P), np.float32)
    for j in range(G):
        sel[HP * j + HD, HP * j:HP * j + HP] = 1.0
    up, lo = [], []
    b = 1
    while b < D:
        m = ((r[:, None] // (2 * b) == r[None] // (2 * b)) & (r[:, None] // b < r[None] // b))
        up.append(m)
        lo.append(m.T)
        b *= 2
    masks = np.stack(up + lo).transpose(1, 0, 2).astype(np.float32)
    below = -(r[:, None] > r[None]).astype(np.float32)
    from_diagonal = (np.arange(C)[None] >= r[:, None]).astype(np.float32)
    sign = np.where(r[None] > r[:, None], 1.0, -1.0).astype(np.float32)
    halves = np.broadcast_to(2.0 ** -np.arange(SQUARINGS), (D, SQUARINGS)).astype(np.float32)
    over_k = np.broadcast_to(1.0 / np.arange(TAYLOR, 0, -1), (D, TAYLOR)).astype(np.float32)
    e = np.arange(E)
    before = np.broadcast_to((e[None] < e[:, None]).astype(np.float32).reshape(1, E * E), (P, E * E))
    above = (r[:, None] < r[None]).astype(np.float32)
    small = np.concatenate([masks.reshape(D, -1), below, from_diagonal, sign, halves, over_k, above, np.ones((D, D), np.float32)], 1)
    return {"c_eye": eye, "c_sel": sel, "c_before": np.ascontiguousarray(before), "c_small": np.ascontiguousarray(small)}


def build(nc, dram):
    ctx = ExitStack()
    with ctx:
        def sb(name, shape, dt=F32):
            return ctx.enter_context(nc.sbuf_tensor(name, shape, dt))

        def sem(name):
            return ctx.enter_context(nc.semaphore(name))

        signals = {"pe": [], "act": [], "dve": [], "pool": []}

        def signal(owner, name, per):
            s = Signal(sem(name), per)
            signals[owner].append(s)
            return s

        def grant_credit(eng, owner):
            for s in signals[owner]:
                eng.sem_inc(s.sem, CREDIT)

        x = sb("x", [P, NT, C])
        w_qkv = sb("w_qkv", [CH, NC3, 3 * C])
        w_proj = sb("w_proj", [P, NG, C])
        b_qkv = sb("b_qkv", [P, 3 * C])
        g_qk = sb("g_qk", [P, 2 * C])
        gates = sb("gates", [P, B, 2, C])
        xhat = sb("xhat", [P, TB, C])
        hT = sb("hT", [CH, NC3, N])
        h2T = sb("h2T", [CH, NC3, B * N])
        tmp = sb("tmp", [P, 2, C])
        eye = sb("eye", [P, P])
        eye16 = sb("eye16", [P, P], BF16)
        sel = sb("sel", [P, P])
        before = sb("before", [P, E * E])
        w_gate = sb("w_gate", [CH, NC3, E])
        cond = sb("cond", [CH, NC3, B])
        silu = sb("silu", [CH, NC3, B])
        silu_t = sb("silu_t", [CH, NC3, B])
        mod_bias = sb("mod_bias", [CH, 3, 4 * NC3])
        modT = sb("modT", [CH, 4, NC3, B])
        stats = sb("stats", [P, TB, 6])
        meanvar = sb("meanvar", [P, TB, 2])
        var_eps = sb("var_eps", [P, 2, TB])
        rstd = sb("rstd", [P, TB])
        consts = sb("consts", [P, 2 * TB])
        half = sb("half", [D, 1])
        mx = sb("mx", [P, TB * G])
        mrest = sb("mrest", [P, TB * G])
        head_sum = sb("head_sum", [P, TB, 2 * NH])
        head_tmp = sb("head_tmp", [P, TB, 2 * NH])
        head_exp = sb("head_exp", [P, TB, 2 * NH])
        head_eps = sb("head_eps", [P, TB, 2 * NH])
        logits = sb("logits", [P, NT, E])
        cw = sb("cw", [P, NT, E])
        A = sb("A", [D, B, D])
        w_a = sb("w_a", [P, W_BYTES // 4])
        arena = sb("arena", [P, A_END // 4])
        assert I_BS + D * D * 4 <= A_END and M_W1 + 6 * C * NC3 * 4 + 2 * C * 4 <= M_LIN

        def at(base, n, dt=F32, p=P):
            a = arena[0:p, base // 4:base // 4 + (n * (2 if dt == BF16 else 4) + 3) // 4]
            return a.bitcast(BF16) if dt == BF16 else a

        qkv = at(A_QKV, TB * 3 * C).rearrange("p (t c) -> p t c", t=TB)
        vg = [at(A_V + i * TB * G * HP * 4, TB * G * HP).rearrange("p (t c) -> p t c", t=TB) for i in range(2)]
        kp = [at(A_KP + i * TB * G * 224, TB * G * 112, BF16).rearrange("p (h c) -> p h c", c=112) for i in range(2)]
        qp = [at(A_QP + i * TB * G * 224, TB * G * 112, BF16).rearrange("p (h c) -> p h c", c=112) for i in range(2)]
        SPL = TB * GW * 8
        rest = [at(A_SPL + i * SPL, TB * GW) for i in range(2)]
        part_h = [at(A_SPL + i * SPL + TB * GW * 4, TB * GW, BF16) for i in range(2)]
        part_m = [at(A_SPL + i * SPL + TB * GW * 6, TB * GW, BF16) for i in range(2)]
        kT = [at(A_KT + i * G * N * 2, G * N, BF16).rearrange("p (h n) -> p h n", h=G) for i in range(2)]
        qT = [at(A_QT + i * G * N * 2, G * N, BF16).rearrange("p (h n) -> p h n", h=G) for i in range(2)]
        pT = at(A_PT, 2 * G * N).rearrange("p (i n) -> p i n", i=2)
        square = at(A_PT, TB * 2 * C).rearrange("p (t c) -> p t c", t=TB)
        oT = at(A_OT, NG * N).rearrange("p (g n) -> p g n", g=NG)
        rD = at(A_RD, N)
        hid = at(M_HID, MH * N).rearrange("p (m n) -> p m n", m=MH)
        top = at(M_HID, 6 * NT * E * E)

        def expert(flat):
            o = NC3 * HID
            return (flat[0:CH, 0:o].rearrange("p (c n) -> p c n", c=NC3),
                    flat[:, o:o + MH * C].rearrange("p (m n) -> p m n", m=MH),
                    flat[:, o + MH * C:o + MH * C + C], flat[:, o + MH * C + C:o + MH * C + C + MH])

        experts = [expert(w_a[:, :]), expert(at(M_W1, W_BYTES // 4))]
        w_mod = at(M_W1, NC3 * 6 * C, p=CH).rearrange("p (c n) -> p c n", c=NC3)
        gate_bias = at(M_W1 + NC3 * 6 * C * 4, 2 * C).rearrange("p (i n) -> p i n", i=2)
        silu_b = at(M_HID, NC3 * B * P, p=CH).rearrange("p (i n) -> p i n", n=P)
        w_skew = [at(I_WS + i * NC3 * 2048, NC3 * 512, p=CH).rearrange("p (c n) -> p c n", c=NC3) for i in range(2)]
        b_skew = at(I_BS, D * D, p=B)
        v_skew = h2T[0:B, :, :].rearrange("p c n -> p (c n)")[:, 0:D * D]

        lin_at = [M_LIN]

        def lin(n, p=D):
            a = at(lin_at[0], n, p=p)
            lin_at[0] += n * 4 + (-n * 4) % 32
            assert lin_at[0] <= A_END
            return a

        small = lin(16 * D + C + SQUARINGS + TAYLOR)
        o = 12 * D
        level_masks = small[:, 0:o].rearrange("p (l n) -> p l n", l=12)
        below = small[:, o:o + D]
        from_diag = small[:, o + D:o + D + C]
        sign = small[:, o + D + C:o + 2 * D + C]
        halves = small[:, o + 2 * D + C:o + 2 * D + C + SQUARINGS]
        over_k = small[:, o + 2 * D + C + SQUARINGS:o + 2 * D + C + SQUARINGS + TAYLOR]
        o += 2 * D + C + SQUARINGS + TAYLOR
        above = small[:, o:o + D]
        eye_row = small[0:1, o + D:o + 2 * D]
        pick = lin(P)
        pT_ = lin(C + D)
        vb = lin(C)
        junk = lin(C)
        hs = lin(16)
        nbs = lin(D)
        cs = lin(D)
        uT = lin(C)
        vT = lin(C)
        inv = lin(2 * D).rearrange("p (i n) -> p i n", i=2)
        lev = lin(2 * D).rearrange("p (i n) -> p i n", i=2)
        mm = lin(2 * D).rearrange("p (i n) -> p i n", i=2)
        prod = lin(2 * D).rearrange("p (i n) -> p i n", i=2)
        tT = lin(D)
        zT_ = lin(D)
        v_c = lin(NC3 * D, p=CH).rearrange("p (c n) -> p c n", c=NC3)
        u_c = lin(NC3 * D, p=CH).rearrange("p (c n) -> p c n", c=NC3)
        xs = lin(2 * B * D).rearrange("p (i n) -> p i n", i=2)
        ex = lin(2 * B * D)
        ex_t = lin(2 * B * D)
        flags = lin(SQUARINGS + 8)
        w_rot = lin(B * C).rearrange("p (b n) -> p b n", b=B)
        zT = lin(N)

        psS = ctx.enter_context(nc.psum_tensor("psS", [P, 4, 512], F32))
        psM = ctx.enter_context(nc.psum_tensor("psM", [P, 2, 512], F32))
        psO = ctx.enter_context(nc.psum_tensor("psO", [P, 512], F32))
        psT = ctx.enter_context(nc.psum_tensor("psT", [P, 512], F32))
        banks3 = [psT[:, :], psM[:, 0, :], psM[:, 1, :]]
        banks3_16 = [b.bitcast(BF16) for b in banks3]
        SET_BANK = (0, 1, 2, 0, 0, 1)

        scratch = nc.dram_tensor("skew_scratch", [B, D * D], F32, kind="Internal").ap()

        s_const = sem("constants_loaded")
        s_start = sem("start_inputs_loaded")
        s_x = sem("x_loaded")
        s_attw = [sem(f"attention_weights_loaded_{l}") for l in range(3)]
        s_modw = [sem(f"mod_weights_loaded_{l}") for l in range(3)]
        s_mlpw = [sem(f"expert_weights_loaded_{q}") for q in range(E + 2)]
        s_skew_w = [sem(f"skew_weights_loaded_{i}") for i in range(2)]
        s_skew_b = sem("skew_bias_loaded")
        s_skew_out = sem("skew_stored")
        s_skew_in = sem("skew_loaded")
        s_lin = sem("rotation_inputs_loaded")
        s_out = sem("output_stored")
        s_init = sem("constant_tiles_set")
        s_exp0 = sem("silu_exp_done")
        s_silu = sem("silu_ready")
        s_silu_b = sem("silu_spread")
        s_skew_mm = sem("skew_product_done")
        s_skew_v = sem("skew_rows_ready")
        s_mod_mm = sem("mod_product_done")
        s_mod = sem("mod_ready")
        s_top = sem("top2_steps")
        s_top_exp = sem("top2_exp_done")
        s_top_in = sem("top2_exp_asked")
        s_modstep = sem("mod_steps")
        s_passed_pool = sem("pool_waits_passed")
        s_passed_dve = sem("vector_waits_passed")
        s_passed_pe = sem("tensor_waits_passed")
        s_eye = sem("eye16_and_silu_steps")
        s_lin_dve = sem("rotation_vector_steps")
        s_lin_pe = sem("rotation_products")

        ln_stats = signal("dve", "ln_stats", TB)
        ln_mv = signal("dve", "ln_meanvar", TB)
        ln_eps = signal("pool", "ln_var_eps", 1)
        ln_rstd = signal("pool", "ln_rstd", 1)
        ln_xhat = signal("dve", "ln_normalised", TB)
        ln_T = signal("pe", "ln_transposed", NC3)
        h_ready = signal("act", "modulated", NC3)
        h2_ready = signal("pool", "mlp_input_kept", 1)
        qkv_mm = signal("pe", "qkv_product", 2 * TB)
        qkv_ready = signal("dve", "qkv_ready", 2 * TB)
        qkn = signal("dve", "qk_norm_steps", 8)
        sq_ready = signal("dve", "qk_squares", 2)
        qkn_eps = signal("pool", "qk_var_eps", 1)
        qkn_rstd = signal("pool", "qk_rstd", 1)
        split = signal("dve", "split_steps", 6 * NG)
        split_ready = signal("dve", "split_ready", 2 * NG)
        rep_done = signal("pool", "parts_stacked", 2 * NG)
        v_staged = signal("pool", "v_staged", NG)
        t_mm = signal("pe", "heads_transposed", 6 * NG)
        t_ev = signal("act", "heads_copied", 6 * NG)
        max_mm = signal("pe", "max_scores", 16 * NG)
        max_done = signal("dve", "max_taken", 16 * NG)
        mparts = signal("dve", "max_split_steps", 3 * NG)
        m_ready = signal("dve", "max_parts_ready", NG)
        s_mm = signal("pe", "scores_ready", 8 * NG)
        exp_done = signal("act", "exp_done", 8 * NG)
        av_done = signal("pe", "values_summed", 4 * NG)
        o_raw = signal("dve", "sums_copied", NG)
        d_mm = signal("pe", "denominators_spread", NG)
        recip = signal("dve", "denominators_inverted", NG)
        o_ready = signal("dve", "heads_ready", NG)
        proj_mm = signal("pe", "projected", TB)
        proj_read = signal("dve", "projection_gated", TB)
        x1_ready = signal("dve", "x_after_attention", TB)
        gate_mm = signal("pe", "gate_product", 1)
        gate_read = signal("dve", "gate_logits_kept", 1)
        f1_mm = signal("pe", "hidden_product", MH)
        hid_ready = signal("act", "hidden_ready", MH)
        f2_mm = signal("pe", "mlp_product", TB)
        f2_read = signal("dve", "mlp_bias_added", TB)
        f2_scaled = signal("dve", "mlp_gated", TB)
        x2_ready = signal("dve", "x_after_mlp", TB)
        hh_pick = signal("pool", "householder_row_picked", 1)
        hh_mm = signal("pe", "householder_column_spread", 1)
        hh_step = signal("dve", "householder_steps", 11)
        hh_nrm2 = signal("dve", "householder_norm2", 1)
        hh_nrm = signal("pool", "householder_norm", 1)
        hh_w = signal("dve", "householder_weights", 1)
        hh_upd = signal("dve", "householder_applied", 1)
        ho_mm = signal("pe", "series_product", 1)
        ho_dve = signal("dve", "series_term_added", 1)
        sq_mm = signal("pe", "square_product", 1)
        sq_t = signal("dve", "square_difference", 1)
        sq_dve = signal("dve", "square_taken", 1)
        rt_x = signal("dve", "rotation_x_copied", 1)
        rt_T = signal("pe", "rotation_x_transposed", NC3)
        rt_h = signal("act", "rotation_xT_copied", NC3)
        rt_z = signal("pe", "rotation_z", 1)
        rt_zc = signal("dve", "rotation_z_copied", 1)
        rt_mm = signal("pe", "rotation_product", TB)
        rt_add = signal("dve", "rotation_added", TB)

        ITER0 = (0, 4 * E, 4 * E + 4)
        NE = (E, 1, 1)
        WSET = (0, E, E + 1)

        block = ctx.enter_context(nc.Block())

        @block.sync
        def _(sp):
            def load_attention(l):
                n = LAYERS[l]
                sp.dma_start(w_qkv[:, :, :], dram[n + "_w_qkv"].rearrange("(c p) n -> p c n", p=CH)).then_inc(s_attw[l], 16)
                sp.dma_start(w_proj[:, :, :], dram[n + "_w_proj"]).then_inc(s_attw[l], 16)
                sp.dma_start(b_qkv[:, :], dram[n + "_b_qkv"].partition_broadcast(P)).then_inc(s_attw[l], 16)

            def load_mod(l):
                n = LAYERS[l]
                sp.dma_start(w_mod, dram[n + "_w_mod"].rearrange("(c p) n -> p c n", p=CH)).then_inc(s_modw[l], 16)
                for i, k in ((0, 2), (1, 5)):
                    sp.dma_start(gate_bias[:, i, :], dram[n + "_b_mod"][k * C:(k + 1) * C].partition_broadcast(P)).then_inc(s_modw[l], 16)

            def load_expert(l, e):
                n, q = LAYERS[l], WSET[l] + e
                w1, w2, b2, b1 = experts[e % 2]
                sp.dma_start(w1, dram[n + "_w1"][e].rearrange("(c p) n -> p c n", p=CH)).then_inc(s_mlpw[q], 16)
                sp.dma_start(w2, dram[n + "_w2"][e].rearrange("(m p) n -> p m n", p=P)).then_inc(s_mlpw[q], 16)
                sp.dma_start(b2, dram[n + "_b2"][e].partition_broadcast(P)).then_inc(s_mlpw[q], 16)
                sp.dma_start(b1, dram[n + "_b1"][e]).then_inc(s_mlpw[q], 16)

            sp.dma_start(cond[:, :, :], dram["cond"]).then_inc(s_start, 16)
            sp.dma_start(mod_bias[:, :, :], dram["mod_bias"]).then_inc(s_start, 16)
            sp.dma_start(eye[:, :], dram["c_eye"]).then_inc(s_const, 16)
            sp.dma_start(sel[:, :], dram["c_sel"]).then_inc(s_const, 16)
            sp.dma_start(before[:, :], dram["c_before"]).then_inc(s_const, 16)
            load_mod(0)
            sp.dma_start(x[:, :, :], dram["x"].rearrange("b (t p) c -> p (b t) c", p=P)).then_inc(s_x, 16)
            load_attention(0)
            sp.dma_start(b_skew, dram["b_skew"].partition_broadcast(B)).then_inc(s_skew_b, 16)
            for i in range(8):
                if i >= 2:
                    sp.wait_ge(s_skew_mm, i - 1)
                sp.dma_start(w_skew[i % 2], dram["w_skew"][:, i * 512:(i + 1) * 512].rearrange("(c p) n -> p c n", p=CH)).then_inc(s_skew_w[i % 2], 16)
            load_expert(0, 0)
            sp.dma_start(w_gate[:, :, :], dram["w_gate"].rearrange("(c p) n -> p c n", p=CH)).then_inc(s_start, 16)
            sp.dma_start(g_qk[:, 0:C], dram["g_q"].partition_broadcast(P)).then_inc(s_start, 16)
            sp.dma_start(g_qk[:, C:2 * C], dram["g_k"].partition_broadcast(P)).then_inc(s_start, 16)
            sp.wait_ge(s_skew_v, 8)
            sp.dma_start(scratch, v_skew).then_inc(s_skew_out, 16)
            sp.wait_ge(s_skew_out, 16)
            sp.dma_start(A[:, :, :], scratch.rearrange("b (i j) -> i b j", j=D)).then_inc(s_skew_in, 16)
            sp.wait_ge(proj_mm.sem, proj_mm.at(B, 0))
            load_expert(0, 1)
            sp.dma_start(small, dram["c_small"]).then_inc(s_lin, 16)
            sp.dma_start(pT_, dram["pT"]).then_inc(s_lin, 16)
            load_attention(1)
            sp.wait_ge(f2_mm.sem, f2_mm.at(4, 0))
            sp.wait_ge(x2_ready.sem, x2_ready.at(4, 0))
            load_expert(0, 2)
            sp.wait_ge(f2_mm.sem, f2_mm.at(8, 0))
            sp.wait_ge(x2_ready.sem, x2_ready.at(8, 0))
            load_expert(0, 3)
            sp.wait_ge(f2_mm.sem, f2_mm.at(12, 0))
            sp.wait_ge(x2_ready.sem, x2_ready.at(12, 0))
            load_expert(1, 0)
            sp.wait_ge(f2_mm.sem, f2_mm.at(16, 0))
            sp.wait_ge(x2_ready.sem, x2_ready.at(16, 0))
            load_mod(1)
            sp.wait_ge(proj_mm.sem, proj_mm.at(2 * B, 0))
            load_attention(2)
            load_mod(2)
            sp.wait_ge(f2_mm.sem, f2_mm.at(20, 0))
            sp.wait_ge(x2_ready.sem, x2_ready.at(20, 0))
            load_expert(2, 0)
            for b in range(B):
                sp.wait_ge(x2_ready.sem, x2_ready.at(21 + b, 0))
                sp.dma_start(dram["out"][b].rearrange("(t p) c -> p t c", p=P), x[:, TB * b:TB * (b + 1), :]).then_inc(s_out, 16)
            sp.wait_ge(s_out, 16 * B)

        @block.gpsimd
        def _(pool):
            grant_credit(pool, "pool")
            def settle():
                pool.sem_inc(s_passed_pool, 1)

            nc.gpsimd.memset(consts[:, 0:TB], -0.5)
            nc.gpsimd.memset(consts[:, TB:2 * TB], EPS)
            nc.gpsimd.memset(half[:, :], 0.5)
            nc.gpsimd.memset(head_exp[:, :, :], -0.5).then_inc(s_init, 1)
            pool.wait_ge(s_init, 1)

            def ln_root(m):
                pool.wait_ge(ln_mv.sem, ln_mv.at(m, TB))
                nc.gpsimd.tensor_tensor(var_eps[:, 0, :], meanvar[:, :, 1], consts[:, TB:2 * TB], ALU.add).then_inc(ln_eps.sem, 1)
                pool.wait_ge(ln_eps.sem, ln_eps.at(m, 1))
                pool.wait_ge(ln_xhat.sem, ln_xhat.at(m, 0))
                nc.gpsimd.tensor_tensor(rstd[:, :], var_eps[:, 0, :], consts[:, 0:TB], ALU.pow).then_inc(ln_rstd.sem, 1)

            def spread_silu(l):
                if l:
                    pool.wait_ge(f2_mm.sem, f2_mm.at(ITER0[l], 0))
                nc.gpsimd.tensor_copy(silu_b, silu[:, :, :].rearrange("p c b -> p (c b)").unsqueeze(2).to_broadcast([CH, NC3 * B, P])).then_inc(s_silu_b, 1)

            def attention(l):
                with pool.Fori(0, B) as b:
                    n = b + l * B
                    ln_root(n * 2)
                    if l == 1:
                        pool.wait_ge(qkn.sem, qkn.at(b, 4))
                        nc.gpsimd.tensor_tensor(head_tmp[:, :, :], head_tmp[:, :, :], eps_t[:, :, :], ALU.add).then_inc(qkn_eps.sem, 1)
                        pool.wait_ge(qkn_eps.sem, qkn_eps.at(b, 1))
                        nc.gpsimd.tensor_tensor(head_tmp[:, :, :], head_tmp[:, :, :], head_exp[:, :, :], ALU.pow).then_inc(qkn_rstd.sem, 1)
                    for g in range(NG):
                        if g == 0:
                            pool.wait_ge(qkv_ready.sem, qkv_ready.at(n, 2 * TB))
                        pool.wait_ge(av_done.sem, av_done.at(n, 4 * (g - 1)))
                        settle()
                        nc.gpsimd.tensor_copy(
                            vg[g % 2].rearrange("p t (h c) -> p t h c", c=HP)[:, :, :, 0:HD],
                            qkv[:, :, 2 * C + g * GW:2 * C + (g + 1) * GW].rearrange("p t (h c) -> p t h c", c=HD)).then_inc(v_staged.sem, 1)
                        for i, parts in ((0, kp), (1, qp)):
                            pool.wait_ge(split_ready.sem, split_ready.at(n, 2 * g + i + 1))
                            settle()
                            def stack(part, slots):
                                src = part[i].rearrange("p (h c) -> p h c", c=HD)
                                dst = parts[g % 2][:, :, 0:KM].rearrange("p h (s c) -> p h s c", c=HD)[:, :, slots, :]
                                k = dst.shape[2]
                                return nc.gpsimd.tensor_copy(dst, src.unsqueeze(2).to_broadcast([P, TB * G, k, HD]))
                            stack(part_h, slice(0, 3) if i == 0 else slice(1, 6, 2))
                            stack(part_m, slice(3, 5) if i == 0 else slice(2, 5, 2)).then_inc(rep_done.sem, 1)
                    ln_root(n * 2 + 1)
                    pool.wait_ge(h_ready.sem, h_ready.at(n * 2 + 2, 0))
                    settle()
                    nc.gpsimd.tensor_copy(h2T[:, :, bass.ds(b * N, N)], hT[:, :, :]).then_inc(h2_ready.sem, 1)

            nc.gpsimd.memset(var_eps[:, 1, :], EPS)
            eps_t = head_eps
            nc.gpsimd.memset(eps_t[:, :, :], EPS).then_inc(s_init, 1)
            pool.wait_ge(s_init, 2)
            pool.wait_ge(s_silu, 1)
            spread_silu(0)

            def set_stage_constants(l):
                pool.wait_ge(s_mod, 9 * (l + 1))
                if l == 0:
                    pool.wait_ge(s_skew_v, 8)
                for i in range(2):
                    v = vg[i].rearrange("p t (h c) -> p (t h) c", c=HP)
                    nc.gpsimd.memset(v[:, :, HD:HD + 1], 1.0)
                    nc.gpsimd.memset(v[:, :, HD + 1:HP], 0.0)
                    nc.gpsimd.memset(kp[i][:, :, KM:KS], 1.0).then_inc(s_init, 1)

            set_stage_constants(0)
            pool.wait_ge(s_skew_out, 16)
            attention(0)
            pool.wait_ge(s_const, 48)
            pool.wait_ge(x1_ready.sem, x1_ready.at(B, 0))
            pool.wait_ge(o_ready.sem, o_ready.at(B, 0))
            with pool.Fori(0, D) as j:
                pool.wait_ge(hh_mm.sem, hh_mm.at(j, 0))
                settle()
                nc.gpsimd.tensor_copy(pick[:, :], eye[0:D, bass.ds(j, 1)].to_broadcast([D, P])).then_inc(hh_pick.sem, 1)
                pool.wait_ge(hh_nrm2.sem, hh_nrm2.at(j, 1))
                nc.gpsimd.tensor_tensor(hs[:, 2:3], hs[:, 1:2], half[:, :], ALU.pow).then_inc(hh_nrm.sem, 1)
            spread_silu(1)
            set_stage_constants(1)
            attention(1)
            spread_silu(2)
            set_stage_constants(2)
            attention(2)

        @block.scalar
        def _(act):
            grant_credit(act, "act")

            def modulate(m, b, kind):
                for c in range(NC3):
                    act.wait_ge(ln_T.sem, ln_T.at(m, c + 1))
                    nc.scalar.activation(hT[:, c, :], banks3[c][0:CH, :], ACT.Identity,
                                         bias=modT[:, kind, c, bass.ds(b, 1)],
                                         scale=modT[:, kind + 1, c, bass.ds(b, 1)]).then_inc(h_ready.sem, 1)

            def copy_heads(n, g, i):
                rows = KM if i in (2, 3) else KS
                dst = (kT if i < 2 else qT)[g % 2]
                act.wait_ge(t_mm.sem, t_mm.at(n, 6 * g + i + 1))
                h = i % 2
                nc.scalar.activation(dst[0:rows, 2 * h:2 * h + 2, :],
                                     banks3_16[SET_BANK[i]][0:rows, :].rearrange("p (h n) -> p h n", h=2),
                                     ACT.Copy).then_inc(t_ev.sem, 1)

            def attention(l):
                with act.Fori(0, B) as b:
                    n = b + l * B
                    act.wait_ge(h2_ready.sem, h2_ready.at(n, 0))
                    modulate(n * 2, b, 0)
                    for i in range(6):
                        copy_heads(n, 0, i)
                    for g in range(NG):
                        if g + 1 < NG:
                            for i in range(4):
                                copy_heads(n, g + 1, i)
                        for kb in range(TB):
                            for h in range(2):
                                if h == 0:
                                    act.wait_ge(av_done.sem, av_done.at(n, 4 * g + kb - 1))
                                act.wait_ge(s_mm.sem, s_mm.at(n, 8 * g + 2 * kb + h + 1))
                                nc.scalar.activation(pT[:, kb % 2, 1024 * h:1024 * (h + 1)],
                                                     psS[:, 2 * h:2 * h + 2, :].rearrange("p a n -> p (a n)"),
                                                     ACT.Exp, scale=SCALE).then_inc(exp_done.sem, 1)
                        if g + 1 < NG:
                            for i in (4, 5):
                                copy_heads(n, g + 1, i)
                    modulate(n * 2 + 1, b, 2)

            def mlp(l, e):
                b1 = experts[e % 2][3]
                act.wait_ge(s_mlpw[WSET[l] + e], 64)
                with act.Fori(0, B) as b:
                    q = b + (ITER0[l] + B * e)
                    for m in range(MH):
                        if m == 0:
                            act.wait_ge(f2_mm.sem, f2_mm.at(q, 0))
                        act.wait_ge(f1_mm.sem, f1_mm.at(q, m + 1))
                        nc.scalar.activation(hid[:, m, :], psS[:, m % 4, :], ACT.Gelu_apprx_tanh,
                                             bias=b1[:, m:m + 1]).then_inc(hid_ready.sem, 1)

            act.wait_ge(s_start, 32)
            nc.scalar.activation(silu_t[:, :, :], cond[:, :, :], ACT.Exp, scale=-1.0).then_inc(s_exp0, 1)
            act.wait_ge(s_mod, 9)
            attention(0)
            act.wait_ge(s_top_in, 1)
            nc.scalar.activation(top[:, 0:NT * E], top[:, 0:NT * E], ACT.Exp).then_inc(s_top_exp, 1)
            act.wait_ge(s_top, TOP_STEPS)
            for e in range(E):
                mlp(0, e)
            with act.Fori(0, B) as b:
                for c in range(NC3):
                    act.wait_ge(rt_T.sem, rt_T.at(b, c + 1))
                    nc.scalar.activation(hT[:, c, :], banks3[c][0:CH, :], ACT.Copy).then_inc(rt_h.sem, 1)
            act.wait_ge(s_mod, 18)
            attention(1)
            act.wait_ge(o_ready.sem, o_ready.at(2 * B, 0))
            mlp(1, 0)
            act.wait_ge(s_mod, 27)
            attention(2)
            act.wait_ge(o_ready.sem, o_ready.at(3 * B, 0))
            mlp(2, 0)

        @block.vector
        def _(dve):
            grant_credit(dve, "dve")
            v = nc.vector
            def settle():
                dve.sem_inc(s_passed_dve, 1)

            def layer_norm(m, b):
                for t in range(TB):
                    v.bn_stats(stats[:, t, :], x[:, b * TB + t, :]).then_inc(ln_stats.sem, 1)
                for t in range(TB):
                    dve.wait_ge(ln_stats.sem, ln_stats.at(m, t + 1))
                    settle()
                    v.bn_aggr(meanvar[:, t, :], stats[:, t, :]).then_inc(ln_mv.sem, 1)
                dve.wait_ge(ln_T.sem, ln_T.at(m, 0))
                dve.wait_ge(ln_rstd.sem, ln_rstd.at(m, 1))
                for t in range(TB):
                    v.tensor_scalar(xhat[:, t, :], x[:, b * TB + t, :], meanvar[:, t, 0:1], rstd[:, t:t + 1],
                                    ALU.subtract, ALU.mult).then_inc(ln_xhat.sem, 1)

            def qk_norm(b):
                heads = qkv[:, :, 0:2 * C].rearrange("p t (h c) -> p t h c", c=HD)
                sq = square.rearrange("p t (h c) -> p t h c", c=HD)

                def step(ins, k):
                    ins.then_inc(qkn.sem, 1)
                    dve.wait_ge(qkn.sem, qkn.at(b, k))

                def wide(a):
                    return a.unsqueeze(3).to_broadcast([P, TB, 2 * NH, HD])

                step(v.tensor_reduce(head_sum[:, :, :], heads, AX_X, ALU.add), 1)
                step(v.tensor_scalar(head_sum[:, :, :], head_sum[:, :, :], 1.0 / HD, None, ALU.mult), 2)
                for t in range(TB):
                    last = v.tensor_tensor(heads[:, t], heads[:, t], wide(head_sum[:, :, :])[:, t], ALU.subtract)
                last.then_inc(qkn.sem, 1)
                dve.wait_ge(qkn.sem, qkn.at(b, 3))
                v.tensor_tensor(square, qkv[:, :, 0:2 * C], qkv[:, :, 0:2 * C], ALU.mult).then_inc(sq_ready.sem, 1)
                dve.wait_ge(sq_ready.sem, sq_ready.at(b, 1))
                v.tensor_reduce(head_sum[:, :, :], sq, AX_X, ALU.add).then_inc(sq_ready.sem, 1)
                dve.wait_ge(sq_ready.sem, sq_ready.at(b, 2))
                v.tensor_scalar(head_tmp[:, :, :], head_sum[:, :, :], 1.0 / HD, None, ALU.mult).then_inc(qkn.sem, 1)
                v.tensor_tensor(qkv[:, :, 0:2 * C], qkv[:, :, 0:2 * C],
                                g_qk[:, :].unsqueeze(1).to_broadcast([P, TB, 2 * C]), ALU.mult).then_inc(qkn.sem, 1)
                dve.wait_ge(qkn.sem, qkn.at(b, 5))
                dve.wait_ge(qkn_rstd.sem, qkn_rstd.at(b, 1))
                for t in range(TB):
                    last = v.tensor_tensor(heads[:, t], heads[:, t], wide(head_tmp[:, :, :])[:, t], ALU.mult)
                last.then_inc(qkn.sem, 1)
                dve.wait_ge(qkn.sem, qkn.at(b, 6))
                dve.sem_inc(qkn.sem, 2)

            def split_group(n, g):
                for i, (parts, col, low) in enumerate(((kp, C, 5), (qp, 0, 0))):
                    src = qkv[:, :, col + g * GW:col + (g + 1) * GW]
                    r = rest[i].rearrange("p (t c) -> p t c", t=TB)
                    h = part_h[i].rearrange("p (t c) -> p t c", t=TB)
                    k0 = 6 * g + 3 * i
                    dve.wait_ge(rep_done.sem, rep_done.at(n, 2 * (g - 1) + i + 1))
                    v.tensor_copy(h, src).then_inc(split.sem, 1)
                    dve.wait_ge(split.sem, split.at(n, k0 + 1))
                    v.tensor_tensor(r, src, h, ALU.subtract).then_inc(split.sem, 1)
                    dve.wait_ge(split.sem, split.at(n, k0 + 2))
                    v.tensor_copy(part_m[i], rest[i]).then_inc(split.sem, 1)
                    dve.wait_ge(t_mm.sem, t_mm.at(n, 6 * (g - 1)))
                    dve.wait_ge(split.sem, split.at(n, k0 + 3))
                    v.tensor_tensor(parts[g % 2][:, :, low * HD:(low + 1) * HD], rest[i].rearrange("p (h c) -> p h c", c=HD),
                                    part_m[i].rearrange("p (h c) -> p h c", c=HD), ALU.subtract).then_inc(split_ready.sem, 1)

            def maxima(n, g):
                for j in range(G):
                    for t in range(TB):
                        i = 16 * g + 4 * j + t
                        dve.wait_ge(max_mm.sem, max_mm.at(n, i + 1))
                        v.tensor_reduce(mx[:, t * G + j:t * G + j + 1], psM[:, t % 2, :], AX_X, ALU.max).then_inc(max_done.sem, 1)
                neg = [qp[g % 2][:, :, KM + i] for i in range(3)]
                dve.wait_ge(rep_done.sem, rep_done.at(n, 2 * g + 2))
                dve.wait_ge(max_done.sem, max_done.at(n, 16 * (g + 1)))
                v.tensor_scalar(neg[0], mx[:, :], -1.0, None, ALU.mult).then_inc(mparts.sem, 1)
                dve.wait_ge(mparts.sem, mparts.at(n, 3 * g + 1))
                v.scalar_tensor_tensor(out=mrest[:, :], in0=mx[:, :], scalar=-1.0, in1=neg[0], op0=ALU.mult,
                                       op1=ALU.subtract).then_inc(mparts.sem, 1)
                dve.wait_ge(mparts.sem, mparts.at(n, 3 * g + 2))
                v.tensor_copy(neg[1], mrest[:, :]).then_inc(mparts.sem, 1)
                dve.wait_ge(mparts.sem, mparts.at(n, 3 * g + 3))
                v.tensor_tensor(neg[2], mrest[:, :], neg[1], ALU.subtract).then_inc(m_ready.sem, 1)

            def close_group(n, g):
                if g == 0:
                    dve.wait_ge(proj_mm.sem, proj_mm.at(n, 0))
                dve.wait_ge(av_done.sem, av_done.at(n, 4 * g + 4))
                v.tensor_copy(oT[:, g, :], psO[:, :]).then_inc(o_raw.sem, 1)
                dve.wait_ge(d_mm.sem, d_mm.at(n, g + 1))
                v.reciprocal(rD, psM[:, 1, :]).then_inc(recip.sem, 1)
                dve.wait_ge(recip.sem, recip.at(n, g + 1))
                v.tensor_tensor(oT[:, g, :], oT[:, g, :], rD, ALU.mult).then_inc(o_ready.sem, 1)

            def attention(l):
                dve.wait_ge(s_attw[l], 48)
                with dve.Fori(0, B) as b:
                    n = b + l * B
                    layer_norm(n * 2, b)
                    dve.wait_ge(v_staged.sem, v_staged.at(n, 0))
                    for i in range(2 * TB):
                        t, h = divmod(i, 2)
                        w = 3 * C // 2
                        dve.wait_ge(qkv_mm.sem, qkv_mm.at(n, i + 1))
                        v.tensor_tensor(qkv[:, t, h * w:(h + 1) * w], psS[:, i % 4, 0:w], b_qkv[:, h * w:(h + 1) * w],
                                        ALU.add).then_inc(qkv_ready.sem, 1)
                    dve.wait_ge(qkv_ready.sem, qkv_ready.at(n, 2 * TB))
                    if l == 1:
                        qk_norm(b)
                    split_group(n, 0)
                    split_group(n, 1)
                    maxima(n, 0)
                    for g in range(NG):
                        if g + 1 < NG:
                            maxima(n, g + 1)
                        if g + 2 < NG:
                            split_group(n, g + 2)
                        close_group(n, g)
                    for t in range(TB):
                        dve.wait_ge(proj_mm.sem, proj_mm.at(n, t + 1))
                        v.tensor_tensor(tmp[:, t % 2, :], psS[:, t, 0:C], gates[:, b, 0, :], ALU.mult).then_inc(proj_read.sem, 1)
                        dve.wait_ge(proj_read.sem, proj_read.at(n, t + 1))
                        v.tensor_tensor(x[:, b * TB + t, :], x[:, b * TB + t, :], tmp[:, t % 2, :], ALU.add).then_inc(x1_ready.sem, 1)
                    dve.wait_ge(x1_ready.sem, x1_ready.at(n, TB))
                    settle()
                    layer_norm(n * 2 + 1, b)
                    if l == 0:
                        dve.wait_ge(gate_mm.sem, gate_mm.at(b, 1))
                        v.tensor_copy(logits[:, bass.ds(b * TB, TB), :].rearrange("p t e -> p (t e)"),
                                      psT[:, 0:TB * E]).then_inc(gate_read.sem, 1)

            def mlp_out(l, q, b, e):
                b2 = experts[e % 2][2]
                for t in range(TB):
                    xt = x[:, b * TB + t, :]
                    dve.wait_ge(f2_mm.sem, f2_mm.at(q, t + 1))
                    v.tensor_tensor(tmp[:, t % 2, :], psM[:, t % 2, 0:C], b2, ALU.add).then_inc(f2_read.sem, 1)
                    dve.wait_ge(f2_read.sem, f2_read.at(q, t + 1))
                    if l == 0:
                        v.scalar_tensor_tensor(out=tmp[:, t % 2, :], in0=tmp[:, t % 2, :], scalar=cw[:, b * TB + t, e:e + 1],
                                               in1=gates[:, b, 1, :], op0=ALU.mult, op1=ALU.mult).then_inc(f2_scaled.sem, 1)
                    else:
                        v.tensor_tensor(tmp[:, t % 2, :], tmp[:, t % 2, :], gates[:, b, 1, :], ALU.mult).then_inc(f2_scaled.sem, 1)
                    dve.wait_ge(f2_scaled.sem, f2_scaled.at(q, t + 1))
                    v.tensor_tensor(xt, xt, tmp[:, t % 2, :], ALU.add).then_inc(x2_ready.sem, 1)

            def mods(l):
                dve.wait_ge(s_modw[l], 48)
                if l:
                    dve.wait_ge(h_ready.sem, h_ready.at(2 * B * l, 0))
                    dve.wait_ge(x2_ready.sem, x2_ready.at(ITER0[l], 0))
                dve.wait_ge(s_mod_mm, 9 * l + 1)
                flat = modT[:, :, :, :].rearrange("p k c b -> p (k c) b")
                v.tensor_tensor(flat, psM[0:CH, 0, 0:4 * NC3 * B].rearrange("p (k b) -> p k b", b=B),
                                mod_bias[:, l, :].unsqueeze(2).to_broadcast([CH, 4 * NC3, B]), ALU.add).then_inc(s_modstep, 1)
                dve.wait_ge(s_modstep, 3 * l + 1)
                for k in (1, 3):
                    ins = v.tensor_scalar(modT[:, k, :, :], modT[:, k, :, :], 1.0, None, ALU.add)
                    ins.then_inc(s_modstep, 1)
                dve.wait_ge(s_modstep, 3 * l + 3)
                dve.sem_inc(s_mod, 1)
                for i in range(2 * B):
                    dve.wait_ge(s_mod_mm, 9 * l + 2 + i)
                    v.tensor_tensor(gates[:, i // 2, i % 2, :], psS[:, i % 4, 0:C], gate_bias[:, i % 2, :], ALU.add).then_inc(s_mod, 1)
                dve.wait_ge(s_mod, 9 * l + 9)

            def top_two():
                count = [0]

                def step(ins):
                    count[0] += 1
                    ins.then_inc(s_top, 1)
                    dve.wait_ge(s_top, count[0])

                lg = logits[:, :, :]
                d = top[:, 0:NT * E].rearrange("p (t e) -> p t e", e=E)
                big = NT * E * E
                ge = top[:, big:2 * big].rearrange("p (t e f) -> p t e f", e=E, f=E)
                gt = top[:, 2 * big:3 * big].rearrange("p (t e f) -> p t e f", e=E, f=E)
                one = top[:, 3 * big:3 * big + NT]
                inv_s = top[:, 3 * big + NT:3 * big + 2 * NT]
                rank = top[:, 4 * big:4 * big + NT * E].rearrange("p (t e) -> p t e", e=E)
                dve.wait_ge(gate_read.sem, gate_read.at(B, 0))
                dve.wait_ge(o_ready.sem, o_ready.at(B, 0))
                dve.wait_ge(split_ready.sem, split_ready.at(B, 0))
                step(v.tensor_reduce(one, lg, AX_X, ALU.max))
                step(v.tensor_tensor(d, lg, one.unsqueeze(2).to_broadcast([P, NT, E]), ALU.subtract))
                dve.sem_inc(s_top_in, 1)
                other = lg.unsqueeze(2).to_broadcast([P, NT, E, E])
                own = lg.unsqueeze(3).to_broadcast([P, NT, E, E])
                step(v.tensor_tensor(ge, other, own, ALU.is_ge))
                step(v.tensor_tensor(gt, other, own, ALU.is_gt))
                ge_f = ge.rearrange("p t e f -> p t (e f)")
                gt_f = gt.rearrange("p t e f -> p t (e f)")
                step(v.tensor_tensor(ge_f, ge_f, gt_f, ALU.subtract))
                step(v.tensor_tensor(ge_f, ge_f, before[:, :].unsqueeze(1).to_broadcast([P, NT, E * E]), ALU.mult))
                step(v.tensor_tensor(ge_f, ge_f, gt_f, ALU.add))
                step(v.tensor_reduce(rank, ge, AX_X, ALU.add))
                dve.wait_ge(s_top_exp, 1)
                step(v.scalar_tensor_tensor(out=rank, in0=rank, scalar=1.5, in1=d, op0=ALU.is_lt, op1=ALU.mult))
                step(v.tensor_reduce(one, rank, AX_X, ALU.add))
                step(v.reciprocal(inv_s, one))
                step(v.tensor_tensor(cw[:, :, :], rank, inv_s.unsqueeze(2).to_broadcast([P, NT, E]), ALU.mult))
                assert count[0] == TOP_STEPS, count

            def householder(j):
                col = pT_[:, bass.ds(j, C)]
                s = lambda i: hs[:, i:i + 1]
                done = [0]

                def step(ins):
                    done[0] += 1
                    ins.then_inc(hh_step.sem, 1)
                    return done[0]

                def after(k):
                    dve.wait_ge(hh_step.sem, hh_step.at(j, k))

                dve.wait_ge(hh_mm.sem, hh_mm.at(j, 1))
                dve.wait_ge(hh_upd.sem, hh_upd.at(j, 0))
                after(step(v.tensor_copy(vb, psO[0:D, 0:C])))
                step(v.tensor_tensor_reduce(junk[:, 1:C], vb[:, 1:C], vb[:, 1:C], 1.0, 0.0, ALU.mult, ALU.add, s(0)))
                after(step(v.scalar_tensor_tensor(out=uT, in0=vb, scalar=1.0, in1=col, op0=ALU.mult, op1=ALU.mult, accum_out=s(3))))
                v.scalar_tensor_tensor(out=s(1), in0=vb[:, 0:1], scalar=vb[:, 0:1], in1=s(0), op0=ALU.mult, op1=ALU.add).then_inc(hh_nrm2.sem, 1)
                step(v.tensor_scalar(s(4), vb[:, 0:1], 0.0, 2.0, ALU.is_ge, ALU.mult))
                after(4)
                dve.wait_ge(hh_nrm.sem, hh_nrm.at(j, 1))
                nb = nbs[:, bass.ds(j, 1)]
                after(step(v.scalar_tensor_tensor(out=nb, in0=s(4), scalar=-1.0, in1=s(2), op0=ALU.add, op1=ALU.mult)))
                after(step(v.tensor_tensor(vb[:, 0:1], vb[:, 0:1], nb, ALU.add)))
                after(step(v.tensor_tensor(s(5), vb[:, 0:1], nb, ALU.mult)))
                after(step(v.tensor_scalar(s(5), s(5), 1e-37, None, ALU.max)))
                step(v.scalar_tensor_tensor(out=s(3), in0=pT_[:, bass.ds(j, 1)], scalar=nb, in1=s(3), op0=ALU.mult, op1=ALU.add))
                after(step(v.reciprocal(s(6), s(5))))
                after(step(v.scalar_tensor_tensor(out=cs[:, bass.ds(j, 1)], in0=s(0), scalar=0.0, in1=s(6), op0=ALU.is_gt, op1=ALU.mult)))
                assert done[0] == hh_step.per, done
                v.scalar_tensor_tensor(out=s(7), in0=s(3), scalar=cs[:, bass.ds(j, 1)], in1=below[:, bass.ds(j, 1)],
                                       op0=ALU.mult, op1=ALU.mult).then_inc(hh_w.sem, 1)
                dve.wait_ge(hh_w.sem, hh_w.at(j, 1))
                v.scalar_tensor_tensor(out=col, in0=vb, scalar=s(7), in1=col, op0=ALU.mult, op1=ALU.add).then_inc(hh_upd.sem, 1)

            def rotation():
                count = [0]

                def step(ins):
                    count[0] += 1
                    ins.then_inc(s_lin_dve, 1)
                    dve.wait_ge(s_lin_dve, count[0])

                def product(k):
                    dve.wait_ge(s_lin_pe, k)

                e64 = eye[0:D, 0:D]
                dve.wait_ge(hh_upd.sem, hh_upd.at(D, 0))
                step(v.tensor_tensor_reduce(junk[:, 0:D], nbs, e64, 1.0, 0.0, ALU.mult, ALU.add, hs[:, 8:9]))
                step(v.tensor_tensor_reduce(junk[:, 0:D], cs, e64, 1.0, 0.0, ALU.mult, ALU.add, hs[:, 9:10]))
                step(v.tensor_tensor(vT, pT_[:, 0:C], from_diag, ALU.mult))
                step(v.scalar_tensor_tensor(out=vT[:, 0:D], in0=e64, scalar=hs[:, 8:9], in1=vT[:, 0:D], op0=ALU.mult, op1=ALU.add))
                product(1)
                step(v.tensor_copy(v_c, psS[0:CH, 0, 0:NC3 * D].rearrange("p (c n) -> p c n", c=NC3)))
                product(2)
                step(v.scalar_tensor_tensor(out=mm[:, 0, :], in0=psS[0:D, 1, 0:D], scalar=hs[:, 9:10], in1=above, op0=ALU.mult, op1=ALU.mult))
                step(v.tensor_tensor(mm[:, 1, :], psS[0:D, 1, 0:D], cs, ALU.mult))
                step(v.tensor_tensor(mm[:, 1, :], mm[:, 1, :], below, ALU.mult))
                step(v.tensor_scalar(mm[:, 1, :], mm[:, 1, :], -1.0, None, ALU.mult))
                step(v.tensor_copy(inv, e64.unsqueeze(1).to_broadcast([D, 2, D])))
                for i in range(6):
                    step(v.tensor_tensor(lev[:, 0, :], mm[:, 0, :], level_masks[:, i, :], ALU.mult))
                    step(v.tensor_tensor(lev[:, 1, :], mm[:, 1, :], level_masks[:, 6 + i, :], ALU.mult))
                    product(3 + 2 * i)
                    step(v.tensor_copy(prod, psS[0:D, 0, 0:2 * D].rearrange("p (i n) -> p i n", i=2)))
                    product(4 + 2 * i)
                    step(v.tensor_tensor(inv, inv, psS[0:D, 1, 0:2 * D].rearrange("p (i n) -> p i n", i=2), ALU.subtract))
                step(v.tensor_scalar(tT, inv[:, 1, :], hs[:, 9:10], None, ALU.mult))
                product(15)
                step(v.tensor_copy(zT_, psS[0:D, 0, 0:D]))
                product(16)
                step(v.tensor_scalar(uT, psS[0:D, 1, 0:C], -1.0, None, ALU.mult))
                step(v.tensor_tensor(uT[:, 0:D], uT[:, 0:D], e64, ALU.add))
                product(17)
                step(v.tensor_copy(u_c, psS[0:CH, 0, 0:NC3 * D].rearrange("p (c n) -> p c n", c=NC3)))
                dve.wait_ge(s_skew_in, 16)
                step(v.tensor_tensor(A[:, :, :], A[:, :, :], sign.unsqueeze(1).to_broadcast([D, B, D]), ALU.mult))
                step(v.tensor_reduce(hs[:, 10:14], A[:, :, :], AX_X, ALU.add, apply_absolute_value=True))
                step(v.tensor_reduce(hs[:, 14:15], hs[:, 10:14], AX_X, ALU.max))
                product(18)
                step(v.tensor_reduce(junk[0:1, 0:1], psS[0:1, 0, 0:D], AX_X, ALU.max))
                product(19)
                step(v.tensor_copy(hs[:, 15:16], psS[0:D, 1, 0:1]))
                step(v.tensor_scalar(flags[:, 0:SQUARINGS], halves, hs[:, 15:16], 1.0, ALU.mult, ALU.is_gt))
                step(v.tensor_scalar(junk[:, 0:SQUARINGS], flags[:, 0:SQUARINGS], -0.5, 1.0, ALU.mult, ALU.add))
                w = SQUARINGS
                while w > 1:
                    w //= 2
                    step(v.tensor_tensor(junk[:, 0:w], junk[:, 0:w], junk[:, w:2 * w], ALU.mult))
                flat_a = A[:, :, :].rearrange("p b n -> p (b n)")
                step(v.tensor_scalar(xs[:, 0, :], flat_a, junk[:, 0:1], None, ALU.mult))
                step(v.tensor_scalar(xs[:, 1, :], xs[:, 0, :], -1.0, None, ALU.mult))
                ones = e64.unsqueeze(1).to_broadcast([D, 2 * B, D])
                ex3 = ex.rearrange("p (i n) -> p i n", n=D)
                step(v.tensor_copy(ex3, ones))
                assert count[0] == LIN_STEPS, count
                with dve.Fori(0, TAYLOR) as i:
                    dve.wait_ge(ho_mm.sem, ho_mm.at(i, 1))
                    v.scalar_tensor_tensor(out=ex3, in0=psS[0:D, 0, :].rearrange("p (i n) -> p i n", n=D),
                                           scalar=over_k[:, bass.ds(i, 1)], in1=ones, op0=ALU.mult, op1=ALU.add).then_inc(ho_dve.sem, 1)
                with dve.Fori(0, SQUARINGS) as i:
                    dve.wait_ge(sq_dve.sem, sq_dve.at(i, 0))
                    dve.wait_ge(sq_mm.sem, sq_mm.at(i, 1))
                    v.tensor_tensor(ex_t, psS[0:D, 1, :], ex, ALU.subtract).then_inc(sq_t.sem, 1)
                    dve.wait_ge(sq_t.sem, sq_t.at(i, 1))
                    v.scalar_tensor_tensor(out=ex, in0=ex_t, scalar=flags[:, bass.ds(i, 1)], in1=ex, op0=ALU.mult, op1=ALU.add).then_inc(sq_dve.sem, 1)
                dve.wait_ge(sq_dve.sem, sq_dve.at(SQUARINGS, 0))
                half_e = ex_t.rearrange("p (i n) -> p i n", n=D)[:, 0:B, :]
                step(v.tensor_tensor(half_e, ex3[:, B:2 * B, :], e64.unsqueeze(1).to_broadcast([D, B, D]), ALU.subtract))
                product(20)
                step(v.tensor_copy(w_rot, psS[0:D, :, 0:C]))
                dve.wait_ge(x2_ready.sem, x2_ready.at(4 * E, 0))
                with dve.Fori(0, B) as b:
                    dve.wait_ge(rt_T.sem, rt_T.at(b, 0))
                    v.tensor_copy(xhat[:, :, :], x[:, bass.ds(b * TB, TB), :]).then_inc(rt_x.sem, 1)
                    dve.wait_ge(rt_z.sem, rt_z.at(b, 1))
                    v.tensor_copy(zT, psO[0:D, :]).then_inc(rt_zc.sem, 1)
                    for t in range(TB):
                        xt = x[:, b * TB + t, :]
                        dve.wait_ge(rt_mm.sem, rt_mm.at(b, t + 1))
                        v.tensor_tensor(xt, psS[:, t, 0:C], xt, ALU.add).then_inc(rt_add.sem, 1)
                dve.wait_ge(rt_add.sem, rt_add.at(B, 0))

            dve.wait_ge(s_const, 48)
            v.tensor_copy(eye16[:, :], eye[:, :]).then_inc(s_eye, 1)
            dve.wait_ge(s_exp0, 1)
            v.tensor_scalar(silu_t[:, :, :], silu_t[:, :, :], 1.0, None, ALU.add).then_inc(s_eye, 1)
            dve.wait_ge(s_eye, 2)
            v.reciprocal(silu_t[:, :, :], silu_t[:, :, :]).then_inc(s_eye, 1)
            dve.wait_ge(s_eye, 3)
            v.tensor_tensor(silu[:, :, :], cond[:, :, :], silu_t[:, :, :], ALU.mult).then_inc(s_silu, 1)
            mods(0)
            dve.wait_ge(s_skew_b, 16)
            for i in range(8):
                dve.wait_ge(s_skew_mm, i + 1)
                v.tensor_tensor(v_skew[:, i * 512:(i + 1) * 512], psS[0:B, i % 4, :], b_skew[:, i * 512:(i + 1) * 512],
                                ALU.add).then_inc(s_skew_v, 1)
            dve.wait_ge(s_skew_v, 8)
            dve.wait_ge(s_x, 16)
            dve.wait_ge(s_init, 4)
            attention(0)
            top_two()
            dve.wait_ge(s_lin, 32)
            for e in range(E):
                dve.wait_ge(s_mlpw[e], 64)
                with dve.Fori(0, B) as b:
                    for s in range(4):
                        householder(b * 4 + (16 * e + s))
                    mlp_out(0, b + 4 * e, b, e)
                dve.wait_ge(x2_ready.sem, x2_ready.at(4 * (e + 1), 0))
            rotation()
            mods(1)
            dve.wait_ge(s_init, 6)
            dve.wait_ge(s_start, 80)
            attention(1)
            dve.wait_ge(s_mlpw[WSET[1]], 64)
            dve.wait_ge(x1_ready.sem, x1_ready.at(2 * B, 0))
            with dve.Fori(0, B) as b:
                mlp_out(1, b + ITER0[1], b, 0)
            dve.wait_ge(x2_ready.sem, x2_ready.at(ITER0[2], 0))
            mods(2)
            dve.wait_ge(s_init, 8)
            attention(2)
            dve.wait_ge(s_mlpw[WSET[2]], 64)
            with dve.Fori(0, B) as b:
                mlp_out(2, b + ITER0[2], b, 0)

        @block.tensor
        def _(pe):
            grant_credit(pe, "pe")
            mmul = nc.tensor.matmul
            def settle():
                pe.sem_inc(s_passed_pe, 1)

            def mods(l):
                pe.wait_ge(s_modw[l], 48)
                pe.wait_ge(s_silu, 1)
                if l:
                    pe.wait_ge(hid_ready.sem, hid_ready.at(ITER0[l], 0))
                    pe.wait_ge(x2_ready.sem, x2_ready.at(ITER0[l], 0))
                    if l == 1:
                        pe.wait_ge(rt_add.sem, rt_add.at(B, 0))
                for k, col in enumerate((0, 1, 3, 4)):
                    for c2 in range(NC3):
                        o = (k * NC3 + c2) * B
                        for c in range(NC3):
                            last = mmul(psM[0:CH, 0, o:o + B], w_mod[:, c, col * C + c2 * CH:col * C + (c2 + 1) * CH],
                                        silu[:, c, :], start=(c == 0), stop=(c == NC3 - 1))
                last.then_inc(s_mod_mm, 1)
                pe.wait_ge(s_silu_b, l + 1)
                for i in range(2 * B):
                    if i >= 4:
                        pe.wait_ge(s_mod, 9 * l + 1 + i - 3)
                    col = (2, 5)[i % 2] * C
                    for c in range(NC3):
                        last = mmul(psS[:, i % 4, 0:C], silu_b[:, c * B + i // 2, :], w_mod[:, c, col:col + C],
                                    start=(c == 0), stop=(c == NC3 - 1))
                    last.then_inc(s_mod_mm, 1)
                pe.wait_ge(s_mod, 9 * l + 9)

            def transpose_rows(sig, turn):
                for c in range(NC3):
                    for t in range(TB):
                        last = nc.tensor.transpose(banks3[c][0:CH, t * P:(t + 1) * P], xhat[:, t, c * CH:(c + 1) * CH], eye[:, :])
                    last.then_inc(sig.sem, 1)

            def transpose_heads(n, g, i):
                rows = KM if i in (2, 3) else KS
                src = (kp if i < 2 else qp)[g % 2]
                if i == 0:
                    pe.wait_ge(t_ev.sem, t_ev.at(n, 6 * g - 1))
                    pe.wait_ge(rep_done.sem, rep_done.at(n, 2 * g + 1))
                elif i == 1:
                    pe.wait_ge(t_ev.sem, t_ev.at(n, 6 * g))
                elif i == 2:
                    pe.wait_ge(recip.sem, recip.at(n, g - 1))
                    pe.wait_ge(rep_done.sem, rep_done.at(n, 2 * g + 2))
                elif i == 3:
                    pe.wait_ge(t_ev.sem, t_ev.at(n, 6 * g + 1))
                elif i == 4:
                    pe.wait_ge(t_ev.sem, t_ev.at(n, 6 * g + 4))
                    pe.wait_ge(m_ready.sem, m_ready.at(n, g + 1))
                for hh in range(2):
                    for t in range(TB):
                        o = (hh * TB + t) * P
                        last = nc.tensor.transpose(banks3_16[SET_BANK[i]][0:rows, o:o + P],
                                                   src[:, t * G + 2 * (i % 2) + hh, 0:rows], eye16[:, :])
                last.then_inc(t_mm.sem, 1)

            def max_scores(n, g, j):
                for t in range(TB):
                    i = 16 * g + 4 * j + t
                    if j == 0 and t < 2:
                        pe.wait_ge(t_ev.sem, t_ev.at(n, 6 * g + 4))
                    else:
                        pe.wait_ge(max_done.sem, max_done.at(n, i - 1))
                    mmul(psM[:, t % 2, :], qT[g % 2][0:KM, j, t * P:(t + 1) * P], kT[g % 2][0:KM, j, :],
                         start=True, stop=True).then_inc(max_mm.sem, 1)

            def scores(n, g, kb, h):
                i = 8 * g + 2 * kb + h
                if i % 8 == 0:
                    pe.wait_ge(t_ev.sem, t_ev.at(n, 6 * g + 6))
                pe.wait_ge(exp_done.sem, exp_done.at(n, i - 1))
                for hh in range(2):
                    last = mmul(psS[:, 2 * h + hh, :], kT[g % 2][0:KS, 2 * h + hh, kb * P:(kb + 1) * P],
                                qT[g % 2][0:KS, 2 * h + hh, :], start=True, stop=True)
                last.then_inc(s_mm.sem, 1)

            def values(n, g, kb):
                u = 4 * g + kb
                if kb == 0:
                    pe.wait_ge(v_staged.sem, v_staged.at(n, g + 1))
                    pe.wait_ge(o_raw.sem, o_raw.at(n, g))
                pe.wait_ge(exp_done.sem, exp_done.at(n, 2 * u + 2))
                for j in range(G):
                    last = mmul(psO[HP * j:HP * (j + 1), :], vg[g % 2][:, kb, HP * j:HP * (j + 1)],
                                pT[:, kb % 2, j * N:(j + 1) * N], start=(kb == 0), stop=(kb == TB - 1))
                last.then_inc(av_done.sem, 1)

            def denominators(n, g):
                pe.wait_ge(o_raw.sem, o_raw.at(n, g + 1))
                pe.wait_ge(max_done.sem, max_done.at(n, 16 * min(g + 2, NG)))
                mmul(psM[:, 1, :], sel[:, :], oT[:, g, :], start=True, stop=True).then_inc(d_mm.sem, 1)

            def attention(l):
                pe.wait_ge(s_attw[l], 48)
                with pe.Fori(0, B) as b:
                    n = b + l * B
                    if l == 0:
                        pe.wait_ge(gate_read.sem, gate_read.at(b, 0))
                    pe.wait_ge(ln_xhat.sem, ln_xhat.at(n * 2 + 1, 0))
                    pe.wait_ge(h_ready.sem, h_ready.at(n * 2, 0))
                    transpose_rows(ln_T, n * 2)
                    pe.wait_ge(h_ready.sem, h_ready.at(n * 2 + 1, 0))
                    pe.wait_ge(proj_read.sem, proj_read.at(n, 0))
                    for i in range(2 * TB):
                        t, h = divmod(i, 2)
                        w = 3 * C // 2
                        if i >= 4:
                            pe.wait_ge(qkv_ready.sem, qkv_ready.at(n, i - 3))
                        for c in range(NC3):
                            last = mmul(psS[:, i % 4, 0:w], hT[:, c, t * P:(t + 1) * P], w_qkv[:, c, h * w:(h + 1) * w],
                                        start=(c == 0), stop=(c == NC3 - 1))
                        last.then_inc(qkv_mm.sem, 1)
                    for i in range(4):
                        transpose_heads(n, 0, i)
                    for j in range(G):
                        max_scores(n, 0, j)
                    for i in (4, 5):
                        transpose_heads(n, 0, i)
                    pe.wait_ge(qkv_ready.sem, qkv_ready.at(n, 2 * TB))
                    for g in range(NG):
                        more = g + 1 < NG
                        if more:
                            for i in range(4):
                                transpose_heads(n, g + 1, i)
                        for kb in range(TB):
                            for h in range(2):
                                scores(n, g, kb, h)
                            if more:
                                max_scores(n, g + 1, kb)
                            if kb:
                                values(n, g, kb - 1)
                        values(n, g, TB - 1)
                        if more:
                            for i in (4, 5):
                                if i == 5:
                                    pe.wait_ge(max_done.sem, max_done.at(n, 16 * (g + 2)))
                                transpose_heads(n, g + 1, i)
                        denominators(n, g)
                    pe.wait_ge(o_ready.sem, o_ready.at(n, NG))
                    for t in range(TB):
                        for g in range(NG):
                            last = mmul(psS[:, t, 0:C], oT[:, g, t * P:(t + 1) * P], w_proj[:, g, :], start=(g == 0), stop=(g == NG - 1))
                        last.then_inc(proj_mm.sem, 1)
                    pe.wait_ge(ln_xhat.sem, ln_xhat.at(n * 2 + 2, 0))
                    transpose_rows(ln_T, n * 2 + 1)
                    if l == 0:
                        pe.wait_ge(h_ready.sem, h_ready.at(n * 2 + 2, 0))
                        for t in range(TB):
                            for c in range(NC3):
                                last = mmul(psT[:, t * E:(t + 1) * E], hT[:, c, t * P:(t + 1) * P], w_gate[:, c, :],
                                            start=(c == 0), stop=(c == NC3 - 1))
                        last.then_inc(gate_mm.sem, 1)

            def mlp(l, e):
                w1, w2, _, _ = experts[e % 2]
                pe.wait_ge(s_mlpw[WSET[l] + e], 64)
                if e == 0:
                    pe.wait_ge(h2_ready.sem, h2_ready.at(B * (l + 1), 0))
                    pe.wait_ge(proj_read.sem, proj_read.at(B * (l + 1), 0))
                    if l == 0:
                        pe.wait_ge(s_lin, 32)
                with pe.Fori(0, B) as b:
                    q = b + (ITER0[l] + B * e)
                    for m in range(MH):
                        pe.wait_ge(hid_ready.sem, hid_ready.at(q, m - 3))
                        for c in range(NC3):
                            last = mmul(psS[:, m % 4, :], w1[:, c, m * P:(m + 1) * P], h2T[:, c, bass.ds(b * N, N)],
                                        start=(c == 0), stop=(c == NC3 - 1))
                        last.then_inc(f1_mm.sem, 1)
                        if l == 0 and m % 2:
                            j = b * 4 + (16 * e + m // 2)
                            pe.wait_ge(hh_pick.sem, hh_pick.at(j, 1))
                            pe.wait_ge(hh_upd.sem, hh_upd.at(j, 0))
                            mmul(psO[:, 0:C], pick, pT_[:, bass.ds(j, C)], start=True, stop=True).then_inc(hh_mm.sem, 1)
                    for t in range(TB):
                        if t == 0:
                            pe.wait_ge(hid_ready.sem, hid_ready.at(q, MH))
                        pe.wait_ge(f2_read.sem, f2_read.at(q, t - 1))
                        for m in range(MH):
                            last = mmul(psM[:, t % 2, 0:C], hid[:, m, t * P:(t + 1) * P], w2[:, m, :],
                                        start=(m == 0), stop=(m == MH - 1))
                        last.then_inc(f2_mm.sem, 1)

            def rotation():
                def ready(k):
                    pe.wait_ge(s_lin_dve, k)

                e64 = eye[0:D, 0:D]
                pe.wait_ge(hid_ready.sem, hid_ready.at(4 * E, 0))
                ready(4)
                for c in range(NC3):
                    last = nc.tensor.transpose(psS[0:CH, 0, c * D:(c + 1) * D], vT[:, c * CH:(c + 1) * CH], e64)
                last.then_inc(s_lin_pe, 1)
                ready(5)
                for c in range(NC3):
                    last = mmul(psS[0:D, 1, 0:D], v_c[:, c, :], v_c[:, c, :], start=(c == 0), stop=(c == NC3 - 1))
                last.then_inc(s_lin_pe, 1)
                for i in range(6):
                    ready(12 + 4 * i)
                    mmul(psS[0:D, 0, 0:D], lev[:, 1, :], inv[:, 0, :], start=True, stop=True)
                    mmul(psS[0:D, 0, D:2 * D], lev[:, 0, :], inv[:, 1, :], start=True, stop=True).then_inc(s_lin_pe, 1)
                    ready(13 + 4 * i)
                    mmul(psS[0:D, 1, 0:D], inv[:, 1, :], prod[:, 0, :], start=True, stop=True)
                    mmul(psS[0:D, 1, D:2 * D], inv[:, 0, :], prod[:, 1, :], start=True, stop=True).then_inc(s_lin_pe, 1)
                ready(35)
                mmul(psS[0:D, 0, 0:D], tT, vT[:, 0:D], start=True, stop=True).then_inc(s_lin_pe, 1)
                ready(36)
                mmul(psS[0:D, 1, 0:C], zT_, vT, start=True, stop=True).then_inc(s_lin_pe, 1)
                ready(38)
                for c in range(NC3):
                    last = nc.tensor.transpose(psS[0:CH, 0, c * D:(c + 1) * D], uT[:, c * CH:(c + 1) * CH], e64)
                last.then_inc(s_lin_pe, 1)
                ready(42)
                mmul(psS[0:1, 0, 0:D], hs[:, 14:15], e64, start=True, stop=True).then_inc(s_lin_pe, 1)
                ready(43)
                mmul(psS[0:D, 1, 0:1], eye_row, junk[0:1, 0:1], start=True, stop=True).then_inc(s_lin_pe, 1)
                ready(LIN_STEPS)
                ex3 = ex.rearrange("p (i n) -> p i n", n=D)
                xs3 = xs.rearrange("p i (b n) -> p i b n", n=D)
                with pe.Fori(0, TAYLOR) as i:
                    pe.wait_ge(ho_dve.sem, ho_dve.at(i, 0))
                    settle()
                    for k in range(2 * B):
                        last = mmul(psS[0:D, 0, k * D:(k + 1) * D], xs3[:, 1 - k // B, k % B, :], ex3[:, k, :], start=True, stop=True)
                    last.then_inc(ho_mm.sem, 1)
                pe.wait_ge(ho_dve.sem, ho_dve.at(TAYLOR, 0))
                with pe.Fori(0, SQUARINGS) as i:
                    pe.wait_ge(sq_dve.sem, sq_dve.at(i, 0))
                    settle()
                    for k in range(2 * B):
                        last = mmul(psS[0:D, 1, k * D:(k + 1) * D], ex3[:, (k + B) % (2 * B), :], ex3[:, k, :], start=True, stop=True)
                    last.then_inc(sq_mm.sem, 1)
                ready(LIN_STEPS + 1)
                half_e = ex_t.rearrange("p (i n) -> p i n", n=D)
                for b in range(B):
                    last = mmul(psS[0:D, b, 0:C], half_e[:, b, :], uT, start=True, stop=True)
                last.then_inc(s_lin_pe, 1)
                ready(LIN_STEPS + 2)
                pe.wait_ge(x2_ready.sem, x2_ready.at(4 * E, 0))
                with pe.Fori(0, B) as b:
                    pe.wait_ge(rt_h.sem, rt_h.at(b, 0))
                    pe.wait_ge(rt_x.sem, rt_x.at(b, 1))
                    transpose_rows(rt_T, b)
                    pe.wait_ge(rt_zc.sem, rt_zc.at(b, 0))
                    pe.wait_ge(rt_h.sem, rt_h.at(b, NC3))
                    for c in range(NC3):
                        last = mmul(psO[0:D, :], u_c[:, c, :], hT[:, c, :], start=(c == 0), stop=(c == NC3 - 1))
                    last.then_inc(rt_z.sem, 1)
                    pe.wait_ge(rt_zc.sem, rt_zc.at(b, 1))
                    for t in range(TB):
                        pe.wait_ge(rt_add.sem, rt_add.at(b, t - 3))
                        settle()
                        mmul(psS[:, t, 0:C], zT[:, t * P:(t + 1) * P], w_rot[:, b, :], start=True, stop=True).then_inc(rt_mm.sem, 1)

            pe.wait_ge(s_eye, 1)
            mods(0)
            for i in range(8):
                pe.wait_ge(s_skew_w[i % 2], 16 * (i // 2 + 1))
                if i >= 4:
                    pe.wait_ge(s_skew_v, i - 3)
                for c in range(NC3):
                    last = mmul(psS[0:B, i % 4, :], silu[:, c, :], w_skew[i % 2][:, c, :], start=(c == 0), stop=(c == NC3 - 1))
                last.then_inc(s_skew_mm, 1)
            pe.wait_ge(s_skew_v, 8)
            pe.wait_ge(s_init, 4)
            pe.wait_ge(s_start, 80)
            attention(0)
            for e in range(E):
                mlp(0, e)
            rotation()
            mods(1)
            pe.wait_ge(s_init, 6)
            attention(1)
            mlp(1, 0)
            mods(2)
            pe.wait_ge(s_init, 8)
            attention(2)
            mlp(2, 0)


TOP_STEPS = 12
LIN_STEPS = 53


def lay_out(inputs):
    a = {k: np.ascontiguousarray(v) for k, v in inputs.items()}
    out = dict(host_constants())
    out["x"] = a["x"]
    out["cond"] = np.ascontiguousarray(a["cond_1152"].T.reshape(NC3, CH, B).transpose(1, 0, 2))
    names = {
        "L0": ("L0_cond_w_adaln", "L0_cond_b_adaln", "L0_cond_w_qkv", "L0_cond_b_qkv", "L0_cond_w_proj", "L0_cond_b_proj",
               "L0_cond_w1", "L0_cond_b1", "L0_cond_w2", "L0_cond_b2"),
        "L2": ("L2_cond_w_mod", "L2_cond_b_mod", "L2_cond_w_qkv", "L2_cond_b_qkv", "L2_cond_w_proj", "L2_cond_b_proj",
               "L2_cond_w1", "L2_cond_b1", "L2_cond_w2", "L2_cond_b2"),
        "L3": ("L3_cond_W_ada", "L3_cond_b_ada", "L3_cond_W_qkv", "L3_cond_b_qkv", "L3_cond_W_proj", "L3_cond_b_proj",
               "L3_cond_W_fc1", "L3_cond_b_fc1", "L3_cond_W_fc2", "L3_cond_b_fc2"),
    }
    mod_bias = np.zeros((CH, 3, 4 * NC3), np.float32)
    for l, n in enumerate(LAYERS):
        wm, bm, wq, bq, wp, bp, w1, b1, w2, b2 = (a[k] for k in names[n])
        ne = w1.size // (C * HID)
        out[n + "_w_mod"], out[n + "_b_mod"], out[n + "_w_qkv"], out[n + "_b_qkv"] = wm, bm, wq, bq
        pad = np.zeros((NG, G, HP, C), np.float32)
        pad[:, :, 0:HD] = wp.reshape(NG, G, HD, C)
        pad[0, 0, HD] = bp
        out[n + "_w_proj"] = np.ascontiguousarray(pad.transpose(1, 2, 0, 3).reshape(P, NG, C))
        out[n + "_w1"], out[n + "_w2"] = w1.reshape(ne, C, HID), w2.reshape(ne, HID, C)
        out[n + "_b2"] = b2.reshape(ne, C)
        out[n + "_b1"] = np.ascontiguousarray(b1.reshape(ne, MH, P).transpose(0, 2, 1))
        mod_bias[:, l] = bm.reshape(6, NC3, CH)[[0, 1, 3, 4]].reshape(4 * NC3, CH).T
    out["mod_bias"] = mod_bias
    out["w_gate"] = a["L0_cond_w_gate"]
    out["g_q"] = np.tile(a["L2_cond_g_q"], NH)
    out["g_k"] = np.tile(a["L2_cond_g_k"], NH)
    iu, ju = np.triu_indices(D, k=1)
    w = np.zeros((D, D, C), np.float32)
    w[iu, ju] = a["L1_cond_W"]
    w[ju, iu] = a["L1_cond_W"]
    out["w_skew"] = np.ascontiguousarray(w.reshape(D * D, C).T)
    bs = np.zeros((D, D), np.float32)
    bs[iu, ju] = a["L1_cond_b"]
    bs[ju, iu] = a["L1_cond_b"]
    out["b_skew"] = bs.reshape(D * D)
    pT = np.zeros((D, C + D), np.float32)
    pT[:, 0:C] = a["L1_cond_P"].T
    out["pT"] = pT
    return out


def kernel(**inputs):
    import concourse.bacc as bacc
    from concourse.bass_utils import run_bass_kernel_spmd as run

    nc = bacc.Bacc("TRN2", target_bir_lowering=False, num_devices=1)
    arrays = {"in_" + k: v for k, v in lay_out(inputs).items()}
    dram = {k[3:]: nc.dram_tensor(k, v.shape, F32, kind="ExternalInput").ap() for k, v in arrays.items()}
    dram["out"] = nc.dram_tensor("out_x", (B, N, C), F32, kind="ExternalOutput").ap()
    build(nc, dram)
    r = run(nc, [arrays], core_ids=[0])
    return r.results[0]["out_x"]
```

```python
from contextlib import ExitStack

import numpy as np

import concourse.bass as bass
from concourse import mybir

F32 = mybir.dt.float32
BF16 = mybir.dt.bfloat16
ALU = mybir.AluOpType
ACT = mybir.ActivationFunctionType
AX_X = mybir.AxisListType.X

P = 128
B, N, C = 4, 512, 288
TB = N // P
NT = B * TB
CH = 96
NC3 = C // CH
NH, HD = 16, C // 16
G = 4
NG = NH // G
GW = G * HD
HP = 32
HID = 4 * C
MH = HID // P
E = 4
D = 64
LAYERS = ("L0", "L2", "L3")
KM = 6 * HD
KS = KM + 3
SCALE = float(HD) ** -0.5
EPS = 1e-6
TAYLOR = 12
SQUARINGS = 16
SET_ORDER = [(0, 0), (0, 1), (0, 2), (0, 3), (1, 0), (1, 1), (0, 4), (0, 5), (1, 2), (1, 3)]
for _g in range(NG - 1):
    SET_ORDER += [(_g + 2, _i) for _i in range(4) if _g + 2 < NG] + [(_g + 1, 4), (_g + 1, 5)]
SET_TURN = {_s: _k + 1 for _k, _s in enumerate(SET_ORDER)}
CREDIT = 16

A_QKV = 0
A_V = A_QKV + TB * 3 * C * 4
A_KP = A_V + 2 * TB * G * HP * 4
A_QP = A_KP + 2 * TB * G * 112 * 2
A_SPL = A_QP + 2 * TB * G * 112 * 2
A_KT = A_SPL + 2 * (TB * GW * 4 + 2 * TB * GW * 2)
A_QT = A_KT + 3 * G * N * 2
A_PT = A_QT + 3 * G * N * 2
A_OT = A_PT + 2 * G * N * 4
A_RD = A_OT + NG * N * 4
A_END = A_RD + N * 4
M_HID = 0
M_W1 = MH * N * 4
W1_B, W2_B = NC3 * HID * 4, MH * C * 4
W_BYTES = W1_B + W2_B + C * 4 + MH * 4
M_LIN = M_W1 + W_BYTES + 28
M_LIN += -M_LIN % 32
I_WS = M_LIN
I_BS = I_WS + 2 * NC3 * 512 * 4


class Signal:

    def __init__(self, sem, per):
        self.sem, self.per = sem, per

    def at(self, turn, k):
        return turn * self.per + (k + CREDIT)


def host_constants():
    r = np.arange(D)
    eye = np.eye(P, dtype=np.float32)
    sel = np.zeros((P, P), np.float32)
    for j in range(G):
        sel[HP * j + HD, HP * j:HP * j + HP] = 1.0
    gather = np.zeros((P, NG - 1, (NG - 1) * G), np.float32)
    for g in range(NG - 1):
        for j in range(G):
            gather[HP * j + HD, g, G * g + j] = 1.0
    spread = np.ascontiguousarray(np.repeat(np.eye((NG - 1) * G, dtype=np.float32), HP, axis=1).reshape((NG - 1) * G, NG - 1, P))
    up, lo = [], []
    b = 1
    while b < D:
        m = ((r[:, None] // (2 * b) == r[None] // (2 * b)) & (r[:, None] // b < r[None] // b))
        up.append(m)
        lo.append(m.T)
        b *= 2
    masks = np.stack(up + lo).transpose(1, 0, 2).astype(np.float32)
    below = -(r[:, None] > r[None]).astype(np.float32)
    from_diagonal = (np.arange(C)[None] >= r[:, None]).astype(np.float32)
    sign = np.where(r[None] > r[:, None], 1.0, -1.0).astype(np.float32)
    halves = np.broadcast_to(2.0 ** -np.arange(SQUARINGS), (D, SQUARINGS)).astype(np.float32)
    over_k = np.broadcast_to(1.0 / np.arange(TAYLOR, 0, -1), (D, TAYLOR)).astype(np.float32)
    e = np.arange(E)
    before = np.broadcast_to((e[None] < e[:, None]).astype(np.float32).reshape(1, E * E), (P, E * E))
    above = (r[:, None] < r[None]).astype(np.float32)
    small = np.concatenate([masks.reshape(D, -1), below, from_diagonal, sign, halves, over_k, above, np.ones((D, D), np.float32)], 1)
    return {"c_eye": eye, "c_sel": sel, "c_gather": gather, "c_spread": spread, "c_before": np.ascontiguousarray(before), "c_small": np.ascontiguousarray(small)}


def build(nc, dram):
    ctx = ExitStack()
    with ctx:
        def sb(name, shape, dt=F32):
            return ctx.enter_context(nc.sbuf_tensor(name, shape, dt))

        def sem(name):
            return ctx.enter_context(nc.semaphore(name))

        signals = {"pe": [], "act": [], "dve": [], "pool": []}

        def signal(owner, name, per):
            s = Signal(sem(name), per)
            signals[owner].append(s)
            return s

        def grant_credit(eng, owner):
            for s in signals[owner]:
                eng.sem_inc(s.sem, CREDIT)

        x = sb("x", [P, NT, C])
        w_qkv = sb("w_qkv", [CH, NC3, 3 * C])
        w_proj = sb("w_proj", [P, NG, C])
        b_qkv = sb("b_qkv", [P, 3 * C])
        g_qk = sb("g_qk", [P, 2 * C])
        gates = sb("gates", [P, B, 2, C])
        xhat = sb("xhat", [P, TB, C])
        hT = sb("hT", [CH, NC3, N])
        h2T = sb("h2T", [CH, NC3, B * N])
        tmp = sb("tmp", [P, 2, C])
        eye = sb("eye", [P, P])
        eye16 = sb("eye16", [P, P], BF16)
        sel = sb("sel", [P, P])
        gather = sb("gather", [P, NG - 1, (NG - 1) * G])
        spread = sb("spread", [(NG - 1) * G, NG - 1, P])
        before = sb("before", [P, E * E])
        w_gate = sb("w_gate", [CH, NC3, E])
        cond = sb("cond", [CH, NC3, B])
        silu = sb("silu", [CH, NC3, B])
        silu_t = sb("silu_t", [CH, NC3, B])
        mod_bias = sb("mod_bias", [CH, 3, 4 * NC3])
        modT = sb("modT", [CH, 4, NC3, B])
        stats = sb("stats", [P, TB, 6])
        meanvar = sb("meanvar", [P, TB, 2])
        var_eps = sb("var_eps", [P, 2, TB])
        rstd = sb("rstd", [P, TB])
        consts = sb("consts", [P, 2 * TB])
        half = sb("half", [D, 1])
        mx = sb("mx", [P, TB * G])
        mrest = sb("mrest", [P, TB * G])
        head_sum = sb("head_sum", [P, TB, 2 * NH])
        head_tmp = sb("head_tmp", [P, TB, 2 * NH])
        head_inv = sb("head_inv", [P, TB, 2 * NH])
        logits = sb("logits", [P, NT, E])
        cw = sb("cw", [P, NT, E])
        A = sb("A", [D, B, D])
        w_a = sb("w_a", [P, W_BYTES // 4])
        arena = sb("arena", [P, A_END // 4])
        assert I_BS + D * D * 4 <= A_END and M_W1 + 6 * C * NC3 * 4 + 2 * C * 4 <= M_LIN

        def at(base, n, dt=F32, p=P):
            a = arena[0:p, base // 4:base // 4 + (n * (2 if dt == BF16 else 4) + 3) // 4]
            return a.bitcast(BF16) if dt == BF16 else a

        qkv = at(A_QKV, TB * 3 * C).rearrange("p (t c) -> p t c", t=TB)
        vg = [at(A_V + i * TB * G * HP * 4, TB * G * HP).rearrange("p (t c) -> p t c", t=TB) for i in range(2)]
        kp = [at(A_KP + i * TB * G * 224, TB * G * 112, BF16).rearrange("p (h c) -> p h c", c=112) for i in range(2)]
        qp = [at(A_QP + i * TB * G * 224, TB * G * 112, BF16).rearrange("p (h c) -> p h c", c=112) for i in range(2)]
        SPL = TB * GW * 8
        rest = [at(A_SPL + i * SPL, TB * GW) for i in range(2)]
        part_h = [at(A_SPL + i * SPL + TB * GW * 4, TB * GW, BF16) for i in range(2)]
        part_m = [at(A_SPL + i * SPL + TB * GW * 6, TB * GW, BF16) for i in range(2)]
        kT = [at(A_KT + i * G * N * 2, G * N, BF16).rearrange("p (h n) -> p h n", h=G) for i in range(3)]
        qT = [at(A_QT + i * G * N * 2, G * N, BF16).rearrange("p (h n) -> p h n", h=G) for i in range(3)]
        pT = at(A_PT, 2 * G * N).rearrange("p (i n) -> p i n", i=2)
        square = at(A_PT, TB * 2 * C).rearrange("p (t c) -> p t c", t=TB)
        oT = at(A_OT, NG * N).rearrange("p (g n) -> p g n", g=NG)
        rD = at(A_RD, N)
        hid = at(M_HID, MH * N).rearrange("p (m n) -> p m n", m=MH)
        top = at(M_HID, 6 * NT * E * E)

        def expert(flat):
            o = NC3 * HID
            return (flat[0:CH, 0:o].rearrange("p (c n) -> p c n", c=NC3),
                    flat[:, o:o + MH * C].rearrange("p (m n) -> p m n", m=MH),
                    flat[:, o + MH * C:o + MH * C + C], flat[:, o + MH * C + C:o + MH * C + C + MH])

        experts = [expert(w_a[:, :]), expert(at(M_W1, W_BYTES // 4))]
        w_mod = at(M_W1, NC3 * 6 * C, p=CH).rearrange("p (c n) -> p c n", c=NC3)
        gate_bias = at(M_W1 + NC3 * 6 * C * 4, 2 * C).rearrange("p (i n) -> p i n", i=2)
        silu_b = at(M_HID, NC3 * B * P, p=CH).rearrange("p (i n) -> p i n", n=P)
        w_skew = [at(I_WS + i * NC3 * 2048, NC3 * 512, p=CH).rearrange("p (c n) -> p c n", c=NC3) for i in range(2)]
        b_skew = at(I_BS, D * D, p=B)
        v_skew = h2T[0:B, :, :].rearrange("p c n -> p (c n)")[:, 0:D * D]

        lin_at = [M_LIN]

        def lin(n, p=D):
            a = at(lin_at[0], n, p=p)
            lin_at[0] += n * 4 + (-n * 4) % 32
            assert lin_at[0] <= A_END
            return a

        small = lin(16 * D + C + SQUARINGS + TAYLOR)
        o = 12 * D
        level_masks = small[:, 0:o].rearrange("p (l n) -> p l n", l=12)
        below = small[:, o:o + D]
        from_diag = small[:, o + D:o + D + C]
        sign = small[:, o + D + C:o + 2 * D + C]
        halves = small[:, o + 2 * D + C:o + 2 * D + C + SQUARINGS]
        over_k = small[:, o + 2 * D + C + SQUARINGS:o + 2 * D + C + SQUARINGS + TAYLOR]
        o += 2 * D + C + SQUARINGS + TAYLOR
        above = small[:, o:o + D]
        eye_row = small[0:1, o + D:o + 2 * D]
        pick = lin(P)
        pT_ = lin(C + D)
        vb = lin(C)
        junk = lin(C)
        hs = lin(16)
        nbs = lin(D)
        cs = lin(D)
        uT = lin(C)
        vT = lin(C)
        inv = lin(2 * D).rearrange("p (i n) -> p i n", i=2)
        lev = lin(2 * D).rearrange("p (i n) -> p i n", i=2)
        mm = lin(2 * D).rearrange("p (i n) -> p i n", i=2)
        prod = lin(2 * D).rearrange("p (i n) -> p i n", i=2)
        tT = lin(D)
        zT_ = lin(D)
        v_c = lin(NC3 * D, p=CH).rearrange("p (c n) -> p c n", c=NC3)
        u_c = lin(NC3 * D, p=CH).rearrange("p (c n) -> p c n", c=NC3)
        xs = lin(2 * B * D).rearrange("p (i n) -> p i n", i=2)
        ex = lin(2 * B * D)
        ex_t = lin(2 * B * D)
        flags = lin(SQUARINGS + 8)
        w_rot = lin(B * C).rearrange("p (b n) -> p b n", b=B)
        zT = lin(N)

        psS = ctx.enter_context(nc.psum_tensor("psS", [P, 4, 512], F32))
        psM = ctx.enter_context(nc.psum_tensor("psM", [P, 2, 512], F32))
        psO = ctx.enter_context(nc.psum_tensor("psO", [P, 512], F32))
        psT = ctx.enter_context(nc.psum_tensor("psT", [P, 512], F32))
        banks3 = [psT[:, :], psM[:, 0, :], psM[:, 1, :]]
        banks3_16 = [b.bitcast(BF16) for b in banks3]

        def set_bank(g, i):
            return (0, 1, 2, 0, 0, 2)[i] if g == 0 or i > 3 else 0

        scratch = nc.dram_tensor("skew_scratch", [B, D * D], F32, kind="Internal").ap()

        s_const = sem("constants_loaded")
        s_start = sem("start_inputs_loaded")
        s_x = sem("x_loaded")
        s_attw = [sem(f"attention_weights_loaded_{l}") for l in range(3)]
        s_modw = [sem(f"mod_weights_loaded_{l}") for l in range(3)]
        s_mlpw = [sem(f"expert_weights_loaded_{q}") for q in range(E + 2)]
        s_skew_w = [sem(f"skew_weights_loaded_{i}") for i in range(2)]
        s_skew_b = sem("skew_bias_loaded")
        s_skew_out = sem("skew_stored")
        s_skew_in = sem("skew_loaded")
        s_lin = sem("rotation_inputs_loaded")
        s_out = sem("output_stored")
        s_init = sem("constant_tiles_set")
        s_exp0 = sem("silu_exp_done")
        s_silu = sem("silu_ready")
        s_silu_b = sem("silu_spread")
        s_skew_mm = sem("skew_product_done")
        s_skew_v = sem("skew_rows_ready")
        s_mod_mm = sem("mod_product_done")
        s_mod = sem("mod_ready")
        s_top = sem("top2_steps")
        s_top_exp = sem("top2_exp_done")
        s_top_in = sem("top2_exp_asked")
        s_modstep = sem("mod_steps")
        s_passed_pool = sem("pool_waits_passed")
        s_passed_dve = sem("vector_waits_passed")
        s_passed_pe = sem("tensor_waits_passed")
        s_passed_act = sem("scalar_waits_passed")
        s_eye = sem("eye16_and_silu_steps")
        s_lin_dve = sem("rotation_vector_steps")
        s_lin_pe = sem("rotation_products")

        ln_stats = signal("dve", "ln_stats", TB)
        ln_mv = signal("dve", "ln_meanvar", TB)
        ln_eps = signal("pool", "ln_var_eps", 1)
        ln_rstd = signal("pool", "ln_rstd", 1)
        ln_xhat = signal("dve", "ln_normalised", TB)
        ln_T = signal("pe", "ln_transposed", NC3)
        h_ready = signal("act", "modulated", NC3)
        h2_ready = signal("act", "mlp_input_kept", 1)
        qkv_mm = signal("pe", "qkv_product", 2 * TB)
        qkv_ready = signal("dve", "qkv_ready", 2 * TB)
        qkn = signal("dve", "qk_norm_steps", 9)
        sq_ready = signal("dve", "qk_squares", 3)
        qkn_root = signal("act", "qk_deviation", 1)
        split_step = signal("dve", "split_steps", 6 * NG)
        split_ready = signal("dve", "split_ready", 2 * NG)
        rep_first = signal("act", "first_parts_stacked", 2)
        rep_done = signal("pool", "parts_stacked", 2 * NG - 2)
        v_staged = signal("pool", "v_staged", NG)
        t_mm = signal("pe", "heads_transposed", 6 * NG)
        t_ev = signal("act", "heads_copied", 6 * NG)
        max_mm = signal("pe", "max_scores", 16 * NG)
        max_done = signal("dve", "max_taken", 16 * NG)
        mparts = signal("dve", "max_split_steps", 3 * NG)
        m_ready = signal("dve", "max_parts_ready", NG)
        s_mm = signal("pe", "scores_ready", 8 * NG)
        exp_done = signal("act", "exp_done", 8 * NG)
        av_done = signal("pe", "values_summed", 4 * NG)
        o_raw = signal("dve", "sums_copied", NG)
        d_mm = signal("pe", "denominators_moved", NG + 1)
        recip = signal("dve", "denominators_inverted", 2)
        o_ready = signal("dve", "heads_ready", NG)
        proj_mm = signal("pe", "projected", TB)
        proj_read = signal("dve", "projection_gated", TB)
        x1_ready = signal("dve", "x_after_attention", TB)
        gate_mm = signal("pe", "gate_product", 1)
        gate_read = signal("dve", "gate_logits_kept", 1)
        f1_mm = signal("pe", "hidden_product", MH)
        hid_ready = signal("act", "hidden_ready", MH)
        f2_mm = signal("pe", "mlp_product", TB)
        f2_read = signal("dve", "mlp_bias_added", TB)
        f2_scaled = signal("dve", "mlp_gated", TB)
        x2_ready = signal("dve", "x_after_mlp", TB)
        hh_pick = signal("pool", "householder_row_picked", 1)
        hh_mm = signal("pe", "householder_column_spread", 1)
        hh_step = signal("dve", "householder_steps", 11)
        hh_nrm2 = signal("dve", "householder_norm2", 1)
        hh_nrm = signal("pool", "householder_norm", 1)
        hh_w = signal("dve", "householder_weights", 1)
        hh_upd = signal("dve", "householder_applied", 1)
        ho_mm = signal("pe", "series_product", 1)
        ho_dve = signal("dve", "series_term_added", 1)
        sq_mm = signal("pe", "square_product", 1)
        sq_t = signal("dve", "square_difference", 1)
        sq_dve = signal("dve", "square_taken", 1)
        rt_x = signal("dve", "rotation_x_copied", 1)
        rt_T = signal("pe", "rotation_x_transposed", NC3)
        rt_h = signal("act", "rotation_xT_copied", NC3)
        rt_z = signal("pe", "rotation_z", 1)
        rt_zc = signal("dve", "rotation_z_copied", 1)
        rt_mm = signal("pe", "rotation_product", TB)
        rt_add = signal("dve", "rotation_added", TB)

        ITER0 = (0, 4 * E, 4 * E + 4)
        NE = (E, 1, 1)
        WSET = (0, E, E + 1)

        def stacked(part, parts, g, i, slots):
            src = part[i].rearrange("p (h c) -> p h c", c=HD)
            dst = parts[g % 2][:, :, 0:KM].rearrange("p h (s c) -> p h s c", c=HD)[:, :, slots, :]
            return dst, src.unsqueeze(2).to_broadcast([P, TB * G, dst.shape[2], HD])

        HIGH_SLOTS = (slice(0, 3), slice(1, 6, 2))
        MIDDLE_SLOTS = (slice(3, 5), slice(2, 5, 2))

        block = ctx.enter_context(nc.Block())

        @block.sync
        def _(sp):
            def load_attention(l):
                n = LAYERS[l]
                sp.dma_start(w_qkv[:, :, :], dram[n + "_w_qkv"].rearrange("(c p) n -> p c n", p=CH)).then_inc(s_attw[l], 16)
                sp.dma_start(w_proj[:, :, :], dram[n + "_w_proj"]).then_inc(s_attw[l], 16)
                sp.dma_start(b_qkv[:, :], dram[n + "_b_qkv"].partition_broadcast(P)).then_inc(s_attw[l], 16)

            def load_mod(l):
                n = LAYERS[l]
                sp.dma_start(w_mod, dram[n + "_w_mod"].rearrange("(c p) n -> p c n", p=CH)).then_inc(s_modw[l], 16)
                for i, k in ((0, 2), (1, 5)):
                    sp.dma_start(gate_bias[:, i, :], dram[n + "_b_mod"][k * C:(k + 1) * C].partition_broadcast(P)).then_inc(s_modw[l], 16)

            def load_expert(l, e):
                n, q = LAYERS[l], WSET[l] + e
                w1, w2, b2, b1 = experts[e % 2]
                sp.dma_start(w1, dram[n + "_w1"][e].rearrange("(c p) n -> p c n", p=CH)).then_inc(s_mlpw[q], 16)
                sp.dma_start(w2, dram[n + "_w2"][e].rearrange("(m p) n -> p m n", p=P)).then_inc(s_mlpw[q], 16)
                sp.dma_start(b2, dram[n + "_b2"][e].partition_broadcast(P)).then_inc(s_mlpw[q], 16)
                sp.dma_start(b1, dram[n + "_b1"][e]).then_inc(s_mlpw[q], 16)

            sp.dma_start(cond[:, :, :], dram["cond"]).then_inc(s_start, 16)
            sp.dma_start(mod_bias[:, :, :], dram["mod_bias"]).then_inc(s_start, 16)
            sp.dma_start(eye[:, :], dram["c_eye"]).then_inc(s_const, 16)
            sp.dma_start(sel[:, :], dram["c_sel"]).then_inc(s_const, 16)
            sp.dma_start(before[:, :], dram["c_before"]).then_inc(s_const, 16)
            sp.dma_start(gather[:, :, :], dram["c_gather"]).then_inc(s_const, 16)
            sp.dma_start(spread[:, :, :], dram["c_spread"]).then_inc(s_const, 16)
            load_mod(0)
            sp.dma_start(x[:, :, :], dram["x"].rearrange("b (t p) c -> p (b t) c", p=P)).then_inc(s_x, 16)
            load_attention(0)
            sp.dma_start(b_skew, dram["b_skew"].partition_broadcast(B)).then_inc(s_skew_b, 16)
            for i in range(8):
                if i >= 2:
                    sp.wait_ge(s_skew_mm, i - 1)
                sp.dma_start(w_skew[i % 2], dram["w_skew"][:, i * 512:(i + 1) * 512].rearrange("(c p) n -> p c n", p=CH)).then_inc(s_skew_w[i % 2], 16)
            load_expert(0, 0)
            sp.dma_start(w_gate[:, :, :], dram["w_gate"].rearrange("(c p) n -> p c n", p=CH)).then_inc(s_start, 16)
            sp.dma_start(g_qk[:, 0:C], dram["g_q"].partition_broadcast(P)).then_inc(s_start, 16)
            sp.dma_start(g_qk[:, C:2 * C], dram["g_k"].partition_broadcast(P)).then_inc(s_start, 16)
            sp.wait_ge(s_skew_v, 8)
            sp.dma_start(scratch, v_skew).then_inc(s_skew_out, 16)
            sp.wait_ge(s_skew_out, 16)
            sp.dma_start(A[:, :, :], scratch.rearrange("b (i j) -> i b j", j=D)).then_inc(s_skew_in, 16)
            sp.wait_ge(proj_mm.sem, proj_mm.at(B, 0))
            load_expert(0, 1)
            sp.dma_start(small, dram["c_small"]).then_inc(s_lin, 16)
            sp.dma_start(pT_, dram["pT"]).then_inc(s_lin, 16)
            load_attention(1)
            sp.wait_ge(f2_mm.sem, f2_mm.at(4, 0))
            sp.wait_ge(x2_ready.sem, x2_ready.at(4, 0))
            load_expert(0, 2)
            sp.wait_ge(f2_mm.sem, f2_mm.at(8, 0))
            sp.wait_ge(x2_ready.sem, x2_ready.at(8, 0))
            load_expert(0, 3)
            sp.wait_ge(f2_mm.sem, f2_mm.at(12, 0))
            sp.wait_ge(x2_ready.sem, x2_ready.at(12, 0))
            load_expert(1, 0)
            sp.wait_ge(f2_mm.sem, f2_mm.at(16, 0))
            sp.wait_ge(x2_ready.sem, x2_ready.at(16, 0))
            load_mod(1)
            sp.wait_ge(proj_mm.sem, proj_mm.at(2 * B, 0))
            load_attention(2)
            load_mod(2)
            sp.wait_ge(f2_mm.sem, f2_mm.at(20, 0))
            sp.wait_ge(x2_ready.sem, x2_ready.at(20, 0))
            load_expert(2, 0)
            for b in range(B):
                sp.wait_ge(x2_ready.sem, x2_ready.at(21 + b, 0))
                sp.dma_start(dram["out"][b].rearrange("(t p) c -> p t c", p=P), x[:, TB * b:TB * (b + 1), :]).then_inc(s_out, 16)
            sp.wait_ge(s_out, 16 * B)

        @block.gpsimd
        def _(pool):
            grant_credit(pool, "pool")
            def settle():
                pool.sem_inc(s_passed_pool, 1)

            nc.gpsimd.memset(consts[:, 0:TB], -0.5)
            nc.gpsimd.memset(consts[:, TB:2 * TB], EPS)
            nc.gpsimd.memset(half[:, :], 0.5)
            nc.gpsimd.memset(var_eps[:, 1, :], EPS).then_inc(s_init, 2)
            pool.wait_ge(s_init, 2)

            def ln_root(m):
                pool.wait_ge(ln_mv.sem, ln_mv.at(m, TB))
                nc.gpsimd.tensor_tensor(var_eps[:, 0, :], meanvar[:, :, 1], consts[:, TB:2 * TB], ALU.add).then_inc(ln_eps.sem, 1)
                pool.wait_ge(ln_eps.sem, ln_eps.at(m, 1))
                pool.wait_ge(ln_xhat.sem, ln_xhat.at(m, 0))
                nc.gpsimd.tensor_tensor(rstd[:, :], var_eps[:, 0, :], consts[:, 0:TB], ALU.pow).then_inc(ln_rstd.sem, 1)

            def spread_silu(l):
                if l:
                    pool.wait_ge(f2_mm.sem, f2_mm.at(ITER0[l], 0))
                nc.gpsimd.tensor_copy(silu_b, silu[:, :, :].rearrange("p c b -> p (c b)").unsqueeze(2).to_broadcast([CH, NC3 * B, P])).then_inc(s_silu_b, 1)

            def stack(n, g, i):
                pool.wait_ge(split_ready.sem, split_ready.at(n, 2 * g + i + 1))
                settle()
                nc.gpsimd.tensor_copy(*stacked(part_h, (kp, qp)[i], g, i, HIGH_SLOTS[i]))
                nc.gpsimd.tensor_copy(*stacked(part_m, (kp, qp)[i], g, i, MIDDLE_SLOTS[i])).then_inc(rep_done.sem, 1)

            def stage_values(n, g):
                if g == 0:
                    pool.wait_ge(qkv_ready.sem, qkv_ready.at(n, 2 * TB))
                pool.wait_ge(av_done.sem, av_done.at(n, 4 * (g - 1)))
                settle()
                nc.gpsimd.tensor_copy(
                    vg[g % 2].rearrange("p t (h c) -> p t h c", c=HP)[:, :, :, 0:HD],
                    qkv[:, :, 2 * C + g * GW:2 * C + (g + 1) * GW].rearrange("p t (h c) -> p t h c", c=HD)).then_inc(v_staged.sem, 1)

            def attention(l):
                with pool.Fori(0, B) as b:
                    n = b + l * B
                    ln_root(n * 2)
                    for g, i in ((1, 0), (1, 1)):
                        stack(n, g, i)
                    for g in range(2):
                        stage_values(n, g)
                    stack(n, 2, 0)
                    for g in range(2, NG):
                        stack(n, g, 1)
                        if g + 1 < NG:
                            stack(n, g + 1, 0)
                        stage_values(n, g)
                    ln_root(n * 2 + 1)

            pool.wait_ge(s_silu, 1)
            spread_silu(0)

            def set_stage_constants(l):
                pool.wait_ge(s_mod, 9 * (l + 1))
                if l == 0:
                    pool.wait_ge(s_skew_v, 8)
                for i in range(2):
                    v = vg[i].rearrange("p t (h c) -> p (t h) c", c=HP)
                    nc.gpsimd.memset(v[:, :, HD:HD + 1], 1.0)
                    nc.gpsimd.memset(v[:, :, HD + 1:HP], 0.0)
                    nc.gpsimd.memset(kp[i][:, :, KM:KS], 1.0).then_inc(s_init, 1)

            set_stage_constants(0)
            pool.wait_ge(s_skew_out, 16)
            attention(0)
            pool.wait_ge(s_const, 80)
            pool.wait_ge(x1_ready.sem, x1_ready.at(B, 0))
            pool.wait_ge(o_ready.sem, o_ready.at(B, 0))
            with pool.Fori(0, D) as j:
                pool.wait_ge(hh_mm.sem, hh_mm.at(j, 0))
                settle()
                nc.gpsimd.tensor_copy(pick[:, :], eye[0:D, bass.ds(j, 1)].to_broadcast([D, P])).then_inc(hh_pick.sem, 1)
                pool.wait_ge(hh_nrm2.sem, hh_nrm2.at(j, 1))
                nc.gpsimd.tensor_tensor(hs[:, 2:3], hs[:, 1:2], half[:, :], ALU.pow).then_inc(hh_nrm.sem, 1)
            spread_silu(1)
            set_stage_constants(1)
            attention(1)
            spread_silu(2)
            set_stage_constants(2)
            attention(2)

        @block.scalar
        def _(act):
            grant_credit(act, "act")

            def modulate(m, b, kind):
                for c in range(NC3):
                    act.wait_ge(ln_T.sem, ln_T.at(m, c + 1))
                    nc.scalar.activation(hT[:, c, :], banks3[c][0:CH, :], ACT.Identity,
                                         bias=modT[:, kind, c, bass.ds(b, 1)],
                                         scale=modT[:, kind + 1, c, bass.ds(b, 1)]).then_inc(h_ready.sem, 1)

            def copy_heads(n, g, i):
                rows = KM if i in (2, 3) else KS
                dst = (kT if i < 2 else qT)[g % 3]
                act.wait_ge(t_mm.sem, t_mm.at(n, SET_TURN[g, i]))
                h = i % 2
                nc.scalar.activation(dst[0:rows, 2 * h:2 * h + 2, :],
                                     banks3_16[set_bank(g, i)][0:rows, :].rearrange("p (h n) -> p h n", h=2),
                                     ACT.Copy).then_inc(t_ev.sem, 1)

            def attention(l):
                with act.Fori(0, B) as b:
                    n = b + l * B
                    act.wait_ge(h2_ready.sem, h2_ready.at(n, 0))
                    modulate(n * 2, b, 0)
                    if l == 1:
                        act.wait_ge(qkn.sem, qkn.at(b, 4))
                        nc.scalar.activation(head_inv[:, :, :], head_tmp[:, :, :], ACT.Sqrt).then_inc(qkn_root.sem, 1)
                    for i in range(2):
                        act.wait_ge(split_ready.sem, split_ready.at(n, i + 1))
                        for part, slots in ((part_h, HIGH_SLOTS[i]), (part_m, MIDDLE_SLOTS[i])):
                            last = nc.scalar.activation(*stacked(part, (kp, qp)[i], 0, i, slots), ACT.Copy)
                        last.then_inc(rep_first.sem, 1)
                    for g, i in SET_ORDER[0:10]:
                        copy_heads(n, g, i)
                    for g in range(NG):
                        for kb in range(TB):
                            for h in range(2):
                                if h == 0:
                                    act.wait_ge(av_done.sem, av_done.at(n, 4 * g + kb - 1))
                                act.wait_ge(s_mm.sem, s_mm.at(n, 8 * g + 2 * kb + h + 1))
                                nc.scalar.activation(pT[:, kb % 2, 1024 * h:1024 * (h + 1)],
                                                     psS[:, 2 * h:2 * h + 2, :].rearrange("p a n -> p (a n)"),
                                                     ACT.Exp, scale=SCALE).then_inc(exp_done.sem, 1)
                            if g + 2 < NG:
                                copy_heads(n, g + 2, kb)
                        if g + 1 < NG:
                            for i in (4, 5):
                                copy_heads(n, g + 1, i)
                    modulate(n * 2 + 1, b, 2)
                    act.wait_ge(h_ready.sem, h_ready.at(n * 2 + 2, 0))
                    act.sem_inc(s_passed_act, 1)
                    nc.scalar.activation(h2T[:, :, bass.ds(b * N, N)], hT[:, :, :], ACT.Copy).then_inc(h2_ready.sem, 1)

            def mlp(l, e):
                b1 = experts[e % 2][3]
                act.wait_ge(s_mlpw[WSET[l] + e], 64)
                with act.Fori(0, B) as b:
                    q = b + (ITER0[l] + B * e)
                    for m in range(MH):
                        if m == 0:
                            act.wait_ge(f2_mm.sem, f2_mm.at(q, 0))
                        act.wait_ge(f1_mm.sem, f1_mm.at(q, m + 1))
                        nc.scalar.activation(hid[:, m, :], psS[:, m % 4, :], ACT.Gelu_apprx_tanh,
                                             bias=b1[:, m:m + 1]).then_inc(hid_ready.sem, 1)

            act.wait_ge(s_start, 32)
            nc.scalar.activation(silu_t[:, :, :], cond[:, :, :], ACT.Exp, scale=-1.0).then_inc(s_exp0, 1)
            act.wait_ge(s_mod, 9)
            attention(0)
            act.wait_ge(s_top_in, 1)
            nc.scalar.activation(top[:, 0:NT * E], top[:, 0:NT * E], ACT.Exp).then_inc(s_top_exp, 1)
            act.wait_ge(s_top, TOP_STEPS)
            for e in range(E):
                mlp(0, e)
            with act.Fori(0, B) as b:
                for c in range(NC3):
                    act.wait_ge(rt_T.sem, rt_T.at(b, c + 1))
                    nc.scalar.activation(hT[:, c, :], banks3[c][0:CH, :], ACT.Copy).then_inc(rt_h.sem, 1)
            act.wait_ge(s_mod, 18)
            attention(1)
            act.wait_ge(o_ready.sem, o_ready.at(2 * B, 0))
            mlp(1, 0)
            act.wait_ge(s_mod, 27)
            attention(2)
            act.wait_ge(o_ready.sem, o_ready.at(3 * B, 0))
            mlp(2, 0)

        @block.vector
        def _(dve):
            grant_credit(dve, "dve")
            v = nc.vector
            def settle():
                dve.sem_inc(s_passed_dve, 1)

            def layer_norm(m, b):
                for t in range(TB):
                    v.bn_stats(stats[:, t, :], x[:, b * TB + t, :]).then_inc(ln_stats.sem, 1)
                for t in range(TB):
                    dve.wait_ge(ln_stats.sem, ln_stats.at(m, t + 1))
                    settle()
                    v.bn_aggr(meanvar[:, t, :], stats[:, t, :]).then_inc(ln_mv.sem, 1)
                dve.wait_ge(ln_T.sem, ln_T.at(m, 0))
                dve.wait_ge(ln_rstd.sem, ln_rstd.at(m, 1))
                for t in range(TB):
                    v.tensor_scalar(xhat[:, t, :], x[:, b * TB + t, :], meanvar[:, t, 0:1], rstd[:, t:t + 1],
                                    ALU.subtract, ALU.mult).then_inc(ln_xhat.sem, 1)

            def qk_norm(b):
                heads = qkv[:, :, 0:2 * C].rearrange("p t (h c) -> p t h c", c=HD)
                sq = square.rearrange("p t (h c) -> p t h c", c=HD)

                def step(ins, k):
                    ins.then_inc(qkn.sem, 1)
                    dve.wait_ge(qkn.sem, qkn.at(b, k))

                def wide(a):
                    return a.unsqueeze(3).to_broadcast([P, TB, 2 * NH, HD])

                step(v.tensor_reduce(head_sum[:, :, :], heads, AX_X, ALU.add), 1)
                step(v.tensor_scalar(head_sum[:, :, :], head_sum[:, :, :], 1.0 / HD, None, ALU.mult), 2)
                for t in range(TB):
                    last = v.tensor_tensor(heads[:, t], heads[:, t], wide(head_sum[:, :, :])[:, t], ALU.subtract)
                last.then_inc(qkn.sem, 1)
                dve.wait_ge(qkn.sem, qkn.at(b, 3))
                v.tensor_tensor(square, qkv[:, :, 0:2 * C], qkv[:, :, 0:2 * C], ALU.mult).then_inc(sq_ready.sem, 1)
                dve.wait_ge(sq_ready.sem, sq_ready.at(b, 1))
                v.tensor_reduce(head_sum[:, :, :], sq, AX_X, ALU.add).then_inc(sq_ready.sem, 1)
                dve.wait_ge(sq_ready.sem, sq_ready.at(b, 2))
                v.tensor_scalar(head_tmp[:, :, :], head_sum[:, :, :], 1.0 / HD, EPS, ALU.mult, ALU.add).then_inc(qkn.sem, 1)
                v.tensor_tensor(qkv[:, :, 0:2 * C], qkv[:, :, 0:2 * C],
                                g_qk[:, :].unsqueeze(1).to_broadcast([P, TB, 2 * C]), ALU.mult)
                dve.wait_ge(qkn_root.sem, qkn_root.at(b, 1))
                step(v.reciprocal(head_inv[:, :, :], head_inv[:, :, :]), 5)
                step(v.tensor_tensor(head_tmp[:, :, :], head_tmp[:, :, :], head_inv[:, :, :], ALU.mult), 6)
                step(v.tensor_tensor(head_tmp[:, :, :], head_tmp[:, :, :], head_inv[:, :, :], ALU.mult), 7)
                step(v.tensor_scalar(head_tmp[:, :, :], head_tmp[:, :, :], -0.5, 1.5, ALU.mult, ALU.add), 8)
                v.tensor_tensor(head_inv[:, :, :], head_tmp[:, :, :], head_inv[:, :, :], ALU.mult).then_inc(sq_ready.sem, 1)
                dve.wait_ge(sq_ready.sem, sq_ready.at(b, 3))
                for t in range(TB):
                    last = v.tensor_tensor(heads[:, t], heads[:, t], wide(head_inv[:, :, :])[:, t], ALU.mult)
                last.then_inc(qkn.sem, 1)
                dve.wait_ge(qkn.sem, qkn.at(b, 9))

            def split(n, g, i):
                parts, col, low = ((kp, C, 5), (qp, 0, 0))[i]
                src = qkv[:, :, col + g * GW:col + (g + 1) * GW]
                r = rest[i].rearrange("p (t c) -> p t c", t=TB)
                h = part_h[i].rearrange("p (t c) -> p t c", t=TB)
                k0 = 6 * g + 3 * i
                if g == 1:
                    dve.wait_ge(rep_first.sem, rep_first.at(n, i + 1))
                else:
                    dve.wait_ge(rep_done.sem, rep_done.at(n, 2 * (g - 2) + i + 1 if g else 0))
                v.tensor_copy(h, src).then_inc(split_step.sem, 1)
                dve.wait_ge(split_step.sem, split_step.at(n, k0 + 1))
                v.tensor_tensor(r, src, h, ALU.subtract).then_inc(split_step.sem, 1)
                dve.wait_ge(split_step.sem, split_step.at(n, k0 + 2))
                v.tensor_copy(part_m[i], rest[i]).then_inc(split_step.sem, 1)
                dve.wait_ge(t_mm.sem, t_mm.at(n, SET_TURN[g - 2, 5 if i else 1] if g >= 2 else 0))
                dve.wait_ge(split_step.sem, split_step.at(n, k0 + 3))
                v.tensor_tensor(parts[g % 2][:, :, low * HD:(low + 1) * HD], rest[i].rearrange("p (h c) -> p h c", c=HD),
                                part_m[i].rearrange("p (h c) -> p h c", c=HD), ALU.subtract).then_inc(split_ready.sem, 1)

            def maxima(n, g):
                for j in range(G):
                    if j == 2 and g + 2 < NG:
                        split(n, g + 2, 0)
                    for t in range(TB):
                        i = 16 * g + 4 * j + t
                        dve.wait_ge(max_mm.sem, max_mm.at(n, i + 1))
                        v.tensor_reduce(mx[:, t * G + j:t * G + j + 1], psM[:, t % 2, :], AX_X, ALU.max).then_inc(max_done.sem, 1)
                neg = [qp[g % 2][:, :, KM + i] for i in range(3)]
                dve.wait_ge(max_done.sem, max_done.at(n, 16 * (g + 1)))
                v.tensor_scalar(neg[0], mx[:, :], -1.0, None, ALU.mult).then_inc(mparts.sem, 1)
                dve.wait_ge(mparts.sem, mparts.at(n, 3 * g + 1))
                v.scalar_tensor_tensor(out=mrest[:, :], in0=mx[:, :], scalar=-1.0, in1=neg[0], op0=ALU.mult,
                                       op1=ALU.subtract).then_inc(mparts.sem, 1)
                dve.wait_ge(mparts.sem, mparts.at(n, 3 * g + 2))
                v.tensor_copy(neg[1], mrest[:, :]).then_inc(mparts.sem, 1)
                dve.wait_ge(mparts.sem, mparts.at(n, 3 * g + 3))
                v.tensor_tensor(neg[2], mrest[:, :], neg[1], ALU.subtract).then_inc(m_ready.sem, 1)

            def keep_sums(n, g):
                if g == 0:
                    dve.wait_ge(proj_mm.sem, proj_mm.at(n, 0))
                dve.wait_ge(av_done.sem, av_done.at(n, 4 * g + 4))
                v.tensor_copy(oT[:, g, :], psO[:, :]).then_inc(o_raw.sem, 1)

            def divide_first_groups(n):
                dve.wait_ge(d_mm.sem, d_mm.at(n, 1))
                v.reciprocal(rD[0:(NG - 1) * G], psM[0:(NG - 1) * G, 0, :]).then_inc(recip.sem, 1)
                for g in range(NG - 1):
                    dve.wait_ge(d_mm.sem, d_mm.at(n, 2 + g))
                    v.tensor_tensor(oT[:, g, :], oT[:, g, :], banks3[(2, 0, 1)[g]], ALU.mult).then_inc(o_ready.sem, 1)

            def divide_last_group(n):
                dve.wait_ge(d_mm.sem, d_mm.at(n, NG + 1))
                v.reciprocal(rD, psM[:, 1, :]).then_inc(recip.sem, 1)
                dve.wait_ge(recip.sem, recip.at(n, 2))
                v.tensor_tensor(oT[:, NG - 1, :], oT[:, NG - 1, :], rD, ALU.mult).then_inc(o_ready.sem, 1)

            def attention(l):
                dve.wait_ge(s_attw[l], 48)
                with dve.Fori(0, B) as b:
                    n = b + l * B
                    layer_norm(n * 2, b)
                    dve.wait_ge(v_staged.sem, v_staged.at(n, 0))
                    for i in range(2 * TB):
                        t, h = divmod(i, 2)
                        w = 3 * C // 2
                        dve.wait_ge(qkv_mm.sem, qkv_mm.at(n, i + 1))
                        v.tensor_tensor(qkv[:, t, h * w:(h + 1) * w], psS[:, i % 4, 0:w], b_qkv[:, h * w:(h + 1) * w],
                                        ALU.add).then_inc(qkv_ready.sem, 1)
                    dve.wait_ge(qkv_ready.sem, qkv_ready.at(n, 2 * TB))
                    if l == 1:
                        qk_norm(b)
                    for g, i in ((0, 0), (0, 1), (1, 0), (1, 1)):
                        split(n, g, i)
                    maxima(n, 0)
                    for g in range(NG):
                        if g + 2 < NG:
                            split(n, g + 2, 1)
                        if g + 1 < NG:
                            maxima(n, g + 1)
                        else:
                            divide_first_groups(n)
                        keep_sums(n, g)
                    divide_last_group(n)
                    for t in range(TB):
                        dve.wait_ge(proj_mm.sem, proj_mm.at(n, t + 1))
                        v.tensor_tensor(tmp[:, t % 2, :], psS[:, t, 0:C], gates[:, b, 0, :], ALU.mult).then_inc(proj_read.sem, 1)
                        dve.wait_ge(proj_read.sem, proj_read.at(n, t + 1))
                        v.tensor_tensor(x[:, b * TB + t, :], x[:, b * TB + t, :], tmp[:, t % 2, :], ALU.add).then_inc(x1_ready.sem, 1)
                    dve.wait_ge(x1_ready.sem, x1_ready.at(n, TB))
                    settle()
                    layer_norm(n * 2 + 1, b)
                    if l == 0:
                        dve.wait_ge(gate_mm.sem, gate_mm.at(b, 1))
                        v.tensor_copy(logits[:, bass.ds(b * TB, TB), :].rearrange("p t e -> p (t e)"),
                                      psT[:, 0:TB * E]).then_inc(gate_read.sem, 1)

            def mlp_out(l, q, b, e):
                b2 = experts[e % 2][2]
                for t in range(TB):
                    xt = x[:, b * TB + t, :]
                    dve.wait_ge(f2_mm.sem, f2_mm.at(q, t + 1))
                    v.tensor_tensor(tmp[:, t % 2, :], psM[:, t % 2, 0:C], b2, ALU.add).then_inc(f2_read.sem, 1)
                    dve.wait_ge(f2_read.sem, f2_read.at(q, t + 1))
                    if l == 0:
                        v.scalar_tensor_tensor(out=tmp[:, t % 2, :], in0=tmp[:, t % 2, :], scalar=cw[:, b * TB + t, e:e + 1],
                                               in1=gates[:, b, 1, :], op0=ALU.mult, op1=ALU.mult).then_inc(f2_scaled.sem, 1)
                    else:
                        v.tensor_tensor(tmp[:, t % 2, :], tmp[:, t % 2, :], gates[:, b, 1, :], ALU.mult).then_inc(f2_scaled.sem, 1)
                    dve.wait_ge(f2_scaled.sem, f2_scaled.at(q, t + 1))
                    v.tensor_tensor(xt, xt, tmp[:, t % 2, :], ALU.add).then_inc(x2_ready.sem, 1)

            def mods(l):
                dve.wait_ge(s_modw[l], 48)
                if l:
                    dve.wait_ge(h_ready.sem, h_ready.at(2 * B * l, 0))
                    dve.wait_ge(x2_ready.sem, x2_ready.at(ITER0[l], 0))
                dve.wait_ge(s_mod_mm, 9 * l + 1)
                flat = modT[:, :, :, :].rearrange("p k c b -> p (k c) b")
                v.tensor_tensor(flat, psM[0:CH, 0, 0:4 * NC3 * B].rearrange("p (k b) -> p k b", b=B),
                                mod_bias[:, l, :].unsqueeze(2).to_broadcast([CH, 4 * NC3, B]), ALU.add).then_inc(s_modstep, 1)
                dve.wait_ge(s_modstep, 3 * l + 1)
                for k in (1, 3):
                    ins = v.tensor_scalar(modT[:, k, :, :], modT[:, k, :, :], 1.0, None, ALU.add)
                    ins.then_inc(s_modstep, 1)
                dve.wait_ge(s_modstep, 3 * l + 3)
                dve.sem_inc(s_mod, 1)
                for i in range(2 * B):
                    dve.wait_ge(s_mod_mm, 9 * l + 2 + i)
                    v.tensor_tensor(gates[:, i // 2, i % 2, :], psS[:, i % 4, 0:C], gate_bias[:, i % 2, :], ALU.add).then_inc(s_mod, 1)
                dve.wait_ge(s_mod, 9 * l + 9)

            def top_two():
                count = [0]

                def step(ins):
                    count[0] += 1
                    ins.then_inc(s_top, 1)
                    dve.wait_ge(s_top, count[0])

                lg = logits[:, :, :]
                d = top[:, 0:NT * E].rearrange("p (t e) -> p t e", e=E)
                big = NT * E * E
                ge = top[:, big:2 * big].rearrange("p (t e f) -> p t e f", e=E, f=E)
                gt = top[:, 2 * big:3 * big].rearrange("p (t e f) -> p t e f", e=E, f=E)
                one = top[:, 3 * big:3 * big + NT]
                inv_s = top[:, 3 * big + NT:3 * big + 2 * NT]
                rank = top[:, 4 * big:4 * big + NT * E].rearrange("p (t e) -> p t e", e=E)
                dve.wait_ge(gate_read.sem, gate_read.at(B, 0))
                dve.wait_ge(o_ready.sem, o_ready.at(B, 0))
                dve.wait_ge(split_ready.sem, split_ready.at(B, 0))
                step(v.tensor_reduce(one, lg, AX_X, ALU.max))
                step(v.tensor_tensor(d, lg, one.unsqueeze(2).to_broadcast([P, NT, E]), ALU.subtract))
                dve.sem_inc(s_top_in, 1)
                other = lg.unsqueeze(2).to_broadcast([P, NT, E, E])
                own = lg.unsqueeze(3).to_broadcast([P, NT, E, E])
                step(v.tensor_tensor(ge, other, own, ALU.is_ge))
                step(v.tensor_tensor(gt, other, own, ALU.is_gt))
                ge_f = ge.rearrange("p t e f -> p t (e f)")
                gt_f = gt.rearrange("p t e f -> p t (e f)")
                step(v.tensor_tensor(ge_f, ge_f, gt_f, ALU.subtract))
                step(v.tensor_tensor(ge_f, ge_f, before[:, :].unsqueeze(1).to_broadcast([P, NT, E * E]), ALU.mult))
                step(v.tensor_tensor(ge_f, ge_f, gt_f, ALU.add))
                step(v.tensor_reduce(rank, ge, AX_X, ALU.add))
                dve.wait_ge(s_top_exp, 1)
                step(v.scalar_tensor_tensor(out=rank, in0=rank, scalar=1.5, in1=d, op0=ALU.is_lt, op1=ALU.mult))
                step(v.tensor_reduce(one, rank, AX_X, ALU.add))
                step(v.reciprocal(inv_s, one))
                step(v.tensor_tensor(cw[:, :, :], rank, inv_s.unsqueeze(2).to_broadcast([P, NT, E]), ALU.mult))
                assert count[0] == TOP_STEPS, count

            def householder(j):
                col = pT_[:, bass.ds(j, C)]
                s = lambda i: hs[:, i:i + 1]
                done = [0]

                def step(ins):
                    done[0] += 1
                    ins.then_inc(hh_step.sem, 1)
                    return done[0]

                def after(k):
                    dve.wait_ge(hh_step.sem, hh_step.at(j, k))

                dve.wait_ge(hh_mm.sem, hh_mm.at(j, 1))
                dve.wait_ge(hh_upd.sem, hh_upd.at(j, 0))
                after(step(v.tensor_copy(vb, psO[0:D, 0:C])))
                step(v.tensor_tensor_reduce(junk[:, 1:C], vb[:, 1:C], vb[:, 1:C], 1.0, 0.0, ALU.mult, ALU.add, s(0)))
                after(step(v.scalar_tensor_tensor(out=uT, in0=vb, scalar=1.0, in1=col, op0=ALU.mult, op1=ALU.mult, accum_out=s(3))))
                v.scalar_tensor_tensor(out=s(1), in0=vb[:, 0:1], scalar=vb[:, 0:1], in1=s(0), op0=ALU.mult, op1=ALU.add).then_inc(hh_nrm2.sem, 1)
                step(v.tensor_scalar(s(4), vb[:, 0:1], 0.0, 2.0, ALU.is_ge, ALU.mult))
                after(4)
                dve.wait_ge(hh_nrm.sem, hh_nrm.at(j, 1))
                nb = nbs[:, bass.ds(j, 1)]
                after(step(v.scalar_tensor_tensor(out=nb, in0=s(4), scalar=-1.0, in1=s(2), op0=ALU.add, op1=ALU.mult)))
                after(step(v.tensor_tensor(vb[:, 0:1], vb[:, 0:1], nb, ALU.add)))
                after(step(v.tensor_tensor(s(5), vb[:, 0:1], nb, ALU.mult)))
                after(step(v.tensor_scalar(s(5), s(5), 1e-37, None, ALU.max)))
                step(v.scalar_tensor_tensor(out=s(3), in0=pT_[:, bass.ds(j, 1)], scalar=nb, in1=s(3), op0=ALU.mult, op1=ALU.add))
                after(step(v.reciprocal(s(6), s(5))))
                after(step(v.scalar_tensor_tensor(out=cs[:, bass.ds(j, 1)], in0=s(0), scalar=0.0, in1=s(6), op0=ALU.is_gt, op1=ALU.mult)))
                assert done[0] == hh_step.per, done
                v.scalar_tensor_tensor(out=s(7), in0=s(3), scalar=cs[:, bass.ds(j, 1)], in1=below[:, bass.ds(j, 1)],
                                       op0=ALU.mult, op1=ALU.mult).then_inc(hh_w.sem, 1)
                dve.wait_ge(hh_w.sem, hh_w.at(j, 1))
                v.scalar_tensor_tensor(out=col, in0=vb, scalar=s(7), in1=col, op0=ALU.mult, op1=ALU.add).then_inc(hh_upd.sem, 1)

            def rotation():
                count = [0]

                def step(ins):
                    count[0] += 1
                    ins.then_inc(s_lin_dve, 1)
                    dve.wait_ge(s_lin_dve, count[0])

                def product(k):
                    dve.wait_ge(s_lin_pe, k)

                e64 = eye[0:D, 0:D]
                dve.wait_ge(hh_upd.sem, hh_upd.at(D, 0))
                step(v.tensor_tensor_reduce(junk[:, 0:D], nbs, e64, 1.0, 0.0, ALU.mult, ALU.add, hs[:, 8:9]))
                step(v.tensor_tensor_reduce(junk[:, 0:D], cs, e64, 1.0, 0.0, ALU.mult, ALU.add, hs[:, 9:10]))
                step(v.tensor_tensor(vT, pT_[:, 0:C], from_diag, ALU.mult))
                step(v.scalar_tensor_tensor(out=vT[:, 0:D], in0=e64, scalar=hs[:, 8:9], in1=vT[:, 0:D], op0=ALU.mult, op1=ALU.add))
                product(1)
                step(v.tensor_copy(v_c, psS[0:CH, 0, 0:NC3 * D].rearrange("p (c n) -> p c n", c=NC3)))
                product(2)
                step(v.scalar_tensor_tensor(out=mm[:, 0, :], in0=psS[0:D, 1, 0:D], scalar=hs[:, 9:10], in1=above, op0=ALU.mult, op1=ALU.mult))
                step(v.tensor_tensor(mm[:, 1, :], psS[0:D, 1, 0:D], cs, ALU.mult))
                step(v.tensor_tensor(mm[:, 1, :], mm[:, 1, :], below, ALU.mult))
                step(v.tensor_scalar(mm[:, 1, :], mm[:, 1, :], -1.0, None, ALU.mult))
                step(v.tensor_copy(inv, e64.unsqueeze(1).to_broadcast([D, 2, D])))
                for i in range(6):
                    step(v.tensor_tensor(lev[:, 0, :], mm[:, 0, :], level_masks[:, i, :], ALU.mult))
                    step(v.tensor_tensor(lev[:, 1, :], mm[:, 1, :], level_masks[:, 6 + i, :], ALU.mult))
                    product(3 + 2 * i)
                    step(v.tensor_copy(prod, psS[0:D, 0, 0:2 * D].rearrange("p (i n) -> p i n", i=2)))
                    product(4 + 2 * i)
                    step(v.tensor_tensor(inv, inv, psS[0:D, 1, 0:2 * D].rearrange("p (i n) -> p i n", i=2), ALU.subtract))
                step(v.tensor_scalar(tT, inv[:, 1, :], hs[:, 9:10], None, ALU.mult))
                product(15)
                step(v.tensor_copy(zT_, psS[0:D, 0, 0:D]))
                product(16)
                step(v.tensor_scalar(uT, psS[0:D, 1, 0:C], -1.0, None, ALU.mult))
                step(v.tensor_tensor(uT[:, 0:D], uT[:, 0:D], e64, ALU.add))
                product(17)
                step(v.tensor_copy(u_c, psS[0:CH, 0, 0:NC3 * D].rearrange("p (c n) -> p c n", c=NC3)))
                dve.wait_ge(s_skew_in, 16)
                step(v.tensor_tensor(A[:, :, :], A[:, :, :], sign.unsqueeze(1).to_broadcast([D, B, D]), ALU.mult))
                step(v.tensor_reduce(hs[:, 10:14], A[:, :, :], AX_X, ALU.add, apply_absolute_value=True))
                step(v.tensor_reduce(hs[:, 14:15], hs[:, 10:14], AX_X, ALU.max))
                product(18)
                step(v.tensor_reduce(junk[0:1, 0:1], psS[0:1, 0, 0:D], AX_X, ALU.max))
                product(19)
                step(v.tensor_copy(hs[:, 15:16], psS[0:D, 1, 0:1]))
                step(v.tensor_scalar(flags[:, 0:SQUARINGS], halves, hs[:, 15:16], 1.0, ALU.mult, ALU.is_gt))
                step(v.tensor_scalar(junk[:, 0:SQUARINGS], flags[:, 0:SQUARINGS], -0.5, 1.0, ALU.mult, ALU.add))
                w = SQUARINGS
                while w > 1:
                    w //= 2
                    step(v.tensor_tensor(junk[:, 0:w], junk[:, 0:w], junk[:, w:2 * w], ALU.mult))
                flat_a = A[:, :, :].rearrange("p b n -> p (b n)")
                step(v.tensor_scalar(xs[:, 0, :], flat_a, junk[:, 0:1], None, ALU.mult))
                step(v.tensor_scalar(xs[:, 1, :], xs[:, 0, :], -1.0, None, ALU.mult))
                ones = e64.unsqueeze(1).to_broadcast([D, 2 * B, D])
                ex3 = ex.rearrange("p (i n) -> p i n", n=D)
                step(v.tensor_copy(ex3, ones))
                assert count[0] == LIN_STEPS, count
                with dve.Fori(0, TAYLOR) as i:
                    dve.wait_ge(ho_mm.sem, ho_mm.at(i, 1))
                    v.scalar_tensor_tensor(out=ex3, in0=psS[0:D, 0, :].rearrange("p (i n) -> p i n", n=D),
                                           scalar=over_k[:, bass.ds(i, 1)], in1=ones, op0=ALU.mult, op1=ALU.add).then_inc(ho_dve.sem, 1)
                with dve.Fori(0, SQUARINGS) as i:
                    dve.wait_ge(sq_dve.sem, sq_dve.at(i, 0))
                    dve.wait_ge(sq_mm.sem, sq_mm.at(i, 1))
                    v.tensor_tensor(ex_t, psS[0:D, 1, :], ex, ALU.subtract).then_inc(sq_t.sem, 1)
                    dve.wait_ge(sq_t.sem, sq_t.at(i, 1))
                    v.scalar_tensor_tensor(out=ex, in0=ex_t, scalar=flags[:, bass.ds(i, 1)], in1=ex, op0=ALU.mult, op1=ALU.add).then_inc(sq_dve.sem, 1)
                dve.wait_ge(sq_dve.sem, sq_dve.at(SQUARINGS, 0))
                half_e = ex_t.rearrange("p (i n) -> p i n", n=D)[:, 0:B, :]
                step(v.tensor_tensor(half_e, ex3[:, B:2 * B, :], e64.unsqueeze(1).to_broadcast([D, B, D]), ALU.subtract))
                product(20)
                step(v.tensor_copy(w_rot, psS[0:D, :, 0:C]))
                dve.wait_ge(x2_ready.sem, x2_ready.at(4 * E, 0))
                with dve.Fori(0, B) as b:
                    dve.wait_ge(rt_T.sem, rt_T.at(b, 0))
                    v.tensor_copy(xhat[:, :, :], x[:, bass.ds(b * TB, TB), :]).then_inc(rt_x.sem, 1)
                    dve.wait_ge(rt_z.sem, rt_z.at(b, 1))
                    v.tensor_copy(zT, psO[0:D, :]).then_inc(rt_zc.sem, 1)
                    for t in range(TB):
                        xt = x[:, b * TB + t, :]
                        dve.wait_ge(rt_mm.sem, rt_mm.at(b, t + 1))
                        v.tensor_tensor(xt, psS[:, t, 0:C], xt, ALU.add).then_inc(rt_add.sem, 1)
                dve.wait_ge(rt_add.sem, rt_add.at(B, 0))

            dve.wait_ge(s_const, 80)
            v.tensor_copy(eye16[:, :], eye[:, :]).then_inc(s_eye, 1)
            dve.wait_ge(s_exp0, 1)
            v.tensor_scalar(silu_t[:, :, :], silu_t[:, :, :], 1.0, None, ALU.add).then_inc(s_eye, 1)
            dve.wait_ge(s_eye, 2)
            v.reciprocal(silu_t[:, :, :], silu_t[:, :, :]).then_inc(s_eye, 1)
            dve.wait_ge(s_eye, 3)
            v.tensor_tensor(silu[:, :, :], cond[:, :, :], silu_t[:, :, :], ALU.mult).then_inc(s_silu, 1)
            mods(0)
            dve.wait_ge(s_skew_b, 16)
            for i in range(8):
                dve.wait_ge(s_skew_mm, i + 1)
                v.tensor_tensor(v_skew[:, i * 512:(i + 1) * 512], psS[0:B, i % 4, :], b_skew[:, i * 512:(i + 1) * 512],
                                ALU.add).then_inc(s_skew_v, 1)
            dve.wait_ge(s_skew_v, 8)
            dve.wait_ge(s_x, 16)
            dve.wait_ge(s_init, 4)
            attention(0)
            top_two()
            dve.wait_ge(s_lin, 32)
            for e in range(E):
                dve.wait_ge(s_mlpw[e], 64)
                with dve.Fori(0, B) as b:
                    for s in range(4):
                        householder(b * 4 + (16 * e + s))
                    mlp_out(0, b + 4 * e, b, e)
                dve.wait_ge(x2_ready.sem, x2_ready.at(4 * (e + 1), 0))
            rotation()
            mods(1)
            dve.wait_ge(s_init, 6)
            dve.wait_ge(s_start, 80)
            attention(1)
            dve.wait_ge(s_mlpw[WSET[1]], 64)
            dve.wait_ge(x1_ready.sem, x1_ready.at(2 * B, 0))
            with dve.Fori(0, B) as b:
                mlp_out(1, b + ITER0[1], b, 0)
            dve.wait_ge(x2_ready.sem, x2_ready.at(ITER0[2], 0))
            mods(2)
            dve.wait_ge(s_init, 8)
            attention(2)
            dve.wait_ge(s_mlpw[WSET[2]], 64)
            with dve.Fori(0, B) as b:
                mlp_out(2, b + ITER0[2], b, 0)

        @block.tensor
        def _(pe):
            grant_credit(pe, "pe")
            mmul = nc.tensor.matmul
            def settle():
                pe.sem_inc(s_passed_pe, 1)

            def mods(l):
                pe.wait_ge(s_modw[l], 48)
                pe.wait_ge(s_silu, 1)
                if l:
                    pe.wait_ge(hid_ready.sem, hid_ready.at(ITER0[l], 0))
                    pe.wait_ge(x2_ready.sem, x2_ready.at(ITER0[l], 0))
                    if l == 1:
                        pe.wait_ge(rt_add.sem, rt_add.at(B, 0))
                for k, col in enumerate((0, 1, 3, 4)):
                    for c2 in range(NC3):
                        o = (k * NC3 + c2) * B
                        for c in range(NC3):
                            last = mmul(psM[0:CH, 0, o:o + B], w_mod[:, c, col * C + c2 * CH:col * C + (c2 + 1) * CH],
                                        silu[:, c, :], start=(c == 0), stop=(c == NC3 - 1))
                last.then_inc(s_mod_mm, 1)
                pe.wait_ge(s_silu_b, l + 1)
                for i in range(2 * B):
                    if i >= 4:
                        pe.wait_ge(s_mod, 9 * l + 1 + i - 3)
                    col = (2, 5)[i % 2] * C
                    for c in range(NC3):
                        last = mmul(psS[:, i % 4, 0:C], silu_b[:, c * B + i // 2, :], w_mod[:, c, col:col + C],
                                    start=(c == 0), stop=(c == NC3 - 1))
                    last.then_inc(s_mod_mm, 1)
                pe.wait_ge(s_mod, 9 * l + 9)

            def transpose_rows(sig, turn):
                for c in range(NC3):
                    for t in range(TB):
                        last = nc.tensor.transpose(banks3[c][0:CH, t * P:(t + 1) * P], xhat[:, t, c * CH:(c + 1) * CH], eye[:, :])
                    last.then_inc(sig.sem, 1)

            def transpose_heads(n, g, i):
                rows = KM if i in (2, 3) else KS
                src = (kp if i < 2 else qp)[g % 2]
                turn = SET_TURN[g, i]
                earlier = [k for k in range(1, turn) if set_bank(*SET_ORDER[k - 1]) == set_bank(g, i)]
                if earlier:
                    pe.wait_ge(t_ev.sem, t_ev.at(n, earlier[-1]))
                if i in (0, 2):
                    if g == 0:
                        pe.wait_ge(rep_first.sem, rep_first.at(n, i // 2 + 1))
                    else:
                        pe.wait_ge(rep_done.sem, rep_done.at(n, 2 * (g - 1) + i // 2 + 1))
                elif i == 4:
                    pe.wait_ge(m_ready.sem, m_ready.at(n, g + 1))
                for hh in range(2):
                    for t in range(TB):
                        o = (hh * TB + t) * P
                        last = nc.tensor.transpose(banks3_16[set_bank(g, i)][0:rows, o:o + P],
                                                   src[:, t * G + 2 * (i % 2) + hh, 0:rows], eye16[:, :])
                last.then_inc(t_mm.sem, 1)

            def max_scores(n, g, j, tiles=range(TB)):
                for t in tiles:
                    i = 16 * g + 4 * j + t
                    if j == 0 and t == 0:
                        pe.wait_ge(t_ev.sem, t_ev.at(n, SET_TURN[g, 3]))
                    if j == 0 and t == 1 and g:
                        pe.wait_ge(t_ev.sem, t_ev.at(n, SET_TURN[g - 1, 5]))
                    if j or t > 1:
                        pe.wait_ge(max_done.sem, max_done.at(n, i - 1))
                    mmul(psM[:, t % 2, :], qT[g % 3][0:KM, j, t * P:(t + 1) * P], kT[g % 3][0:KM, j, :],
                         start=True, stop=True).then_inc(max_mm.sem, 1)

            def scores(n, g, kb, h):
                i = 8 * g + 2 * kb + h
                if kb == 0:
                    pe.wait_ge(t_ev.sem, t_ev.at(n, SET_TURN[g, 4 + h]))
                pe.wait_ge(exp_done.sem, exp_done.at(n, i - 1))
                for hh in range(2):
                    last = mmul(psS[:, 2 * h + hh, :], kT[g % 3][0:KS, 2 * h + hh, kb * P:(kb + 1) * P],
                                qT[g % 3][0:KS, 2 * h + hh, :], start=True, stop=True)
                last.then_inc(s_mm.sem, 1)

            def values(n, g, kb):
                u = 4 * g + kb
                if kb == 0:
                    pe.wait_ge(v_staged.sem, v_staged.at(n, g + 1))
                    pe.wait_ge(o_raw.sem, o_raw.at(n, g))
                pe.wait_ge(exp_done.sem, exp_done.at(n, 2 * u + 2))
                for j in range(G):
                    last = mmul(psO[HP * j:HP * (j + 1), :], vg[g % 2][:, kb, HP * j:HP * (j + 1)],
                                pT[:, kb % 2, j * N:(j + 1) * N], start=(kb == 0), stop=(kb == TB - 1))
                last.then_inc(av_done.sem, 1)

            def gather_denominators(n):
                pe.wait_ge(o_raw.sem, o_raw.at(n, NG - 1))
                for g in range(NG - 1):
                    last = mmul(psM[0:(NG - 1) * G, 0, :], gather[:, g, :], oT[:, g, :], start=(g == 0), stop=(g == NG - 2))
                last.then_inc(d_mm.sem, 1)

            def spread_reciprocals(n):
                pe.wait_ge(recip.sem, recip.at(n, 1))
                k = (NG - 1) * G
                for g in range(NG - 1):
                    mmul(banks3[(2, 0, 1)[g]], spread[:, g, :], rD[0:k],
                         start=True, stop=True).then_inc(d_mm.sem, 1)

            def last_denominators(n):
                pe.wait_ge(o_raw.sem, o_raw.at(n, NG))
                pe.wait_ge(o_ready.sem, o_ready.at(n, 1))
                mmul(psM[:, 1, :], sel[:, :], oT[:, NG - 1, :], start=True, stop=True).then_inc(d_mm.sem, 1)

            def attention(l):
                pe.wait_ge(s_attw[l], 48)
                with pe.Fori(0, B) as b:
                    n = b + l * B
                    if l == 0:
                        pe.wait_ge(gate_read.sem, gate_read.at(b, 0))
                    pe.wait_ge(ln_xhat.sem, ln_xhat.at(n * 2 + 1, 0))
                    pe.wait_ge(h_ready.sem, h_ready.at(n * 2, 0))
                    transpose_rows(ln_T, n * 2)
                    pe.wait_ge(h_ready.sem, h_ready.at(n * 2 + 1, 0))
                    pe.wait_ge(proj_read.sem, proj_read.at(n, 0))
                    for i in range(2 * TB):
                        t, h = divmod(i, 2)
                        w = 3 * C // 2
                        if i >= 4:
                            pe.wait_ge(qkv_ready.sem, qkv_ready.at(n, i - 3))
                        for c in range(NC3):
                            last = mmul(psS[:, i % 4, 0:w], hT[:, c, t * P:(t + 1) * P], w_qkv[:, c, h * w:(h + 1) * w],
                                        start=(c == 0), stop=(c == NC3 - 1))
                        last.then_inc(qkv_mm.sem, 1)
                    for i in range(4):
                        transpose_heads(n, 0, i)
                    for j in range(G):
                        max_scores(n, 0, j)
                        if j >= 2:
                            transpose_heads(n, 1, j - 2)
                    for g, i in SET_ORDER[6:10]:
                        transpose_heads(n, g, i)
                    pe.wait_ge(qkv_ready.sem, qkv_ready.at(n, 2 * TB))
                    for g in range(NG):
                        more = g + 1 < NG
                        for kb in range(TB):
                            scores(n, g, kb, 0)
                            if more:
                                max_scores(n, g + 1, kb, (0, 1))
                            scores(n, g, kb, 1)
                            if more:
                                max_scores(n, g + 1, kb, (2,))
                            if kb:
                                values(n, g, kb - 1)
                            if g + 2 < NG:
                                transpose_heads(n, g + 2, kb)
                            if more:
                                max_scores(n, g + 1, kb, (3,))
                            elif kb == 0:
                                gather_denominators(n)
                            elif kb == 2:
                                spread_reciprocals(n)
                        values(n, g, TB - 1)
                        if more:
                            for i in (4, 5):
                                transpose_heads(n, g + 1, i)
                    last_denominators(n)
                    pe.wait_ge(o_ready.sem, o_ready.at(n, NG))
                    for t in range(TB):
                        for g in range(NG):
                            last = mmul(psS[:, t, 0:C], oT[:, g, t * P:(t + 1) * P], w_proj[:, g, :], start=(g == 0), stop=(g == NG - 1))
                        last.then_inc(proj_mm.sem, 1)
                    pe.wait_ge(ln_xhat.sem, ln_xhat.at(n * 2 + 2, 0))
                    transpose_rows(ln_T, n * 2 + 1)
                    if l == 0:
                        pe.wait_ge(h_ready.sem, h_ready.at(n * 2 + 2, 0))
                        for t in range(TB):
                            for c in range(NC3):
                                last = mmul(psT[:, t * E:(t + 1) * E], hT[:, c, t * P:(t + 1) * P], w_gate[:, c, :],
                                            start=(c == 0), stop=(c == NC3 - 1))
                        last.then_inc(gate_mm.sem, 1)

            def mlp(l, e):
                w1, w2, _, _ = experts[e % 2]
                pe.wait_ge(s_mlpw[WSET[l] + e], 64)
                if e == 0:
                    pe.wait_ge(h2_ready.sem, h2_ready.at(B * (l + 1), 0))
                    pe.wait_ge(proj_read.sem, proj_read.at(B * (l + 1), 0))
                    if l == 0:
                        pe.wait_ge(s_lin, 32)
                with pe.Fori(0, B) as b:
                    q = b + (ITER0[l] + B * e)
                    for m in range(MH):
                        pe.wait_ge(hid_ready.sem, hid_ready.at(q, m - 3))
                        for c in range(NC3):
                            last = mmul(psS[:, m % 4, :], w1[:, c, m * P:(m + 1) * P], h2T[:, c, bass.ds(b * N, N)],
                                        start=(c == 0), stop=(c == NC3 - 1))
                        last.then_inc(f1_mm.sem, 1)
                        if l == 0 and m % 2:
                            j = b * 4 + (16 * e + m // 2)
                            pe.wait_ge(hh_pick.sem, hh_pick.at(j, 1))
                            pe.wait_ge(hh_upd.sem, hh_upd.at(j, 0))
                            mmul(psO[:, 0:C], pick, pT_[:, bass.ds(j, C)], start=True, stop=True).then_inc(hh_mm.sem, 1)
                    for t in range(TB):
                        if t == 0:
                            pe.wait_ge(hid_ready.sem, hid_ready.at(q, MH))
                        pe.wait_ge(f2_read.sem, f2_read.at(q, t - 1))
                        for m in range(MH):
                            last = mmul(psM[:, t % 2, 0:C], hid[:, m, t * P:(t + 1) * P], w2[:, m, :],
                                        start=(m == 0), stop=(m == MH - 1))
                        last.then_inc(f2_mm.sem, 1)

            def rotation():
                def ready(k):
                    pe.wait_ge(s_lin_dve, k)

                e64 = eye[0:D, 0:D]
                pe.wait_ge(hid_ready.sem, hid_ready.at(4 * E, 0))
                ready(4)
                for c in range(NC3):
                    last = nc.tensor.transpose(psS[0:CH, 0, c * D:(c + 1) * D], vT[:, c * CH:(c + 1) * CH], e64)
                last.then_inc(s_lin_pe, 1)
                ready(5)
                for c in range(NC3):
                    last = mmul(psS[0:D, 1, 0:D], v_c[:, c, :], v_c[:, c, :], start=(c == 0), stop=(c == NC3 - 1))
                last.then_inc(s_lin_pe, 1)
                for i in range(6):
                    ready(12 + 4 * i)
                    mmul(psS[0:D, 0, 0:D], lev[:, 1, :], inv[:, 0, :], start=True, stop=True)
                    mmul(psS[0:D, 0, D:2 * D], lev[:, 0, :], inv[:, 1, :], start=True, stop=True).then_inc(s_lin_pe, 1)
                    ready(13 + 4 * i)
                    mmul(psS[0:D, 1, 0:D], inv[:, 1, :], prod[:, 0, :], start=True, stop=True)
                    mmul(psS[0:D, 1, D:2 * D], inv[:, 0, :], prod[:, 1, :], start=True, stop=True).then_inc(s_lin_pe, 1)
                ready(35)
                mmul(psS[0:D, 0, 0:D], tT, vT[:, 0:D], start=True, stop=True).then_inc(s_lin_pe, 1)
                ready(36)
                mmul(psS[0:D, 1, 0:C], zT_, vT, start=True, stop=True).then_inc(s_lin_pe, 1)
                ready(38)
                for c in range(NC3):
                    last = nc.tensor.transpose(psS[0:CH, 0, c * D:(c + 1) * D], uT[:, c * CH:(c + 1) * CH], e64)
                last.then_inc(s_lin_pe, 1)
                ready(42)
                mmul(psS[0:1, 0, 0:D], hs[:, 14:15], e64, start=True, stop=True).then_inc(s_lin_pe, 1)
                ready(43)
                mmul(psS[0:D, 1, 0:1], eye_row, junk[0:1, 0:1], start=True, stop=True).then_inc(s_lin_pe, 1)
                ready(LIN_STEPS)
                ex3 = ex.rearrange("p (i n) -> p i n", n=D)
                xs3 = xs.rearrange("p i (b n) -> p i b n", n=D)
                with pe.Fori(0, TAYLOR) as i:
                    pe.wait_ge(ho_dve.sem, ho_dve.at(i, 0))
                    settle()
                    for k in range(2 * B):
                        last = mmul(psS[0:D, 0, k * D:(k + 1) * D], xs3[:, 1 - k // B, k % B, :], ex3[:, k, :], start=True, stop=True)
                    last.then_inc(ho_mm.sem, 1)
                pe.wait_ge(ho_dve.sem, ho_dve.at(TAYLOR, 0))
                with pe.Fori(0, SQUARINGS) as i:
                    pe.wait_ge(sq_dve.sem, sq_dve.at(i, 0))
                    settle()
                    for k in range(2 * B):
                        last = mmul(psS[0:D, 1, k * D:(k + 1) * D], ex3[:, (k + B) % (2 * B), :], ex3[:, k, :], start=True, stop=True)
                    last.then_inc(sq_mm.sem, 1)
                ready(LIN_STEPS + 1)
                half_e = ex_t.rearrange("p (i n) -> p i n", n=D)
                for b in range(B):
                    last = mmul(psS[0:D, b, 0:C], half_e[:, b, :], uT, start=True, stop=True)
                last.then_inc(s_lin_pe, 1)
                ready(LIN_STEPS + 2)
                pe.wait_ge(x2_ready.sem, x2_ready.at(4 * E, 0))
                with pe.Fori(0, B) as b:
                    pe.wait_ge(rt_h.sem, rt_h.at(b, 0))
                    pe.wait_ge(rt_x.sem, rt_x.at(b, 1))
                    transpose_rows(rt_T, b)
                    pe.wait_ge(rt_zc.sem, rt_zc.at(b, 0))
                    pe.wait_ge(rt_h.sem, rt_h.at(b, NC3))
                    for c in range(NC3):
                        last = mmul(psO[0:D, :], u_c[:, c, :], hT[:, c, :], start=(c == 0), stop=(c == NC3 - 1))
                    last.then_inc(rt_z.sem, 1)
                    pe.wait_ge(rt_zc.sem, rt_zc.at(b, 1))
                    for t in range(TB):
                        pe.wait_ge(rt_add.sem, rt_add.at(b, t - 3))
                        settle()
                        mmul(psS[:, t, 0:C], zT[:, t * P:(t + 1) * P], w_rot[:, b, :], start=True, stop=True).then_inc(rt_mm.sem, 1)

            pe.wait_ge(s_eye, 1)
            mods(0)
            for i in range(8):
                pe.wait_ge(s_skew_w[i % 2], 16 * (i // 2 + 1))
                if i >= 4:
                    pe.wait_ge(s_skew_v, i - 3)
                for c in range(NC3):
                    last = mmul(psS[0:B, i % 4, :], silu[:, c, :], w_skew[i % 2][:, c, :], start=(c == 0), stop=(c == NC3 - 1))
                last.then_inc(s_skew_mm, 1)
            pe.wait_ge(s_skew_v, 8)
            pe.wait_ge(s_init, 4)
            pe.wait_ge(s_start, 80)
            attention(0)
            for e in range(E):
                mlp(0, e)
            rotation()
            mods(1)
            pe.wait_ge(s_init, 6)
            attention(1)
            mlp(1, 0)
            mods(2)
            pe.wait_ge(s_init, 8)
            attention(2)
            mlp(2, 0)


TOP_STEPS = 12
LIN_STEPS = 53


def lay_out(inputs):
    a = {k: np.ascontiguousarray(v) for k, v in inputs.items()}
    out = dict(host_constants())
    out["x"] = a["x"]
    out["cond"] = np.ascontiguousarray(a["cond_1152"].T.reshape(NC3, CH, B).transpose(1, 0, 2))
    names = {
        "L0": ("L0_cond_w_adaln", "L0_cond_b_adaln", "L0_cond_w_qkv", "L0_cond_b_qkv", "L0_cond_w_proj", "L0_cond_b_proj",
               "L0_cond_w1", "L0_cond_b1", "L0_cond_w2", "L0_cond_b2"),
        "L2": ("L2_cond_w_mod", "L2_cond_b_mod", "L2_cond_w_qkv", "L2_cond_b_qkv", "L2_cond_w_proj", "L2_cond_b_proj",
               "L2_cond_w1", "L2_cond_b1", "L2_cond_w2", "L2_cond_b2"),
        "L3": ("L3_cond_W_ada", "L3_cond_b_ada", "L3_cond_W_qkv", "L3_cond_b_qkv", "L3_cond_W_proj", "L3_cond_b_proj",
               "L3_cond_W_fc1", "L3_cond_b_fc1", "L3_cond_W_fc2", "L3_cond_b_fc2"),
    }
    mod_bias = np.zeros((CH, 3, 4 * NC3), np.float32)
    for l, n in enumerate(LAYERS):
        wm, bm, wq, bq, wp, bp, w1, b1, w2, b2 = (a[k] for k in names[n])
        ne = w1.size // (C * HID)
        out[n + "_w_mod"], out[n + "_b_mod"], out[n + "_w_qkv"], out[n + "_b_qkv"] = wm, bm, wq, bq
        pad = np.zeros((NG, G, HP, C), np.float32)
        pad[:, :, 0:HD] = wp.reshape(NG, G, HD, C)
        pad[0, 0, HD] = bp
        out[n + "_w_proj"] = np.ascontiguousarray(pad.transpose(1, 2, 0, 3).reshape(P, NG, C))
        out[n + "_w1"], out[n + "_w2"] = w1.reshape(ne, C, HID), w2.reshape(ne, HID, C)
        out[n + "_b2"] = b2.reshape(ne, C)
        out[n + "_b1"] = np.ascontiguousarray(b1.reshape(ne, MH, P).transpose(0, 2, 1))
        mod_bias[:, l] = bm.reshape(6, NC3, CH)[[0, 1, 3, 4]].reshape(4 * NC3, CH).T
    out["mod_bias"] = mod_bias
    out["w_gate"] = a["L0_cond_w_gate"]
    out["g_q"] = np.tile(a["L2_cond_g_q"], NH)
    out["g_k"] = np.tile(a["L2_cond_g_k"], NH)
    iu, ju = np.triu_indices(D, k=1)
    w = np.zeros((D, D, C), np.float32)
    w[iu, ju] = a["L1_cond_W"]
    w[ju, iu] = a["L1_cond_W"]
    out["w_skew"] = np.ascontiguousarray(w.reshape(D * D, C).T)
    bs = np.zeros((D, D), np.float32)
    bs[iu, ju] = a["L1_cond_b"]
    bs[ju, iu] = a["L1_cond_b"]
    out["b_skew"] = bs.reshape(D * D)
    pT = np.zeros((D, C + D), np.float32)
    pT[:, 0:C] = a["L1_cond_P"].T
    out["pT"] = pT
    return out


def kernel(**inputs):
    import concourse.bacc as bacc
    from concourse.bass_utils import run_bass_kernel_spmd as run

    nc = bacc.Bacc("TRN2", target_bir_lowering=False, num_devices=1)
    arrays = {"in_" + k: v for k, v in lay_out(inputs).items()}
    dram = {k[3:]: nc.dram_tensor(k, v.shape, F32, kind="ExternalInput").ap() for k, v in arrays.items()}
    dram["out"] = nc.dram_tensor("out_x", (B, N, C), F32, kind="ExternalOutput").ap()
    build(nc, dram)
    r = run(nc, [arrays], core_ids=[0])
    return r.results[0]["out_x"]
```

```python
from contextlib import ExitStack

import numpy as np

import concourse.bass as bass
from concourse import mybir

F32 = mybir.dt.float32
BF16 = mybir.dt.bfloat16
ALU = mybir.AluOpType
ACT = mybir.ActivationFunctionType
AX_X = mybir.AxisListType.X

P = 128
B, N, C = 4, 512, 288
TB = N // P
NT = B * TB
CH = 96
NC3 = C // CH
NH, HD = 16, C // 16
G = 4
NG = NH // G
GW = G * HD
HP = 32
HID = 4 * C
MH = HID // P
E = 4
D = 64
LAYERS = ("L0", "L2", "L3")
KM = 6 * HD
KS = KM + 3
SCALE = float(HD) ** -0.5
EPS = 1e-6
TAYLOR = 12
SQUARINGS = 16
SET_ORDER = [(0, 0), (0, 1), (0, 2), (0, 3), (1, 0), (1, 1), (0, 4), (0, 5), (1, 2), (1, 3)]
for _g in range(NG - 1):
    SET_ORDER += [(_g + 2, _i) for _i in range(3) if _g + 2 < NG] + [(_g + 1, 4), (_g + 1, 5)]
    SET_ORDER += [(_g + 2, 3)] if _g + 2 < NG else []
SET_TURN = {_s: _k + 1 for _k, _s in enumerate(SET_ORDER)}
MAX_SLOTS = ((0, 1, 3, 3, 5), (5, 6, 8, 9, 10), (10, 11, 12, 13, 15), (15, 16, 16, 16, 16))
HH_TURN = (6, 6, 4, 0)
HH_START = (0, 24, 48)
CREDIT = 16

A_QKV = 0
A_V = A_QKV + TB * 3 * C * 4
A_KP = A_V + 2 * TB * G * HP * 4
A_QP = A_KP + 2 * TB * G * 112 * 2
A_SPL = A_QP + 2 * TB * G * 112 * 2
A_KT = A_SPL + 2 * (TB * GW * 4 + 2 * TB * GW * 2)
A_QT = A_KT + 3 * G * N * 2
A_PT = A_QT + 3 * G * N * 2
A_OT = A_PT + 2 * G * N * 4
A_RD = A_OT + NG * N * 4
A_END = A_RD + N * 4
M_HID = 0
M_W1 = MH * N * 4
W1_B, W2_B = NC3 * HID * 4, MH * C * 4
W_BYTES = W1_B + W2_B + C * 4 + MH * 4
M_LIN = M_W1 + W_BYTES + 28
M_LIN += -M_LIN % 32
I_WS = M_LIN
I_BS = I_WS + 2 * NC3 * 512 * 4


class Signal:

    def __init__(self, sem, per):
        self.sem, self.per = sem, per

    def at(self, turn, k):
        return turn * self.per + (k + CREDIT)


def ln1_turn(l, b, first):
    return 2 * B * l if first else 2 * b + (2 * B * l - 1)


def ln2_turn(l, b, last):
    return 2 * B * (l + 1) - 1 if last else 2 * b + (2 * B * l + 2)


def host_constants():
    r = np.arange(D)
    eye = np.eye(P, dtype=np.float32)
    gather = np.zeros((P, NG, NH), np.float32)
    for g in range(NG):
        for j in range(G):
            gather[HP * j + HD, g, G * g + j] = 1.0
    spread = np.ascontiguousarray(np.repeat(np.eye(NH, dtype=np.float32), HP, axis=1).reshape(NH, NG, P))
    up, lo = [], []
    b = 1
    while b < D:
        m = ((r[:, None] // (2 * b) == r[None] // (2 * b)) & (r[:, None] // b < r[None] // b))
        up.append(m)
        lo.append(m.T)
        b *= 2
    masks = np.stack(up + lo).transpose(1, 0, 2).astype(np.float32)
    below = -(r[:, None] > r[None]).astype(np.float32)
    from_diagonal = (np.arange(C)[None] >= r[:, None]).astype(np.float32)
    sign = np.where(r[None] > r[:, None], 1.0, -1.0).astype(np.float32)
    halves = np.broadcast_to(2.0 ** -np.arange(SQUARINGS), (D, SQUARINGS)).astype(np.float32)
    over_k = np.broadcast_to(1.0 / np.arange(TAYLOR, 0, -1), (D, TAYLOR)).astype(np.float32)
    e = np.arange(E)
    before = np.broadcast_to((e[None] < e[:, None]).astype(np.float32).reshape(1, E * E), (P, E * E))
    above = (r[:, None] < r[None]).astype(np.float32)
    small = np.concatenate([masks.reshape(D, -1), below, from_diagonal, sign, halves, over_k, above, np.ones((D, D), np.float32)], 1)
    return {"c_eye": eye, "c_gather": gather, "c_spread": spread, "c_before": np.ascontiguousarray(before), "c_small": np.ascontiguousarray(small)}


def build(nc, dram):
    ctx = ExitStack()
    with ctx:
        def sb(name, shape, dt=F32):
            return ctx.enter_context(nc.sbuf_tensor(name, shape, dt))

        def sem(name):
            return ctx.enter_context(nc.semaphore(name))

        signals = {"pe": [], "act": [], "dve": [], "pool": []}

        def signal(owner, name, per):
            s = Signal(sem(name), per)
            signals[owner].append(s)
            return s

        def grant_credit(eng, owner):
            for s in signals[owner]:
                eng.sem_inc(s.sem, CREDIT)

        x = sb("x", [P, NT, C])
        w_qkv = sb("w_qkv", [CH, NC3, 3 * C])
        w_proj = sb("w_proj", [P, NG, C])
        b_qkv = sb("b_qkv", [P, 3 * C])
        g_qk = sb("g_qk", [P, 2 * C])
        gates = sb("gates", [P, B, 2, C])
        xhat = sb("xhat", [P, TB, C])
        hT = sb("hT", [CH, NC3, N])
        h2T = sb("h2T", [CH, NC3, B * N])
        tmp = sb("tmp", [P, 2, C])
        eye = sb("eye", [P, P])
        eye16 = sb("eye16", [P, P], BF16)
        gather = sb("gather", [P, NG, NH])
        spread = sb("spread", [NH, NG, P])
        before = sb("before", [P, E * E])
        w_gate = sb("w_gate", [CH, NC3, E])
        cond = sb("cond", [CH, NC3, B])
        silu = sb("silu", [CH, NC3, B])
        silu_t = sb("silu_t", [CH, NC3, B])
        mod_bias = sb("mod_bias", [CH, 3, 4 * NC3])
        modT = sb("modT", [CH, 4, NC3, B])
        stats = sb("stats", [P, TB, 6])
        meanvar = sb("meanvar", [P, TB, 2])
        var_eps = sb("var_eps", [P, 2, TB])
        rstd = sb("rstd", [P, TB])
        consts = sb("consts", [P, 2 * TB])
        half = sb("half", [D, 1])
        mx = sb("mx", [P, TB * G])
        mrest = sb("mrest", [P, TB * G])
        head_sum = sb("head_sum", [P, TB, 2 * NH])
        head_tmp = sb("head_tmp", [P, TB, 2 * NH])
        head_inv = sb("head_inv", [P, TB, 2 * NH])
        logits = sb("logits", [P, NT, E])
        cw = sb("cw", [P, NT, E])
        A = sb("A", [D, B, D])
        w_a = sb("w_a", [P, W_BYTES // 4])
        arena = sb("arena", [P, A_END // 4])
        assert I_BS + D * D * 4 <= A_END and M_W1 + 6 * C * NC3 * 4 + 2 * C * 4 <= M_LIN

        def at(base, n, dt=F32, p=P):
            a = arena[0:p, base // 4:base // 4 + (n * (2 if dt == BF16 else 4) + 3) // 4]
            return a.bitcast(BF16) if dt == BF16 else a

        qkv = at(A_QKV, TB * 3 * C).rearrange("p (t c) -> p t c", t=TB)
        vg = [at(A_V + i * TB * G * HP * 4, TB * G * HP).rearrange("p (t c) -> p t c", t=TB) for i in range(2)]
        kp = [at(A_KP + i * TB * G * 224, TB * G * 112, BF16).rearrange("p (h c) -> p h c", c=112) for i in range(2)]
        qp = [at(A_QP + i * TB * G * 224, TB * G * 112, BF16).rearrange("p (h c) -> p h c", c=112) for i in range(2)]
        SPL = TB * GW * 8
        rest = [at(A_SPL + i * SPL, TB * GW) for i in range(2)]
        part_h = [at(A_SPL + i * SPL + TB * GW * 4, TB * GW, BF16) for i in range(2)]
        part_m = [at(A_SPL + i * SPL + TB * GW * 6, TB * GW, BF16) for i in range(2)]
        kT = [at(A_KT + i * G * N * 2, G * N, BF16).rearrange("p (h n) -> p h n", h=G) for i in range(3)]
        qT = [at(A_QT + i * G * N * 2, G * N, BF16).rearrange("p (h n) -> p h n", h=G) for i in range(3)]
        pT = at(A_PT, 2 * G * N).rearrange("p (i n) -> p i n", i=2)
        oT = at(A_OT, NG * N).rearrange("p (g n) -> p g n", g=NG)
        rD = at(A_RD, N, p=NH)
        hid = at(M_HID, MH * N).rearrange("p (m n) -> p m n", m=MH)
        top = at(M_HID, 6 * NT * E * E)

        def expert(flat):
            o = NC3 * HID
            return (flat[0:CH, 0:o].rearrange("p (c n) -> p c n", c=NC3),
                    flat[:, o:o + MH * C].rearrange("p (m n) -> p m n", m=MH),
                    flat[:, o + MH * C:o + MH * C + C], flat[:, o + MH * C + C:o + MH * C + C + MH])

        experts = [expert(w_a[:, :]), expert(at(M_W1, W_BYTES // 4))]
        w_mod = at(M_W1, NC3 * 6 * C, p=CH).rearrange("p (c n) -> p c n", c=NC3)
        gate_bias = at(M_W1 + NC3 * 6 * C * 4, 2 * C).rearrange("p (i n) -> p i n", i=2)
        silu_b = at(M_HID, NC3 * B * P, p=CH).rearrange("p (i n) -> p i n", n=P)
        w_skew = [at(I_WS + i * NC3 * 2048, NC3 * 512, p=CH).rearrange("p (c n) -> p c n", c=NC3) for i in range(2)]
        b_skew = at(I_BS, D * D, p=B)
        v_skew = h2T[0:B, :, :].rearrange("p c n -> p (c n)")[:, 0:D * D]

        lin_at = [M_LIN]

        def lin(n, p=D):
            a = at(lin_at[0], n, p=p)
            lin_at[0] += n * 4 + (-n * 4) % 32
            assert lin_at[0] <= A_END
            return a

        small = lin(16 * D + C + SQUARINGS + TAYLOR)
        o = 12 * D
        level_masks = small[:, 0:o].rearrange("p (l n) -> p l n", l=12)
        below = small[:, o:o + D]
        from_diag = small[:, o + D:o + D + C]
        sign = small[:, o + D + C:o + 2 * D + C]
        halves = small[:, o + 2 * D + C:o + 2 * D + C + SQUARINGS]
        over_k = small[:, o + 2 * D + C + SQUARINGS:o + 2 * D + C + SQUARINGS + TAYLOR]
        o += 2 * D + C + SQUARINGS + TAYLOR
        above = small[:, o:o + D]
        eye_row = small[0:1, o + D:o + 2 * D]
        pick = lin(P)
        pT_ = lin(C + D)
        vb = lin(C)
        junk = lin(C)
        hs = lin(16)
        nbs = lin(D)
        cs = lin(D)
        uT = lin(C)
        vT = lin(C)
        inv = lin(2 * D).rearrange("p (i n) -> p i n", i=2)
        lev = lin(2 * D).rearrange("p (i n) -> p i n", i=2)
        mm = lin(2 * D).rearrange("p (i n) -> p i n", i=2)
        prod = lin(2 * D).rearrange("p (i n) -> p i n", i=2)
        tT = lin(D)
        zT_ = lin(D)
        v_c = lin(NC3 * D, p=CH).rearrange("p (c n) -> p c n", c=NC3)
        u_c = lin(NC3 * D, p=CH).rearrange("p (c n) -> p c n", c=NC3)
        xs = lin(2 * B * D).rearrange("p (i n) -> p i n", i=2)
        ex = lin(2 * B * D)
        ex_t = lin(2 * B * D)
        flags = lin(SQUARINGS + 8)
        w_rot = lin(B * C).rearrange("p (b n) -> p b n", b=B)
        zT = lin(2 * N).rearrange("p (i n) -> p i n", i=2)

        psS = ctx.enter_context(nc.psum_tensor("psS", [P, 4, 512], F32))
        psM = ctx.enter_context(nc.psum_tensor("psM", [P, 2, 512], F32))
        psO = ctx.enter_context(nc.psum_tensor("psO", [P, 512], F32))
        psT = ctx.enter_context(nc.psum_tensor("psT", [P, 512], F32))
        banks3 = [psT[:, :], psM[:, 0, :], psM[:, 1, :]]
        banksS = [psS[:, c, :] for c in range(NC3)]
        banks_16 = [b.bitcast(BF16) for b in (*banks3, psO[:, :])]

        def set_bank(g, i):
            if g == 0 or i > 3:
                return (0, 1, 2, 0, 1, 2)[i]
            return 3 * (i % 2) if g == 1 else 0

        scratch = nc.dram_tensor("skew_scratch", [B, D * D], F32, kind="Internal").ap()

        s_const = sem("constants_loaded")
        s_start = sem("start_inputs_loaded")
        s_x = sem("x_loaded")
        s_attw = [sem(f"attention_weights_loaded_{l}") for l in range(3)]
        s_modw = [sem(f"mod_weights_loaded_{l}") for l in range(3)]
        s_mlpw = [sem(f"expert_weights_loaded_{q}") for q in range(E + 2)]
        s_skew_w = [sem(f"skew_weights_loaded_{i}") for i in range(2)]
        s_skew_b = sem("skew_bias_loaded")
        s_skew_out = sem("skew_stored")
        s_skew_in = sem("skew_loaded")
        s_lin = sem("rotation_inputs_loaded")
        s_out = sem("output_stored")
        s_init = sem("constant_tiles_set")
        s_exp0 = sem("silu_exp_done")
        s_silu = sem("silu_ready")
        s_silu_b = sem("silu_spread")
        s_skew_mm = sem("skew_product_done")
        s_skew_v = sem("skew_rows_ready")
        s_mod_mm = sem("mod_product_done")
        s_mod = sem("mod_ready")
        s_top = sem("top2_steps")
        s_top_exp = sem("top2_exp_done")
        s_top_in = sem("top2_exp_asked")
        s_modstep = sem("mod_steps")
        s_passed_pool = sem("pool_waits_passed")
        s_passed_dve = sem("vector_waits_passed")
        s_passed_pe = sem("tensor_waits_passed")
        s_passed_act = sem("scalar_waits_passed")
        s_eye = sem("eye16_and_silu_steps")
        s_lin_dve = sem("rotation_vector_steps")
        s_lin_pe = sem("rotation_products")
        s_norm_dve = sem("skew_norm_steps")
        s_norm_pe = sem("skew_norm_moved")

        ln_stats = signal("dve", "ln_stats", TB)
        ln_mv = signal("dve", "ln_meanvar", TB)
        ln_eps = signal("pool", "ln_var_eps", 1)
        ln_rstd = signal("pool", "ln_rstd", 1)
        ln_xhat = signal("dve", "ln_normalised", TB)
        ln_T = signal("pe", "ln_transposed", NC3)
        h_ready = signal("act", "modulated", NC3)
        h2_ready = signal("act", "mlp_input_kept", 1)
        qkv_mm = signal("pe", "qkv_product", 2 * TB)
        qkv_ready = signal("dve", "qkv_ready", 2 * TB)
        qkn = signal("dve", "qk_norm_steps", 5 * TB + 7)
        qkn_root = signal("act", "qk_deviation", 1)
        split_step = signal("dve", "split_steps", 6 * NG)
        split_ready = signal("dve", "split_ready", 2 * NG)
        rep_first = signal("act", "first_parts_stacked", 2)
        rep_done = signal("pool", "parts_stacked", 2 * NG - 2)
        v_staged = signal("pool", "v_staged", NG)
        t_mm = signal("pe", "heads_transposed", 6 * NG)
        t_ev = signal("act", "heads_copied", 6 * NG)
        max_mm = signal("pe", "max_scores", 16 * NG)
        max_done = signal("dve", "max_taken", 16 * NG)
        mparts = signal("dve", "max_split_steps", 3 * NG)
        m_ready = signal("dve", "max_parts_ready", NG)
        s_mm = signal("pe", "scores_ready", 8 * NG)
        exp_done = signal("act", "exp_done", 8 * NG)
        av_done = signal("pe", "values_summed", 4 * NG)
        o_raw = signal("dve", "sums_copied", NG)
        d_mm = signal("pe", "denominators_moved", NG + 1)
        recip = signal("dve", "denominators_inverted", 1)
        o_ready = signal("dve", "heads_ready", NG)
        proj_mm = signal("pe", "projected", TB)
        proj_read = signal("dve", "projection_gated", TB)
        x1_ready = signal("dve", "x_after_attention", TB)
        gate_mm = signal("pe", "gate_product", 1)
        gate_read = signal("dve", "gate_logits_kept", 1)
        f1_mm = signal("pe", "hidden_product", MH)
        hid_ready = signal("act", "hidden_ready", MH)
        f2_mm = signal("pe", "mlp_product", TB)
        f2_read = signal("dve", "mlp_bias_added", TB)
        f2_scaled = signal("dve", "mlp_gated", TB)
        x2_ready = signal("dve", "x_after_mlp", TB)
        hh_pick = signal("pool", "householder_row_picked", 1)
        hh_mm = signal("pe", "householder_column_spread", 1)
        hh_step = signal("dve", "householder_steps", 11)
        hh_nrm2 = signal("dve", "householder_norm2", 1)
        hh_nrm = signal("pool", "householder_norm", 1)
        hh_w = signal("dve", "householder_weights", 1)
        hh_upd = signal("dve", "householder_applied", 1)
        ho_mm = signal("pe", "series_product", 1)
        ho_dve = signal("dve", "series_term_added", 1)
        sq_mm = signal("pe", "square_product", 1)
        sq_t = signal("dve", "square_difference", 1)
        sq_dve = signal("dve", "square_taken", 1)
        rt_T = signal("pe", "rotation_x_transposed", NC3)
        rt_h = signal("act", "rotation_xT_copied", NC3)
        rt_z = signal("pe", "rotation_z", 1)
        rt_zc = signal("dve", "rotation_z_copied", 1)
        rt_mm = signal("pe", "rotation_product", TB)
        rt_add = signal("dve", "rotation_added", TB)

        ITER0 = (0, 4 * E, 4 * E + 4)
        NE = (E, 1, 1)
        WSET = (0, E, E + 1)

        def stacked(part, parts, g, i, slots):
            src = part[i].rearrange("p (h c) -> p h c", c=HD)
            dst = parts[g % 2][:, :, 0:KM].rearrange("p h (s c) -> p h s c", c=HD)[:, :, slots, :]
            return dst, src.unsqueeze(2).to_broadcast([P, TB * G, dst.shape[2], HD])

        HIGH_SLOTS = (slice(0, 3), slice(1, 6, 2))
        MIDDLE_SLOTS = (slice(3, 5), slice(2, 5, 2))

        block = ctx.enter_context(nc.Block())

        @block.sync
        def _(sp):
            def load_attention(l):
                n = LAYERS[l]
                sp.dma_start(w_qkv[:, :, :], dram[n + "_w_qkv"].rearrange("(c p) n -> p c n", p=CH)).then_inc(s_attw[l], 16)
                sp.dma_start(w_proj[:, :, :], dram[n + "_w_proj"]).then_inc(s_attw[l], 16)
                sp.dma_start(b_qkv[:, :], dram[n + "_b_qkv"].partition_broadcast(P)).then_inc(s_attw[l], 16)

            def load_mod(l):
                n = LAYERS[l]
                sp.dma_start(w_mod, dram[n + "_w_mod"].rearrange("(c p) n -> p c n", p=CH)).then_inc(s_modw[l], 16)
                for i, k in ((0, 2), (1, 5)):
                    sp.dma_start(gate_bias[:, i, :], dram[n + "_b_mod"][k * C:(k + 1) * C].partition_broadcast(P)).then_inc(s_modw[l], 16)

            def load_expert(l, e):
                n, q = LAYERS[l], WSET[l] + e
                w1, w2, b2, b1 = experts[e % 2]
                sp.dma_start(w1, dram[n + "_w1"][e].rearrange("(c p) n -> p c n", p=CH)).then_inc(s_mlpw[q], 16)
                sp.dma_start(w2, dram[n + "_w2"][e].rearrange("(m p) n -> p m n", p=P)).then_inc(s_mlpw[q], 16)
                sp.dma_start(b2, dram[n + "_b2"][e].partition_broadcast(P)).then_inc(s_mlpw[q], 16)
                sp.dma_start(b1, dram[n + "_b1"][e]).then_inc(s_mlpw[q], 16)

            sp.dma_start(cond[:, :, :], dram["cond"]).then_inc(s_start, 16)
            sp.dma_start(mod_bias[:, :, :], dram["mod_bias"]).then_inc(s_start, 16)
            sp.dma_start(eye[:, :], dram["c_eye"]).then_inc(s_const, 16)
            sp.dma_start(before[:, :], dram["c_before"]).then_inc(s_const, 16)
            sp.dma_start(gather[:, :, :], dram["c_gather"]).then_inc(s_const, 16)
            sp.dma_start(spread[:, :, :], dram["c_spread"]).then_inc(s_const, 16)
            load_mod(0)
            sp.dma_start(x[:, :, :], dram["x"].rearrange("b (t p) c -> p (b t) c", p=P)).then_inc(s_x, 16)
            load_attention(0)
            sp.dma_start(b_skew, dram["b_skew"].partition_broadcast(B)).then_inc(s_skew_b, 16)
            for i in range(8):
                if i >= 2:
                    sp.wait_ge(s_skew_mm, i - 1)
                sp.dma_start(w_skew[i % 2], dram["w_skew"][:, i * 512:(i + 1) * 512].rearrange("(c p) n -> p c n", p=CH)).then_inc(s_skew_w[i % 2], 16)
            load_expert(0, 0)
            sp.dma_start(w_gate[:, :, :], dram["w_gate"].rearrange("(c p) n -> p c n", p=CH)).then_inc(s_start, 16)
            sp.dma_start(g_qk[:, 0:C], dram["g_q"].partition_broadcast(P)).then_inc(s_start, 16)
            sp.dma_start(g_qk[:, C:2 * C], dram["g_k"].partition_broadcast(P)).then_inc(s_start, 16)
            sp.wait_ge(s_skew_v, 8)
            sp.dma_start(scratch, v_skew).then_inc(s_skew_out, 16)
            sp.wait_ge(s_skew_out, 16)
            sp.dma_start(A[:, :, :], scratch.rearrange("b (i j) -> i b j", j=D)).then_inc(s_skew_in, 16)
            sp.wait_ge(proj_mm.sem, proj_mm.at(B, 0))
            load_expert(0, 1)
            sp.dma_start(small, dram["c_small"]).then_inc(s_lin, 16)
            sp.dma_start(pT_, dram["pT"]).then_inc(s_lin, 16)
            load_attention(1)
            sp.wait_ge(f2_mm.sem, f2_mm.at(4, 0))
            sp.wait_ge(x2_ready.sem, x2_ready.at(4, 0))
            load_expert(0, 2)
            sp.wait_ge(f2_mm.sem, f2_mm.at(8, 0))
            sp.wait_ge(x2_ready.sem, x2_ready.at(8, 0))
            load_expert(0, 3)
            sp.wait_ge(f2_mm.sem, f2_mm.at(12, 0))
            sp.wait_ge(x2_ready.sem, x2_ready.at(12, 0))
            load_expert(1, 0)
            sp.wait_ge(f2_mm.sem, f2_mm.at(16, 0))
            sp.wait_ge(x2_ready.sem, x2_ready.at(16, 0))
            load_mod(1)
            sp.wait_ge(proj_mm.sem, proj_mm.at(2 * B, 0))
            load_attention(2)
            load_mod(2)
            sp.wait_ge(f2_mm.sem, f2_mm.at(20, 0))
            sp.wait_ge(x2_ready.sem, x2_ready.at(20, 0))
            load_expert(2, 0)
            for b in range(B):
                sp.wait_ge(x2_ready.sem, x2_ready.at(21 + b, 0))
                sp.dma_start(dram["out"][b].rearrange("(t p) c -> p t c", p=P), x[:, TB * b:TB * (b + 1), :]).then_inc(s_out, 16)
            sp.wait_ge(s_out, 16 * B)

        @block.gpsimd
        def _(pool):
            grant_credit(pool, "pool")
            def settle():
                pool.sem_inc(s_passed_pool, 1)

            nc.gpsimd.memset(consts[:, 0:TB], -0.5)
            nc.gpsimd.memset(consts[:, TB:2 * TB], EPS)
            nc.gpsimd.memset(half[:, :], 0.5)
            nc.gpsimd.memset(var_eps[:, 1, :], EPS).then_inc(s_init, 2)
            pool.wait_ge(s_init, 2)

            def ln_root(m):
                pool.wait_ge(ln_mv.sem, ln_mv.at(m, TB))
                nc.gpsimd.tensor_tensor(var_eps[:, 0, :], meanvar[:, :, 1], consts[:, TB:2 * TB], ALU.add).then_inc(ln_eps.sem, 1)
                pool.wait_ge(ln_eps.sem, ln_eps.at(m, 1))
                pool.wait_ge(ln_xhat.sem, ln_xhat.at(m, 0))
                nc.gpsimd.tensor_tensor(rstd[:, :], var_eps[:, 0, :], consts[:, 0:TB], ALU.pow).then_inc(ln_rstd.sem, 1)

            def spread_silu(l):
                if l:
                    pool.wait_ge(f2_mm.sem, f2_mm.at(ITER0[l], 0))
                nc.gpsimd.tensor_copy(silu_b, silu[:, :, :].rearrange("p c b -> p (c b)").unsqueeze(2).to_broadcast([CH, NC3 * B, P])).then_inc(s_silu_b, 1)

            def stack(n, g, i):
                pool.wait_ge(split_ready.sem, split_ready.at(n, 2 * g + i + 1))
                settle()
                nc.gpsimd.tensor_copy(*stacked(part_h, (kp, qp)[i], g, i, HIGH_SLOTS[i]))
                nc.gpsimd.tensor_copy(*stacked(part_m, (kp, qp)[i], g, i, MIDDLE_SLOTS[i])).then_inc(rep_done.sem, 1)

            def stage_values(n, g):
                if g == 0:
                    pool.wait_ge(qkv_ready.sem, qkv_ready.at(n, 2 * TB))
                pool.wait_ge(av_done.sem, av_done.at(n, 4 * (g - 1)))
                settle()
                nc.gpsimd.tensor_copy(
                    vg[g % 2].rearrange("p t (h c) -> p t h c", c=HP)[:, :, :, 0:HD],
                    qkv[:, :, 2 * C + g * GW:2 * C + (g + 1) * GW].rearrange("p t (h c) -> p t h c", c=HD)).then_inc(v_staged.sem, 1)

            def open_batch(n):
                stack(n, 1, 0)
                stack(n, 1, 1)
                stage_values(n, 0)
                stage_values(n, 1)

            def batch(l, b, last):
                n = b + l * B
                stack(n, 2, 0)
                for g in range(2, NG):
                    stack(n, g, 1)
                    if g + 1 < NG:
                        stack(n, g + 1, 0)
                    stage_values(n, g)
                if not last:
                    ln_root(ln1_turn(l, b + 1, False))
                    open_batch(n + 1)
                ln_root(ln2_turn(l, b, last))

            def attention(l):
                open_batch(l * B)
                with pool.Fori(0, B - 1) as b:
                    batch(l, b, False)
                batch(l, B - 1, True)

            pool.wait_ge(s_silu, 1)
            spread_silu(0)

            def set_stage_constants(l):
                ln_root(ln1_turn(l, 0, True))
                pool.wait_ge(s_mod, 9 * (l + 1))
                if l == 0:
                    pool.wait_ge(s_skew_v, 8)
                for i in range(2):
                    v = vg[i].rearrange("p t (h c) -> p (t h) c", c=HP)
                    nc.gpsimd.memset(v[:, :, HD:HD + 1], 1.0)
                    nc.gpsimd.memset(v[:, :, HD + 1:HP], 0.0)
                    nc.gpsimd.memset(kp[i][:, :, KM:KS], 1.0).then_inc(s_init, 1)

            set_stage_constants(0)
            pool.wait_ge(s_skew_out, 16)
            attention(0)
            pool.wait_ge(s_const, 64)
            pool.wait_ge(x1_ready.sem, x1_ready.at(B, 0))
            pool.wait_ge(o_ready.sem, o_ready.at(B, 0))
            with pool.Fori(0, D) as j:
                pool.wait_ge(hh_mm.sem, hh_mm.at(j, 0))
                settle()
                nc.gpsimd.tensor_copy(pick[:, :], eye[0:D, bass.ds(j, 1)].to_broadcast([D, P])).then_inc(hh_pick.sem, 1)
                pool.wait_ge(hh_nrm2.sem, hh_nrm2.at(j, 1))
                nc.gpsimd.tensor_tensor(hs[:, 2:3], hs[:, 1:2], half[:, :], ALU.pow).then_inc(hh_nrm.sem, 1)
            spread_silu(1)
            set_stage_constants(1)
            attention(1)
            spread_silu(2)
            set_stage_constants(2)
            attention(2)

        @block.scalar
        def _(act):
            grant_credit(act, "act")

            def modulate(m, b, kind, banks):
                for c in range(NC3):
                    act.wait_ge(ln_T.sem, ln_T.at(m, c + 1))
                    nc.scalar.activation(hT[:, c, :], banks[c][0:CH, :], ACT.Identity,
                                         bias=modT[:, kind, c, bass.ds(b, 1)],
                                         scale=modT[:, kind + 1, c, bass.ds(b, 1)]).then_inc(h_ready.sem, 1)

            def copy_heads(n, g, i):
                rows = KM if i in (2, 3) else KS
                dst = (kT if i < 2 else qT)[g % 3]
                act.wait_ge(t_mm.sem, t_mm.at(n, SET_TURN[g, i]))
                h = i % 2
                nc.scalar.activation(dst[0:rows, 2 * h:2 * h + 2, :],
                                     banks_16[set_bank(g, i)][0:rows, :].rearrange("p (h n) -> p h n", h=2),
                                     ACT.Copy).then_inc(t_ev.sem, 1)

            def first_group(l, n, b):
                if l == 1:
                    act.wait_ge(qkn.sem, qkn.at(b, 5 * TB + 1))
                    nc.scalar.activation(head_inv[:, :, :], head_tmp[:, :, :], ACT.Sqrt).then_inc(qkn_root.sem, 1)
                for i in range(2):
                    act.wait_ge(split_ready.sem, split_ready.at(n, i + 1))
                    for part, slots in ((part_h, HIGH_SLOTS[i]), (part_m, MIDDLE_SLOTS[i])):
                        last = nc.scalar.activation(*stacked(part, (kp, qp)[i], 0, i, slots), ACT.Copy)
                    last.then_inc(rep_first.sem, 1)
                for g, i in SET_ORDER[0:4]:
                    copy_heads(n, g, i)

            def batch(l, b, last):
                n = b + l * B
                for g in range(NG):
                    if g == NG - 1 and not last:
                        act.wait_ge(h2_ready.sem, h2_ready.at(n, 0))
                        modulate(ln1_turn(l, b + 1, False), b + 1, 0, banks3)
                    for kb in range(TB):
                        for h in range(2):
                            if h == 0:
                                act.wait_ge(av_done.sem, av_done.at(n, 4 * g + kb - 1))
                            act.wait_ge(s_mm.sem, s_mm.at(n, 8 * g + 2 * kb + h + 1))
                            nc.scalar.activation(pT[:, kb % 2, 1024 * h:1024 * (h + 1)],
                                                 psS[:, 2 * h:2 * h + 2, :].rearrange("p a n -> p (a n)"),
                                                 ACT.Exp, scale=SCALE).then_inc(exp_done.sem, 1)
                        if g + 2 < NG and kb < 3:
                            copy_heads(n, g + 2, kb)
                    if g + 1 < NG:
                        for i in (4, 5):
                            copy_heads(n, g + 1, i)
                    if g + 2 < NG:
                        copy_heads(n, g + 2, 3)
                if not last:
                    first_group(l, n + 1, b + 1)
                    for g, i in SET_ORDER[4:10]:
                        copy_heads(n + 1, g, i)
                m = ln2_turn(l, b, last)
                modulate(m, b, 2, banksS)
                act.wait_ge(h_ready.sem, h_ready.at(m + 1, 0))
                act.sem_inc(s_passed_act, 1)
                nc.scalar.activation(h2T[:, :, bass.ds(b * N, N)], hT[:, :, :], ACT.Copy).then_inc(h2_ready.sem, 1)

            def attention(l):
                n = l * B
                act.wait_ge(h2_ready.sem, h2_ready.at(n, 0))
                modulate(ln1_turn(l, 0, True), 0, 0, banks3)
                first_group(l, n, 0)
                for g, i in SET_ORDER[4:10]:
                    copy_heads(n, g, i)
                with act.Fori(0, B - 1) as b:
                    batch(l, b, False)
                batch(l, B - 1, True)

            def mlp(l, e):
                b1 = experts[e % 2][3]
                act.wait_ge(s_mlpw[WSET[l] + e], 64)
                with act.Fori(0, B) as b:
                    q = b + (ITER0[l] + B * e)
                    for m in range(MH):
                        if m == 0:
                            act.wait_ge(f2_mm.sem, f2_mm.at(q, 0))
                        act.wait_ge(f1_mm.sem, f1_mm.at(q, m + 1))
                        nc.scalar.activation(hid[:, m, :], psS[:, m % 4, :], ACT.Gelu_apprx_tanh,
                                             bias=b1[:, m:m + 1]).then_inc(hid_ready.sem, 1)

            act.wait_ge(s_start, 32)
            nc.scalar.activation(silu_t[:, :, :], cond[:, :, :], ACT.Exp, scale=-1.0).then_inc(s_exp0, 1)
            act.wait_ge(s_mod, 9)
            attention(0)
            act.wait_ge(s_top_in, 1)
            nc.scalar.activation(top[:, 0:NT * E], top[:, 0:NT * E], ACT.Exp).then_inc(s_top_exp, 1)
            act.wait_ge(s_top, TOP_STEPS)
            for e in range(E):
                mlp(0, e)
            for b in range(B):
                for c in range(NC3):
                    act.wait_ge(rt_T.sem, rt_T.at(b, c + 1))
                    nc.scalar.activation(h2T[:, c, b * N:(b + 1) * N], banks3[c][0:CH, :], ACT.Copy).then_inc(rt_h.sem, 1)
            act.wait_ge(s_mod, 18)
            attention(1)
            act.wait_ge(o_ready.sem, o_ready.at(2 * B, 0))
            mlp(1, 0)
            act.wait_ge(s_mod, 27)
            attention(2)
            act.wait_ge(o_ready.sem, o_ready.at(3 * B, 0))
            mlp(2, 0)

        @block.vector
        def _(dve):
            grant_credit(dve, "dve")
            v = nc.vector
            def settle():
                dve.sem_inc(s_passed_dve, 1)

            def ln_sums(b, t):
                v.bn_stats(stats[:, t, :], x[:, b * TB + t, :]).then_inc(ln_stats.sem, 1)

            def ln_moments(m, b, sums=True):
                for t in range(TB):
                    if sums:
                        ln_sums(b, t)
                for t in range(TB):
                    dve.wait_ge(ln_stats.sem, ln_stats.at(m, t + 1))
                    settle()
                    v.bn_aggr(meanvar[:, t, :], stats[:, t, :]).then_inc(ln_mv.sem, 1)

            def first_rows(l):
                ln_moments(ln1_turn(l, 0, True), 0)
                ln_apply(ln1_turn(l, 0, True), 0)

            def ln_apply(m, b):
                dve.wait_ge(ln_T.sem, ln_T.at(m, 0))
                dve.wait_ge(ln_rstd.sem, ln_rstd.at(m, 1))
                for t in range(TB):
                    v.tensor_scalar(xhat[:, t, :], x[:, b * TB + t, :], meanvar[:, t, 0:1], rstd[:, t:t + 1],
                                    ALU.subtract, ALU.mult).then_inc(ln_xhat.sem, 1)

            def qk_center(b, t):
                heads = qkv[:, t, 0:2 * C].rearrange("p (h c) -> p h c", c=HD)
                squares = xhat[:, 2 * (t % 2):2 * (t % 2) + 2, :].rearrange("p i c -> p (i c)")

                def step(ins, k):
                    ins.then_inc(qkn.sem, 1)
                    dve.wait_ge(qkn.sem, qkn.at(b, 5 * t + k))

                step(v.tensor_reduce(head_sum[:, t, :], heads, AX_X, ALU.add), 1)
                step(v.scalar_tensor_tensor(out=heads, in0=head_sum[:, t, :].unsqueeze(2).to_broadcast([P, 2 * NH, HD]),
                                            scalar=-1.0 / HD, in1=heads, op0=ALU.mult, op1=ALU.add), 2)
                step(v.tensor_tensor(squares, qkv[:, t, 0:2 * C], qkv[:, t, 0:2 * C], ALU.mult), 3)
                step(v.tensor_reduce(head_tmp[:, t, :], squares.rearrange("p (h c) -> p h c", c=HD), AX_X, ALU.add), 4)
                step(v.tensor_tensor(qkv[:, t, 0:2 * C], qkv[:, t, 0:2 * C], g_qk[:, :], ALU.mult), 5)

            def qk_variance(b):
                v.tensor_scalar(head_tmp[:, :, :], head_tmp[:, :, :], 1.0 / HD, EPS, ALU.mult, ALU.add).then_inc(qkn.sem, 1)

            def qk_scale(b):
                heads = qkv[:, :, 0:2 * C].rearrange("p t (h c) -> p t h c", c=HD)

                def step(ins, k):
                    ins.then_inc(qkn.sem, 1)
                    dve.wait_ge(qkn.sem, qkn.at(b, 5 * TB + k))

                dve.wait_ge(qkn_root.sem, qkn_root.at(b, 1))
                step(v.reciprocal(head_inv[:, :, :], head_inv[:, :, :]), 2)
                step(v.tensor_tensor(head_tmp[:, :, :], head_tmp[:, :, :], head_inv[:, :, :], ALU.mult), 3)
                step(v.tensor_tensor(head_tmp[:, :, :], head_tmp[:, :, :], head_inv[:, :, :], ALU.mult), 4)
                step(v.tensor_scalar(head_tmp[:, :, :], head_tmp[:, :, :], -0.5, 1.5, ALU.mult, ALU.add), 5)
                step(v.tensor_tensor(head_inv[:, :, :], head_tmp[:, :, :], head_inv[:, :, :], ALU.mult), 6)
                for t in range(TB):
                    last = v.tensor_tensor(heads[:, t], heads[:, t],
                                           head_inv[:, t, :].unsqueeze(2).to_broadcast([P, 2 * NH, HD]), ALU.mult)
                step(last, 7)

            def split(n, g, i):
                parts, col, low = ((kp, C, 5), (qp, 0, 0))[i]
                src = qkv[:, :, col + g * GW:col + (g + 1) * GW]
                r = rest[i].rearrange("p (t c) -> p t c", t=TB)
                h = part_h[i].rearrange("p (t c) -> p t c", t=TB)
                k0 = 6 * g + 3 * i
                if g == 1:
                    dve.wait_ge(rep_first.sem, rep_first.at(n, i + 1))
                else:
                    dve.wait_ge(rep_done.sem, rep_done.at(n, 2 * (g - 2) + i + 1 if g else 0))
                v.tensor_copy(h, src).then_inc(split_step.sem, 1)
                dve.wait_ge(split_step.sem, split_step.at(n, k0 + 1))
                v.tensor_tensor(r, src, h, ALU.subtract).then_inc(split_step.sem, 1)
                dve.wait_ge(split_step.sem, split_step.at(n, k0 + 2))
                v.tensor_copy(part_m[i], rest[i]).then_inc(split_step.sem, 1)
                dve.wait_ge(t_mm.sem, t_mm.at(n, SET_TURN[g - 2, 5 if i else 1] if g >= 2 else 0))
                dve.wait_ge(split_step.sem, split_step.at(n, k0 + 3))
                v.tensor_tensor(parts[g % 2][:, :, low * HD:(low + 1) * HD], rest[i].rearrange("p (h c) -> p h c", c=HD),
                                part_m[i].rearrange("p (h c) -> p h c", c=HD), ALU.subtract).then_inc(split_ready.sem, 1)

            def maxima(n, g, heads=range(G)):
                for j in heads:
                    if j == 2 and 0 < g < NG - 2:
                        split(n, g + 2, 0)
                    for t in range(TB):
                        i = 16 * g + 4 * j + t
                        dve.wait_ge(max_mm.sem, max_mm.at(n, i + 1))
                        v.tensor_reduce(mx[:, t * G + j:t * G + j + 1], psM[:, t % 2, :], AX_X, ALU.max).then_inc(max_done.sem, 1)
                if heads[-1] < G - 1:
                    return
                neg = [qp[g % 2][:, :, KM + i] for i in range(3)]
                dve.wait_ge(max_done.sem, max_done.at(n, 16 * (g + 1)))
                v.tensor_scalar(neg[0], mx[:, :], -1.0, None, ALU.mult).then_inc(mparts.sem, 1)
                dve.wait_ge(mparts.sem, mparts.at(n, 3 * g + 1))
                v.scalar_tensor_tensor(out=mrest[:, :], in0=mx[:, :], scalar=-1.0, in1=neg[0], op0=ALU.mult,
                                       op1=ALU.subtract).then_inc(mparts.sem, 1)
                dve.wait_ge(mparts.sem, mparts.at(n, 3 * g + 2))
                v.tensor_copy(neg[1], mrest[:, :]).then_inc(mparts.sem, 1)
                dve.wait_ge(mparts.sem, mparts.at(n, 3 * g + 3))
                v.tensor_tensor(neg[2], mrest[:, :], neg[1], ALU.subtract).then_inc(m_ready.sem, 1)

            def keep_sums(n, g):
                if g == 0:
                    dve.wait_ge(proj_mm.sem, proj_mm.at(n, 0))
                dve.wait_ge(av_done.sem, av_done.at(n, 4 * g + 4))
                v.tensor_copy(oT[:, g, :], psO[:, :]).then_inc(o_raw.sem, 1)

            def divide(n):
                dve.wait_ge(d_mm.sem, d_mm.at(n, 1))
                v.reciprocal(rD, psS[0:NH, 0, :]).then_inc(recip.sem, 1)
                for g in range(NG):
                    dve.wait_ge(d_mm.sem, d_mm.at(n, 2 + g))
                    v.tensor_tensor(oT[:, g, :], oT[:, g, :], psS[:, (g + 1) % 4, :], ALU.mult).then_inc(o_ready.sem, 1)

            def take_qkv(l, n, b):
                dve.wait_ge(v_staged.sem, v_staged.at(n, 0))
                for i in range(2 * TB):
                    t, h = divmod(i, 2)
                    w = 3 * C // 2
                    dve.wait_ge(qkv_mm.sem, qkv_mm.at(n, i + 1))
                    v.tensor_tensor(qkv[:, t, h * w:(h + 1) * w], banks3[i % 3][:, 0:w], b_qkv[:, h * w:(h + 1) * w],
                                    ALU.add).then_inc(qkv_ready.sem, 1)
                    if l == 1 and h == 1:
                        dve.wait_ge(qkv_ready.sem, qkv_ready.at(n, i + 1))
                        qk_center(b, t)
                dve.wait_ge(qkv_ready.sem, qkv_ready.at(n, 2 * TB))
                if l == 1:
                    qk_variance(b)
                else:
                    split_first(n)

            def split_first(n):
                for g, i in ((0, 0), (0, 1), (1, 0), (1, 1)):
                    split(n, g, i)

            def batch(l, b, last):
                n = b + l * B
                nxt = None if last else n + 1
                m1, m2 = ln1_turn(l, b + 1, False), ln2_turn(l, b, last)
                for g in range(NG):
                    if g + 2 < NG:
                        split(n, g + 2, 1)
                    if g + 2 == NG and not last:
                        ln_moments(m1, b + 1)
                        maxima(n, g + 1, range(2))
                        ln_apply(m1, b + 1)
                        maxima(n, g + 1, range(2, G))
                    elif g + 1 < NG:
                        maxima(n, g + 1)
                    elif not last:
                        take_qkv(l, nxt, b + 1)
                    keep_sums(n, g)
                divide(n)
                if l == 1 and not last:
                    qk_scale(b + 1)
                    split_first(nxt)
                if not last:
                    split(nxt, 2, 0)
                for t in range(TB):
                    if not last:
                        maxima(nxt, 0, range(t, t + 1))
                    dve.wait_ge(proj_mm.sem, proj_mm.at(n, t + 1))
                    v.tensor_tensor(tmp[:, t % 2, :], psS[:, (t + 1) % 4, 0:C], gates[:, b, 0, :], ALU.mult).then_inc(proj_read.sem, 1)
                    dve.wait_ge(proj_read.sem, proj_read.at(n, t + 1))
                    v.tensor_tensor(x[:, b * TB + t, :], x[:, b * TB + t, :], tmp[:, t % 2, :], ALU.add).then_inc(x1_ready.sem, 1)
                    dve.wait_ge(x1_ready.sem, x1_ready.at(n, t + 1))
                    settle()
                    ln_sums(b, t)
                ln_moments(m2, b, sums=False)
                ln_apply(m2, b)
                if l == 0:
                    dve.wait_ge(gate_mm.sem, gate_mm.at(b, 1))
                    v.tensor_copy(logits[:, bass.ds(b * TB, TB), :].rearrange("p t e -> p (t e)"),
                                  psS[:, 3, 0:TB * E]).then_inc(gate_read.sem, 1)

            def attention(l):
                dve.wait_ge(s_attw[l], 48)
                take_qkv(l, l * B, 0)
                if l == 1:
                    qk_scale(0)
                    split_first(l * B)
                split(l * B, 2, 0)
                maxima(l * B, 0)
                with dve.Fori(0, B - 1) as b:
                    batch(l, b, False)
                batch(l, B - 1, True)

            def mlp_out(l, q, b, e, t):
                b2 = experts[e % 2][2]
                xt = x[:, b * TB + t, :]
                dve.wait_ge(f2_mm.sem, f2_mm.at(q, t + 1))
                v.tensor_tensor(tmp[:, t % 2, :], psM[:, t % 2, 0:C], b2, ALU.add).then_inc(f2_read.sem, 1)
                dve.wait_ge(f2_read.sem, f2_read.at(q, t + 1))
                if l == 0:
                    v.scalar_tensor_tensor(out=tmp[:, t % 2, :], in0=tmp[:, t % 2, :], scalar=cw[:, b * TB + t, e:e + 1],
                                           in1=gates[:, b, 1, :], op0=ALU.mult, op1=ALU.mult).then_inc(f2_scaled.sem, 1)
                else:
                    v.tensor_tensor(tmp[:, t % 2, :], tmp[:, t % 2, :], gates[:, b, 1, :], ALU.mult).then_inc(f2_scaled.sem, 1)
                dve.wait_ge(f2_scaled.sem, f2_scaled.at(q, t + 1))
                v.tensor_tensor(xt, xt, tmp[:, t % 2, :], ALU.add).then_inc(x2_ready.sem, 1)

            def mods(l, k):
                if k == 0:
                    dve.wait_ge(s_modw[l], 48)
                    if l:
                        dve.wait_ge(h_ready.sem, h_ready.at(2 * B * l, 0))
                        dve.wait_ge(x2_ready.sem, x2_ready.at(ITER0[l], 0))
                    dve.wait_ge(s_mod_mm, 9 * l + 1)
                    flat = modT[:, :, :, :].rearrange("p k c b -> p (k c) b")
                    v.tensor_tensor(flat, psM[0:CH, 0, 0:4 * NC3 * B].rearrange("p (k b) -> p k b", b=B),
                                    mod_bias[:, l, :].unsqueeze(2).to_broadcast([CH, 4 * NC3, B]), ALU.add).then_inc(s_modstep, 1)
                    dve.wait_ge(s_modstep, 3 * l + 1)
                    for i in (1, 3):
                        ins = v.tensor_scalar(modT[:, i, :, :], modT[:, i, :, :], 1.0, None, ALU.add)
                        ins.then_inc(s_modstep, 1)
                    dve.wait_ge(s_modstep, 3 * l + 3)
                    dve.sem_inc(s_mod, 1)
                else:
                    i = k - 1
                    dve.wait_ge(s_mod_mm, 9 * l + 2 + i)
                    v.tensor_tensor(gates[:, i // 2, i % 2, :], banks3[2 * (i % 2)][:, 0:C], gate_bias[:, i % 2, :], ALU.add).then_inc(s_mod, 1)
                if k == 8:
                    dve.wait_ge(s_mod, 9 * l + 9)

            def top_two():
                count = [0]

                def step(ins):
                    count[0] += 1
                    ins.then_inc(s_top, 1)
                    dve.wait_ge(s_top, count[0])

                lg = logits[:, :, :]
                d = top[:, 0:NT * E].rearrange("p (t e) -> p t e", e=E)
                big = NT * E * E
                ge = top[:, big:2 * big].rearrange("p (t e f) -> p t e f", e=E, f=E)
                gt = top[:, 2 * big:3 * big].rearrange("p (t e f) -> p t e f", e=E, f=E)
                one = top[:, 3 * big:3 * big + NT]
                inv_s = top[:, 3 * big + NT:3 * big + 2 * NT]
                rank = top[:, 4 * big:4 * big + NT * E].rearrange("p (t e) -> p t e", e=E)
                dve.wait_ge(gate_read.sem, gate_read.at(B, 0))
                dve.wait_ge(o_ready.sem, o_ready.at(B, 0))
                dve.wait_ge(split_ready.sem, split_ready.at(B, 0))
                step(v.tensor_reduce(one, lg, AX_X, ALU.max))
                step(v.tensor_tensor(d, lg, one.unsqueeze(2).to_broadcast([P, NT, E]), ALU.subtract))
                dve.sem_inc(s_top_in, 1)
                other = lg.unsqueeze(2).to_broadcast([P, NT, E, E])
                own = lg.unsqueeze(3).to_broadcast([P, NT, E, E])
                step(v.tensor_tensor(ge, other, own, ALU.is_ge))
                step(v.tensor_tensor(gt, other, own, ALU.is_gt))
                ge_f = ge.rearrange("p t e f -> p t (e f)")
                gt_f = gt.rearrange("p t e f -> p t (e f)")
                step(v.tensor_tensor(ge_f, ge_f, gt_f, ALU.subtract))
                step(v.tensor_tensor(ge_f, ge_f, before[:, :].unsqueeze(1).to_broadcast([P, NT, E * E]), ALU.mult))
                step(v.tensor_tensor(ge_f, ge_f, gt_f, ALU.add))
                step(v.tensor_reduce(rank, ge, AX_X, ALU.add))
                dve.wait_ge(s_top_exp, 1)
                step(v.scalar_tensor_tensor(out=rank, in0=rank, scalar=1.5, in1=d, op0=ALU.is_lt, op1=ALU.mult))
                step(v.tensor_reduce(one, rank, AX_X, ALU.add))
                step(v.reciprocal(inv_s, one))
                step(v.tensor_tensor(cw[:, :, :], rank, inv_s.unsqueeze(2).to_broadcast([P, NT, E]), ALU.mult))
                assert count[0] == TOP_STEPS, count

            def householder(j):
                col = pT_[:, bass.ds(j, C)]
                s = lambda i: hs[:, i:i + 1]
                done = [0]

                def step(ins):
                    done[0] += 1
                    ins.then_inc(hh_step.sem, 1)
                    return done[0]

                def after(k):
                    dve.wait_ge(hh_step.sem, hh_step.at(j, k))

                dve.wait_ge(hh_mm.sem, hh_mm.at(j, 1))
                dve.wait_ge(hh_upd.sem, hh_upd.at(j, 0))
                after(step(v.tensor_copy(vb, psO[0:D, 0:C])))
                step(v.tensor_tensor_reduce(junk[:, 1:C], vb[:, 1:C], vb[:, 1:C], 1.0, 0.0, ALU.mult, ALU.add, s(0)))
                after(step(v.scalar_tensor_tensor(out=uT, in0=vb, scalar=1.0, in1=col, op0=ALU.mult, op1=ALU.mult, accum_out=s(3))))
                v.scalar_tensor_tensor(out=s(1), in0=vb[:, 0:1], scalar=vb[:, 0:1], in1=s(0), op0=ALU.mult, op1=ALU.add).then_inc(hh_nrm2.sem, 1)
                step(v.tensor_scalar(s(4), vb[:, 0:1], 0.0, 2.0, ALU.is_ge, ALU.mult))
                after(4)
                dve.wait_ge(hh_nrm.sem, hh_nrm.at(j, 1))
                nb = nbs[:, bass.ds(j, 1)]
                after(step(v.scalar_tensor_tensor(out=nb, in0=s(4), scalar=-1.0, in1=s(2), op0=ALU.add, op1=ALU.mult)))
                after(step(v.tensor_tensor(vb[:, 0:1], vb[:, 0:1], nb, ALU.add)))
                after(step(v.tensor_tensor(s(5), vb[:, 0:1], nb, ALU.mult)))
                after(step(v.tensor_scalar(s(5), s(5), 1e-37, None, ALU.max)))
                step(v.scalar_tensor_tensor(out=s(3), in0=pT_[:, bass.ds(j, 1)], scalar=nb, in1=s(3), op0=ALU.mult, op1=ALU.add))
                after(step(v.reciprocal(s(6), s(5))))
                after(step(v.scalar_tensor_tensor(out=cs[:, bass.ds(j, 1)], in0=s(0), scalar=0.0, in1=s(6), op0=ALU.is_gt, op1=ALU.mult)))
                assert done[0] == hh_step.per, done
                v.scalar_tensor_tensor(out=s(7), in0=s(3), scalar=cs[:, bass.ds(j, 1)], in1=below[:, bass.ds(j, 1)],
                                       op0=ALU.mult, op1=ALU.mult).then_inc(hh_w.sem, 1)
                dve.wait_ge(hh_w.sem, hh_w.at(j, 1))
                v.scalar_tensor_tensor(out=col, in0=vb, scalar=s(7), in1=col, op0=ALU.mult, op1=ALU.add).then_inc(hh_upd.sem, 1)

            lin_count = [0]

            def lin_step(ins):
                lin_count[0] += 1
                ins.then_inc(s_lin_dve, 1)
                dve.wait_ge(s_lin_dve, lin_count[0])

            def qr_stage(k):
                e64 = eye[0:D, 0:D]
                step = lin_step
                pair = psO[0:D, 0:2 * D].rearrange("p (i n) -> p i n", i=2)
                if k:
                    dve.wait_ge(s_lin_pe, k)
                if k == 0:
                    dve.wait_ge(hh_upd.sem, hh_upd.at(D, 0))
                    step(v.tensor_tensor_reduce(junk[:, 0:D], nbs, e64, 1.0, 0.0, ALU.mult, ALU.add, hs[:, 8:9]))
                    step(v.tensor_tensor_reduce(junk[:, 0:D], cs, e64, 1.0, 0.0, ALU.mult, ALU.add, hs[:, 9:10]))
                    step(v.tensor_tensor(vT, pT_[:, 0:C], from_diag, ALU.mult))
                    step(v.scalar_tensor_tensor(out=vT[:, 0:D], in0=e64, scalar=hs[:, 8:9], in1=vT[:, 0:D], op0=ALU.mult, op1=ALU.add))
                elif k == 1:
                    step(v.tensor_copy(v_c, psO[0:CH, 0:NC3 * D].rearrange("p (c n) -> p c n", c=NC3)))
                elif k == 2:
                    step(v.scalar_tensor_tensor(out=mm[:, 0, :], in0=psO[0:D, 0:D], scalar=hs[:, 9:10], in1=above, op0=ALU.mult, op1=ALU.mult))
                    step(v.tensor_tensor(mm[:, 1, :], psO[0:D, 0:D], cs, ALU.mult))
                    step(v.tensor_tensor(mm[:, 1, :], mm[:, 1, :], below, ALU.mult))
                    step(v.tensor_scalar(mm[:, 1, :], mm[:, 1, :], -1.0, None, ALU.mult))
                    step(v.tensor_copy(inv, e64.unsqueeze(1).to_broadcast([D, 2, D])))
                elif k < 15 and k % 2:
                    step(v.tensor_copy(prod, pair))
                elif k < 15:
                    step(v.tensor_tensor(inv, inv, pair, ALU.subtract))
                elif k == 15:
                    step(v.tensor_copy(zT_, psO[0:D, 0:D]))
                elif k == 16:
                    step(v.tensor_scalar(uT, psO[0:D, 0:C], -1.0, None, ALU.mult))
                    step(v.tensor_tensor(uT[:, 0:D], uT[:, 0:D], e64, ALU.add))
                else:
                    step(v.tensor_copy(u_c, psO[0:CH, 0:NC3 * D].rearrange("p (c n) -> p c n", c=NC3)))
                if k in (2, 4, 6, 8, 10, 12):
                    i = k // 2 - 1
                    step(v.tensor_tensor(lev[:, 0, :], mm[:, 0, :], level_masks[:, i, :], ALU.mult))
                    step(v.tensor_tensor(lev[:, 1, :], mm[:, 1, :], level_masks[:, 6 + i, :], ALU.mult))
                if k == 14:
                    step(v.tensor_scalar(tT, inv[:, 1, :], hs[:, 9:10], None, ALU.mult))

            def rotation():
                count, step = lin_count, lin_step
                e64 = eye[0:D, 0:D]

                def product(k):
                    dve.wait_ge(s_lin_pe, k)

                half_e = ex_t.rearrange("p (i n) -> p i n", n=D)[:, 0:B, :]
                dve.wait_ge(sq_dve.sem, sq_dve.at(SQUARINGS, 0))
                step(v.tensor_tensor(half_e, ex.rearrange("p (i n) -> p i n", n=D)[:, B:2 * B, :],
                                     e64.unsqueeze(1).to_broadcast([D, B, D]), ALU.subtract))
                assert count[0] == LIN_STEPS, count
                product(18)
                step(v.tensor_copy(w_rot, psS[0:D, :, 0:C]))
                for b in range(B):
                    dve.wait_ge(rt_z.sem, rt_z.at(b, 1))
                    v.tensor_copy(zT[:, b % 2, :], psO[0:D, :]).then_inc(rt_zc.sem, 1)
                    for t in range(TB):
                        xt = x[:, b * TB + t, :]
                        dve.wait_ge(rt_mm.sem, rt_mm.at(b, t + 1))
                        v.tensor_tensor(xt, psS[:, t, 0:C], xt, ALU.add).then_inc(rt_add.sem, 1)
                    if b == 1:
                        dve.wait_ge(rt_add.sem, rt_add.at(1, 0))
                        ln_moments(ln1_turn(1, 0, True), 0)
                    if b == 2:
                        ln_apply(ln1_turn(1, 0, True), 0)
                dve.wait_ge(rt_add.sem, rt_add.at(B, 0))

            def skew_norm(part):
                start = (0, 3, 4)[part]
                count = [start]

                def step(ins):
                    count[0] += 1
                    ins.then_inc(s_norm_dve, 1)
                    dve.wait_ge(s_norm_dve, count[0])

                if part == 0:
                    dve.wait_ge(s_skew_in, 16)
                    step(v.tensor_tensor(A[:, :, :], A[:, :, :], sign.unsqueeze(1).to_broadcast([D, B, D]), ALU.mult))
                    step(v.tensor_reduce(hs[:, 10:14], A[:, :, :], AX_X, ALU.add, apply_absolute_value=True))
                    step(v.tensor_reduce(hs[:, 14:15], hs[:, 10:14], AX_X, ALU.max))
                elif part == 1:
                    dve.wait_ge(s_norm_pe, 1)
                    step(v.tensor_reduce(junk[0:1, 0:1], psT[0:1, 0:D], AX_X, ALU.max))
                else:
                    dve.wait_ge(s_norm_pe, 2)
                    step(v.tensor_copy(hs[:, 15:16], psT[0:D, 0:1]))
                    step(v.tensor_scalar(flags[:, 0:SQUARINGS], halves, hs[:, 15:16], 1.0, ALU.mult, ALU.is_gt))
                    step(v.tensor_scalar(junk[:, 0:SQUARINGS], flags[:, 0:SQUARINGS], -0.5, 1.0, ALU.mult, ALU.add))
                    w = SQUARINGS
                    while w > 1:
                        w //= 2
                        step(v.tensor_tensor(junk[:, 0:w], junk[:, 0:w], junk[:, w:2 * w], ALU.mult))
                    flat_a = A[:, :, :].rearrange("p b n -> p (b n)")
                    step(v.tensor_scalar(xs[:, 0, :], flat_a, junk[:, 0:1], None, ALU.mult))
                    step(v.tensor_scalar(xs[:, 1, :], xs[:, 0, :], -1.0, None, ALU.mult))
                    step(v.tensor_copy(ex.rearrange("p (i n) -> p i n", n=D), eye[0:D, 0:D].unsqueeze(1).to_broadcast([D, 2 * B, D])))
                    assert count[0] == NORM_STEPS, count

            def series_term(i):
                dve.wait_ge(ho_mm.sem, ho_mm.at(i, 1))
                v.scalar_tensor_tensor(out=ex.rearrange("p (i n) -> p i n", n=D), in0=psT[0:D, :].rearrange("p (i n) -> p i n", n=D),
                                       scalar=over_k[:, bass.ds(i, 1)], in1=eye[0:D, 0:D].unsqueeze(1).to_broadcast([D, 2 * B, D]),
                                       op0=ALU.mult, op1=ALU.add).then_inc(ho_dve.sem, 1)

            def squaring(i):
                dve.wait_ge(sq_dve.sem, sq_dve.at(i, 0))
                dve.wait_ge(sq_mm.sem, sq_mm.at(i, 1))
                v.tensor_tensor(ex_t, psT[0:D, :], ex, ALU.subtract).then_inc(sq_t.sem, 1)
                dve.wait_ge(sq_t.sem, sq_t.at(i, 1))
                v.scalar_tensor_tensor(out=ex, in0=ex_t, scalar=flags[:, bass.ds(i, 1)], in1=ex, op0=ALU.mult, op1=ALU.add).then_inc(sq_dve.sem, 1)

            dve.wait_ge(s_const, 64)
            v.tensor_copy(eye16[:, :], eye[:, :]).then_inc(s_eye, 1)
            dve.wait_ge(s_exp0, 1)
            v.tensor_scalar(silu_t[:, :, :], silu_t[:, :, :], 1.0, None, ALU.add).then_inc(s_eye, 1)
            dve.wait_ge(s_eye, 2)
            v.reciprocal(silu_t[:, :, :], silu_t[:, :, :]).then_inc(s_eye, 1)
            dve.wait_ge(s_eye, 3)
            v.tensor_tensor(silu[:, :, :], cond[:, :, :], silu_t[:, :, :], ALU.mult).then_inc(s_silu, 1)
            for k in range(9):
                mods(0, k)
            dve.wait_ge(s_x, 16)
            first_rows(0)
            dve.wait_ge(s_skew_b, 16)
            for i in range(8):
                dve.wait_ge(s_skew_mm, i + 1)
                v.tensor_tensor(v_skew[:, i * 512:(i + 1) * 512], psS[0:B, i % 4, :], b_skew[:, i * 512:(i + 1) * 512],
                                ALU.add).then_inc(s_skew_v, 1)
            dve.wait_ge(s_skew_v, 8)
            dve.wait_ge(s_init, 4)
            attention(0)
            top_two()
            dve.wait_ge(s_lin, 32)
            skew_norm(0)
            for e in range(E):
                dve.wait_ge(s_mlpw[e], 64)
                if e < E - 1:
                    with dve.Fori(0, B) as b:
                        for s in range(4):
                            householder(b * HH_TURN[e] + (HH_START[e] + s))
                            if e == 2 and s < 3:
                                series_term(b * 3 + s)
                        for t in range(TB):
                            mlp_out(0, b + 4 * e, b, e, t)
                            if HH_TURN[e] == 6 and t in (0, 2):
                                householder(b * HH_TURN[e] + (HH_START[e] + 4 + t // 2))
                else:
                    for b in range(B):
                        for m in range(MH):
                            if m % 2:
                                squaring(4 * b + m // 2)
                            elif 5 * b + m // 2 < QR_STAGES:
                                qr_stage(5 * b + m // 2)
                        for t in range(TB):
                            mlp_out(0, b + 4 * e, b, e, t)
                dve.wait_ge(x2_ready.sem, x2_ready.at(4 * (e + 1), 0))
                if e < 2:
                    skew_norm(e + 1)
            rotation()
            for k in range(9):
                mods(1, k)
            dve.wait_ge(s_init, 6)
            dve.wait_ge(s_start, 80)
            attention(1)
            dve.wait_ge(s_mlpw[WSET[1]], 64)
            dve.wait_ge(x1_ready.sem, x1_ready.at(2 * B, 0))
            with dve.Fori(0, B) as b:
                for t in range(TB):
                    mlp_out(1, b + ITER0[1], b, 0, t)
            dve.wait_ge(x2_ready.sem, x2_ready.at(ITER0[2], 0))
            first_rows(2)
            for k in range(9):
                mods(2, k)
            dve.wait_ge(s_init, 8)
            attention(2)
            dve.wait_ge(s_mlpw[WSET[2]], 64)
            with dve.Fori(0, B) as b:
                for t in range(TB):
                    mlp_out(2, b + ITER0[2], b, 0, t)

        @block.tensor
        def _(pe):
            grant_credit(pe, "pe")
            mmul = nc.tensor.matmul
            def settle():
                pe.sem_inc(s_passed_pe, 1)

            def mods(l, k):
                if k == 0:
                    pe.wait_ge(s_modw[l], 48)
                    pe.wait_ge(s_silu, 1)
                    if l:
                        pe.wait_ge(x2_ready.sem, x2_ready.at(ITER0[l], 0))
                    if l == 1:
                        pe.wait_ge(rt_h.sem, rt_h.at(B, 0))
                    for i, col in enumerate((0, 1, 3, 4)):
                        for c2 in range(NC3):
                            o = (i * NC3 + c2) * B
                            for c in range(NC3):
                                last = mmul(psM[0:CH, 0, o:o + B], w_mod[:, c, col * C + c2 * CH:col * C + (c2 + 1) * CH],
                                            silu[:, c, :], start=(c == 0), stop=(c == NC3 - 1))
                    last.then_inc(s_mod_mm, 1)
                    return
                i = k - 1
                if i == 0:
                    pe.wait_ge(s_silu_b, l + 1)
                if i > 1:
                    pe.wait_ge(s_mod, 9 * l + i)
                col = (2, 5)[i % 2] * C
                for c in range(NC3):
                    last = mmul(banks3[2 * (i % 2)][:, 0:C], silu_b[:, c * B + i // 2, :], w_mod[:, c, col:col + C],
                                start=(c == 0), stop=(c == NC3 - 1))
                last.then_inc(s_mod_mm, 1)
                if k == 8:
                    pe.wait_ge(s_mod, 9 * l + 9)

            def transpose_rows(sig, turn, banks):
                for c in range(NC3):
                    for t in range(TB):
                        last = nc.tensor.transpose(banks[c][0:CH, t * P:(t + 1) * P], xhat[:, t, c * CH:(c + 1) * CH], eye[:, :])
                    last.then_inc(sig.sem, 1)

            def transpose_heads(n, g, i):
                rows = KM if i in (2, 3) else KS
                src = (kp if i < 2 else qp)[g % 2]
                turn = SET_TURN[g, i]
                earlier = [k for k in range(1, turn) if set_bank(*SET_ORDER[k - 1]) == set_bank(g, i)]
                if earlier:
                    pe.wait_ge(t_ev.sem, t_ev.at(n, earlier[-1]))
                if i in (0, 2):
                    if g == 0:
                        pe.wait_ge(rep_first.sem, rep_first.at(n, i // 2 + 1))
                    else:
                        pe.wait_ge(rep_done.sem, rep_done.at(n, 2 * (g - 1) + i // 2 + 1))
                elif i == 4:
                    pe.wait_ge(m_ready.sem, m_ready.at(n, g + 1))
                for hh in range(2):
                    for t in range(TB):
                        o = (hh * TB + t) * P
                        last = nc.tensor.transpose(banks_16[set_bank(g, i)][0:rows, o:o + P],
                                                   src[:, t * G + 2 * (i % 2) + hh, 0:rows], eye16[:, :])
                last.then_inc(t_mm.sem, 1)

            def max_scores(n, g, turns):
                for k in turns:
                    j, t = divmod(k, TB)
                    i = 16 * g + k
                    if k == 0:
                        pe.wait_ge(t_ev.sem, t_ev.at(n, SET_TURN[g, 3]))
                    if k < 2 and g:
                        pe.wait_ge(t_ev.sem, t_ev.at(n, SET_TURN[g - 1, 4 + k]))
                    if k > 1:
                        pe.wait_ge(max_done.sem, max_done.at(n, i - 1))
                    mmul(psM[:, t % 2, :], qT[g % 3][0:KM, j, t * P:(t + 1) * P], kT[g % 3][0:KM, j, :],
                         start=True, stop=True).then_inc(max_mm.sem, 1)

            def scores(n, g, kb, h):
                i = 8 * g + 2 * kb + h
                if kb == 0:
                    pe.wait_ge(t_ev.sem, t_ev.at(n, SET_TURN[g, 4 + h]))
                pe.wait_ge(exp_done.sem, exp_done.at(n, i - 1))
                for hh in range(2):
                    last = mmul(psS[:, 2 * h + hh, :], kT[g % 3][0:KS, 2 * h + hh, kb * P:(kb + 1) * P],
                                qT[g % 3][0:KS, 2 * h + hh, :], start=True, stop=True)
                last.then_inc(s_mm.sem, 1)

            def values(n, g, kb):
                u = 4 * g + kb
                if kb == 0:
                    pe.wait_ge(v_staged.sem, v_staged.at(n, g + 1))
                    pe.wait_ge(o_raw.sem, o_raw.at(n, g))
                pe.wait_ge(exp_done.sem, exp_done.at(n, 2 * u + 2))
                for j in range(G):
                    last = mmul(psO[HP * j:HP * (j + 1), :], vg[g % 2][:, kb, HP * j:HP * (j + 1)],
                                pT[:, kb % 2, j * N:(j + 1) * N], start=(kb == 0), stop=(kb == TB - 1))
                last.then_inc(av_done.sem, 1)

            def gather_denominators(n):
                for g in range(NG):
                    if g == NG - 1:
                        pe.wait_ge(o_raw.sem, o_raw.at(n, NG))
                    last = mmul(psS[0:NH, 0, :], gather[:, g, :], oT[:, g, :], start=(g == 0), stop=(g == NG - 1))
                last.then_inc(d_mm.sem, 1)

            def spread_reciprocals(n):
                pe.wait_ge(recip.sem, recip.at(n, 1))
                for g in range(NG):
                    mmul(psS[:, (g + 1) % 4, :], spread[:, g, :], rD, start=True, stop=True).then_inc(d_mm.sem, 1)

            def open_rows(n, m):
                pe.wait_ge(t_ev.sem, t_ev.at(n, 0))
                pe.wait_ge(ln_xhat.sem, ln_xhat.at(m + 1, 0))
                transpose_rows(ln_T, m, banks3)

            def qkv_products(n, m, turns):
                w = 3 * C // 2
                for i in turns:
                    t, h = divmod(i, 2)
                    if i == 0:
                        pe.wait_ge(h_ready.sem, h_ready.at(m + 1, 0))
                    if i >= 3:
                        pe.wait_ge(qkv_ready.sem, qkv_ready.at(n, i - 2))
                    for c in range(NC3):
                        last = mmul(banks3[i % 3][:, 0:w], hT[:, c, t * P:(t + 1) * P], w_qkv[:, c, h * w:(h + 1) * w],
                                    start=(c == 0), stop=(c == NC3 - 1))
                    last.then_inc(qkv_mm.sem, 1)

            def first_transposes(n):
                pe.wait_ge(qkv_ready.sem, qkv_ready.at(n, 2 * TB))
                for g, i in SET_ORDER[0:4]:
                    transpose_heads(n, g, i)

            def project(n, t, groups=range(NG)):
                for g in groups:
                    if t == 0:
                        pe.wait_ge(o_ready.sem, o_ready.at(n, g + 1))
                    last = mmul(psS[:, (t + 1) % 4, 0:C], oT[:, g, t * P:(t + 1) * P], w_proj[:, g, :], start=(g == 0), stop=(g == NG - 1))
                if groups[-1] == NG - 1:
                    last.then_inc(proj_mm.sem, 1)

            def first_maxima(n, j, projecting=False):
                for k, groups in ((0, None), (1, range(0, 1)), (2, range(1, 2)), (3, range(2, NG))):
                    max_scores(n, 0, range(TB * j + k, TB * j + k + 1))
                    if projecting and k:
                        project(n - 1, j, groups)
                if j >= 2:
                    transpose_heads(n, 1, j - 2)

            def mlp_rows(l, n, m):
                pe.wait_ge(proj_read.sem, proj_read.at(n + 1, 0))
                pe.wait_ge(ln_xhat.sem, ln_xhat.at(m + 1, 0))
                transpose_rows(ln_T, m, banksS)

            def gate_product(m):
                pe.wait_ge(h_ready.sem, h_ready.at(m + 1, 0))
                for t in range(TB):
                    for c in range(NC3):
                        last = mmul(psS[:, 3, t * E:(t + 1) * E], hT[:, c, t * P:(t + 1) * P], w_gate[:, c, :],
                                    start=(c == 0), stop=(c == NC3 - 1))
                last.then_inc(gate_mm.sem, 1)

            def batch(l, b, last):
                n = b + l * B
                m1, m2 = ln1_turn(l, b + 1, False), ln2_turn(l, b, last)
                for g in range(NG):
                    more = g + 1 < NG
                    if not more and not last:
                        open_rows(n + 1, m1)
                    for kb in range(TB):
                        s0, s1, s2, s3, s4 = MAX_SLOTS[kb]
                        scores(n, g, kb, 0)
                        if more:
                            max_scores(n, g + 1, range(s0, s1))
                        scores(n, g, kb, 1)
                        if more:
                            max_scores(n, g + 1, range(s1, s2))
                        if kb:
                            values(n, g, kb - 1)
                        if more:
                            max_scores(n, g + 1, range(s2, s3))
                        if g + 2 < NG and kb < 3:
                            transpose_heads(n, g + 2, kb)
                        if more:
                            max_scores(n, g + 1, range(s3, s4))
                        elif not last:
                            qkv_products(n + 1, m1, range(3 * kb, min(3 * kb + 3, 2 * TB)))
                    if more:
                        for i in (4, 5):
                            transpose_heads(n, g + 1, i)
                    values(n, g, TB - 1)
                    if g + 2 < NG:
                        transpose_heads(n, g + 2, 3)
                gather_denominators(n)
                if not last and l != 1:
                    first_transposes(n + 1)
                spread_reciprocals(n)
                if l == 1 and not last:
                    for t in range(TB):
                        project(n, t)
                    first_transposes(n + 1)
                for t in range(TB):
                    if last:
                        project(n, t)
                    else:
                        first_maxima(n + 1, t, projecting=(l != 1))
                if last:
                    mlp_rows(l, n, m2)
                    if l == 0:
                        gate_product(m2)
                    return
                for g, i in SET_ORDER[6:10]:
                    transpose_heads(n + 1, g, i)
                mlp_rows(l, n, m2)
                if l == 0:
                    gate_product(m2)
                    pe.wait_ge(gate_read.sem, gate_read.at(b + 1, 0))
                pe.wait_ge(h_ready.sem, h_ready.at(m2 + 1, 0))

            def attention(l):
                pe.wait_ge(s_attw[l], 48)
                n, m = l * B, ln1_turn(l, 0, True)
                open_rows(n, m)
                qkv_products(n, m, range(2 * TB))
                first_transposes(n)
                for j in range(G):
                    first_maxima(n, j)
                for g, i in SET_ORDER[6:10]:
                    transpose_heads(n, g, i)
                with pe.Fori(0, B - 1) as b:
                    batch(l, b, False)
                batch(l, B - 1, True)

            def mlp(l, e):
                pe.wait_ge(s_mlpw[WSET[l] + e], 64)
                if e == 0:
                    pe.wait_ge(h2_ready.sem, h2_ready.at(B * (l + 1), 0))
                    pe.wait_ge(proj_read.sem, proj_read.at(B * (l + 1), 0))
                    if l == 0:
                        pe.wait_ge(s_lin, 32)
                        pe.wait_ge(gate_read.sem, gate_read.at(B, 0))
                if l == 0 and e == E - 1:
                    for b in range(B):
                        mlp_turn(l, e, b)
                else:
                    with pe.Fori(0, B) as b:
                        mlp_turn(l, e, b)

            def householder_spread(j):
                pe.wait_ge(hh_pick.sem, hh_pick.at(j, 1))
                pe.wait_ge(hh_upd.sem, hh_upd.at(j, 0))
                mmul(psO[:, 0:C], pick, pT_[:, bass.ds(j, C)], start=True, stop=True).then_inc(hh_mm.sem, 1)

            def mlp_turn(l, e, b):
                w1, w2, _, _ = experts[e % 2]
                q = b + (ITER0[l] + B * e)
                for m in range(MH):
                    pe.wait_ge(hid_ready.sem, hid_ready.at(q, m - 3))
                    for c in range(NC3):
                        last = mmul(psS[:, m % 4, :], w1[:, c, m * P:(m + 1) * P], h2T[:, c, bass.ds(b * N, N)],
                                    start=(c == 0), stop=(c == NC3 - 1))
                    last.then_inc(f1_mm.sem, 1)
                    if l == 0 and e == 2 and m in (2, 4, 6):
                        series_product(b * 3 + (m // 2 - 1))
                    if l == 0 and e < 3 and m % 2:
                        householder_spread(b * HH_TURN[e] + (HH_START[e] + m // 2))
                    if l == 0 and e == 3 and m % 2:
                        square_product(4 * b + m // 2)
                    if l == 0 and e == 3 and m % 2 == 0 and 0 < 5 * b + m // 2 + 1 < QR_STAGES:
                        qr_product(5 * b + m // 2 + 1)
                for t in range(TB):
                    pe.wait_ge(f2_read.sem, f2_read.at(q, t - 1))
                    for m in range(MH):
                        if t == 0 and m >= MH - 4:
                            pe.wait_ge(hid_ready.sem, hid_ready.at(q, m + 1))
                        last = mmul(psM[:, t % 2, 0:C], hid[:, m, t * P:(t + 1) * P], w2[:, m, :],
                                    start=(m == 0), stop=(m == MH - 1))
                    last.then_inc(f2_mm.sem, 1)
                    if l == 0 and HH_TURN[e] == 6 and t in (0, 2):
                        householder_spread(b * HH_TURN[e] + (HH_START[e] + 4 + t // 2))

            def norm_moved(part):
                if part == 0:
                    pe.wait_ge(s_norm_dve, 3)
                    mmul(psT[0:1, 0:D], hs[:, 14:15], eye[0:D, 0:D], start=True, stop=True).then_inc(s_norm_pe, 1)
                else:
                    pe.wait_ge(s_norm_dve, 4)
                    mmul(psT[0:D, 0:1], eye_row, junk[0:1, 0:1], start=True, stop=True).then_inc(s_norm_pe, 1)

            ex3 = ex.rearrange("p (i n) -> p i n", n=D)
            xs3 = xs.rearrange("p i (b n) -> p i b n", n=D)

            def series_product(i):
                pe.wait_ge(s_norm_dve, NORM_STEPS)
                pe.wait_ge(ho_dve.sem, ho_dve.at(i, 0))
                settle()
                for k in range(2 * B):
                    last = mmul(psT[0:D, k * D:(k + 1) * D], xs3[:, 1 - k // B, k % B, :], ex3[:, k, :], start=True, stop=True)
                last.then_inc(ho_mm.sem, 1)

            def square_product(i):
                pe.wait_ge(sq_dve.sem, sq_dve.at(i, 0))
                settle()
                for k in range(2 * B):
                    last = mmul(psT[0:D, k * D:(k + 1) * D], ex3[:, (k + B) % (2 * B), :], ex3[:, k, :], start=True, stop=True)
                last.then_inc(sq_mm.sem, 1)

            def ready(k):
                pe.wait_ge(s_lin_dve, k)

            def qr_product(k):
                e64 = eye[0:D, 0:D]
                if k == 1:
                    ready(4)
                    for c in range(NC3):
                        last = nc.tensor.transpose(psO[0:CH, c * D:(c + 1) * D], vT[:, c * CH:(c + 1) * CH], e64)
                elif k == 2:
                    ready(5)
                    for c in range(NC3):
                        last = mmul(psO[0:D, 0:D], v_c[:, c, :], v_c[:, c, :], start=(c == 0), stop=(c == NC3 - 1))
                elif k < 15 and k % 2:
                    ready(12 + 2 * (k - 3))
                    mmul(psO[0:D, 0:D], lev[:, 1, :], inv[:, 0, :], start=True, stop=True)
                    last = mmul(psO[0:D, D:2 * D], lev[:, 0, :], inv[:, 1, :], start=True, stop=True)
                elif k < 15:
                    ready(13 + 2 * (k - 4))
                    mmul(psO[0:D, 0:D], inv[:, 1, :], prod[:, 0, :], start=True, stop=True)
                    last = mmul(psO[0:D, D:2 * D], inv[:, 0, :], prod[:, 1, :], start=True, stop=True)
                elif k == 15:
                    ready(35)
                    last = mmul(psO[0:D, 0:D], tT, vT[:, 0:D], start=True, stop=True)
                elif k == 16:
                    ready(36)
                    last = mmul(psO[0:D, 0:C], zT_, vT, start=True, stop=True)
                else:
                    ready(38)
                    for c in range(NC3):
                        last = nc.tensor.transpose(psO[0:CH, c * D:(c + 1) * D], uT[:, c * CH:(c + 1) * CH], e64)
                last.then_inc(s_lin_pe, 1)

            def rotation():
                pe.wait_ge(hid_ready.sem, hid_ready.at(4 * E, 0))
                ready(LIN_STEPS)
                half_e = ex_t.rearrange("p (i n) -> p i n", n=D)
                for b in range(B):
                    last = mmul(psS[0:D, b, 0:C], half_e[:, b, :], uT, start=True, stop=True)
                last.then_inc(s_lin_pe, 1)
                pe.wait_ge(x2_ready.sem, x2_ready.at(4 * E, 0))

                def rows(b):
                    for c in range(NC3):
                        if b:
                            pe.wait_ge(rt_h.sem, rt_h.at(b - 1, c + 1))
                        for t in range(TB):
                            last = nc.tensor.transpose(banks3[c][0:CH, t * P:(t + 1) * P], x[:, b * TB + t, c * CH:(c + 1) * CH], eye[:, :])
                        last.then_inc(rt_T.sem, 1)

                def into_subspace(b):
                    pe.wait_ge(rt_h.sem, rt_h.at(b, NC3))
                    pe.wait_ge(rt_zc.sem, rt_zc.at(b, 0))
                    for c in range(NC3):
                        last = mmul(psO[0:D, :], u_c[:, c, :], h2T[:, c, b * N:(b + 1) * N], start=(c == 0), stop=(c == NC3 - 1))
                    last.then_inc(rt_z.sem, 1)

                def rotated(b):
                    pe.wait_ge(rt_zc.sem, rt_zc.at(b, 1))
                    if b == 0:
                        ready(LIN_STEPS + 1)
                    for t in range(TB):
                        pe.wait_ge(rt_add.sem, rt_add.at(b, t - 3))
                        mmul(psS[:, t, 0:C], zT[:, b % 2, t * P:(t + 1) * P], w_rot[:, b, :], start=True, stop=True).then_inc(rt_mm.sem, 1)

                rows(0)
                rows(1)
                for b in range(B):
                    into_subspace(b)
                    if b + 2 < B:
                        rows(b + 2)
                    rotated(b)

            pe.wait_ge(s_eye, 1)
            for k in range(9):
                mods(0, k)
            for i in range(8):
                pe.wait_ge(s_skew_w[i % 2], 16 * (i // 2 + 1))
                if i >= 4:
                    pe.wait_ge(s_skew_v, i - 3)
                for c in range(NC3):
                    last = mmul(psS[0:B, i % 4, :], silu[:, c, :], w_skew[i % 2][:, c, :], start=(c == 0), stop=(c == NC3 - 1))
                last.then_inc(s_skew_mm, 1)
            pe.wait_ge(s_skew_v, 8)
            pe.wait_ge(s_init, 4)
            pe.wait_ge(s_start, 80)
            attention(0)
            for e in range(E):
                mlp(0, e)
                if e < 2:
                    norm_moved(e)
                if e == 2:
                    pe.wait_ge(ho_dve.sem, ho_dve.at(TAYLOR, 0))
            rotation()
            for k in range(9):
                mods(1, k)
            pe.wait_ge(s_init, 6)
            attention(1)
            mlp(1, 0)
            for k in range(9):
                mods(2, k)
            pe.wait_ge(s_init, 8)
            attention(2)
            mlp(2, 0)


TOP_STEPS = 12
QR_STAGES = 18
LIN_STEPS = 40
NORM_STEPS = 14


def lay_out(inputs):
    a = {k: np.ascontiguousarray(v) for k, v in inputs.items()}
    out = dict(host_constants())
    out["x"] = a["x"]
    out["cond"] = np.ascontiguousarray(a["cond_1152"].T.reshape(NC3, CH, B).transpose(1, 0, 2))
    names = {
        "L0": ("L0_cond_w_adaln", "L0_cond_b_adaln", "L0_cond_w_qkv", "L0_cond_b_qkv", "L0_cond_w_proj", "L0_cond_b_proj",
               "L0_cond_w1", "L0_cond_b1", "L0_cond_w2", "L0_cond_b2"),
        "L2": ("L2_cond_w_mod", "L2_cond_b_mod", "L2_cond_w_qkv", "L2_cond_b_qkv", "L2_cond_w_proj", "L2_cond_b_proj",
               "L2_cond_w1", "L2_cond_b1", "L2_cond_w2", "L2_cond_b2"),
        "L3": ("L3_cond_W_ada", "L3_cond_b_ada", "L3_cond_W_qkv", "L3_cond_b_qkv", "L3_cond_W_proj", "L3_cond_b_proj",
               "L3_cond_W_fc1", "L3_cond_b_fc1", "L3_cond_W_fc2", "L3_cond_b_fc2"),
    }
    mod_bias = np.zeros((CH, 3, 4 * NC3), np.float32)
    for l, n in enumerate(LAYERS):
        wm, bm, wq, bq, wp, bp, w1, b1, w2, b2 = (a[k] for k in names[n])
        ne = w1.size // (C * HID)
        out[n + "_w_mod"], out[n + "_b_mod"], out[n + "_w_qkv"], out[n + "_b_qkv"] = wm, bm, wq, bq
        pad = np.zeros((NG, G, HP, C), np.float32)
        pad[:, :, 0:HD] = wp.reshape(NG, G, HD, C)
        pad[0, 0, HD] = bp
        out[n + "_w_proj"] = np.ascontiguousarray(pad.transpose(1, 2, 0, 3).reshape(P, NG, C))
        out[n + "_w1"], out[n + "_w2"] = w1.reshape(ne, C, HID), w2.reshape(ne, HID, C)
        out[n + "_b2"] = b2.reshape(ne, C)
        out[n + "_b1"] = np.ascontiguousarray(b1.reshape(ne, MH, P).transpose(0, 2, 1))
        mod_bias[:, l] = bm.reshape(6, NC3, CH)[[0, 1, 3, 4]].reshape(4 * NC3, CH).T
    out["mod_bias"] = mod_bias
    out["w_gate"] = a["L0_cond_w_gate"]
    out["g_q"] = np.tile(a["L2_cond_g_q"], NH)
    out["g_k"] = np.tile(a["L2_cond_g_k"], NH)
    iu, ju = np.triu_indices(D, k=1)
    w = np.zeros((D, D, C), np.float32)
    w[iu, ju] = a["L1_cond_W"]
    w[ju, iu] = a["L1_cond_W"]
    out["w_skew"] = np.ascontiguousarray(w.reshape(D * D, C).T)
    bs = np.zeros((D, D), np.float32)
    bs[iu, ju] = a["L1_cond_b"]
    bs[ju, iu] = a["L1_cond_b"]
    out["b_skew"] = bs.reshape(D * D)
    pT = np.zeros((D, C + D), np.float32)
    pT[:, 0:C] = a["L1_cond_P"].T
    out["pT"] = pT
    return out


def kernel(**inputs):
    import concourse.bacc as bacc
    from concourse.bass_utils import run_bass_kernel_spmd as run

    nc = bacc.Bacc("TRN2", target_bir_lowering=False, num_devices=1)
    arrays = {"in_" + k: v for k, v in lay_out(inputs).items()}
    dram = {k[3:]: nc.dram_tensor(k, v.shape, F32, kind="ExternalInput").ap() for k, v in arrays.items()}
    dram["out"] = nc.dram_tensor("out_x", (B, N, C), F32, kind="ExternalOutput").ap()
    build(nc, dram)
    r = run(nc, [arrays], core_ids=[0])
    return r.results[0]["out_x"]
```
